# Optimizing a Trainium2 kernel written in Bass

```python
import numpy as np
import jax
import jax.numpy as jnp

def _softmax(x, axis=-1):
    return jax.nn.softmax(x, axis=axis)

def _gelu(x):
    return jax.nn.gelu(x, approximate=True)

def _silu(x):
    return jax.nn.silu(x)

def _sigmoid(x):
    return jax.nn.sigmoid(x)

def _layernorm(x, axis=-1, eps=1e-05):
    m = jnp.mean(x, axis=axis, keepdims=True)
    v = jnp.var(x, axis=axis, keepdims=True)
    return (x - m) / jnp.sqrt(v + eps)

def _scatter_add(tgt, idx, src, axis=0):
    return tgt.at[idx].add(src)

def _segment_sum(src, seg, n):
    return jax.ops.segment_sum(src, seg, n)
kernel_name = 'mk_sandwich_d1_jaxref_r4_401f01'

def setup_inputs(seed: int=0):
    np.random.seed(seed)
    _w = jnp.asarray

    def _L0_attn_setup():
        import jax, jax.numpy as jnp
        import numpy as np
        EMBED_DIM = 256
        NUM_HEADS = 16
        HEAD_DIM = EMBED_DIM // NUM_HEADS
        BATCH = 2
        SEQ = 512
        key = jax.random.key(seed)
        ks = jax.random.split(key, 9)
        f16 = jnp.float16

        def w(k):
            return (jax.random.normal(k, (EMBED_DIM, EMBED_DIM), dtype=jnp.float32) * 0.02).astype(f16)

        def b(k):
            return (jax.random.normal(k, (EMBED_DIM,), dtype=jnp.float32) * 0.02).astype(f16)
        hidden = (jax.random.normal(ks[0], (BATCH, SEQ, EMBED_DIM), dtype=jnp.float32) * 0.5).astype(f16)
        return {'hidden_states': hidden, 'wq': w(ks[1]), 'bq': b(ks[2]), 'wk': w(ks[3]), 'bk': b(ks[4]), 'wv': w(ks[5]), 'bv': b(ks[6]), 'wo': w(ks[7]), 'bo': b(ks[8])}
    _L0_attn_in = _L0_attn_setup()

    def _L0_ffn_setup():
        import jax, jax.numpy as jnp
        import numpy as np
        D, F, E, K = (256, 688, 8, 2)
        key = jax.random.key(seed)
        k0, k1, k2, k3, k4 = jax.random.split(key, 5)
        s = 0.02
        x = jax.random.normal(k0, (2, 128, D), jnp.float32)
        Ws = jax.random.normal(k1, (D, E), jnp.float32) * s
        bs = jnp.zeros((E,), jnp.float32)
        Wg = jax.random.normal(k2, (E, D, F), jnp.float32) * s
        Wu = jax.random.normal(k3, (E, D, F), jnp.float32) * s
        Wd = jax.random.normal(k4, (E, F, D), jnp.float32) * s
        return {'x': x, 'Ws': Ws, 'bs': bs, 'Wg': Wg, 'Wu': Wu, 'Wd': Wd}
    _L0_ffn_in = _L0_ffn_setup()
    _d = {'L0_attn_hidden_states': _L0_attn_in['hidden_states'], 'L0_attn_wq': _L0_attn_in['wq'], 'L0_attn_bq': _L0_attn_in['bq'], 'L0_attn_wk': _L0_attn_in['wk'], 'L0_attn_bk': _L0_attn_in['bk'], 'L0_attn_wv': _L0_attn_in['wv'], 'L0_attn_bv': _L0_attn_in['bv'], 'L0_attn_wo': _L0_attn_in['wo'], 'L0_attn_bo': _L0_attn_in['bo'], 'L0_ffn_Ws': _L0_ffn_in['Ws'], 'L0_ffn_bs': _L0_ffn_in['bs'], 'L0_ffn_Wg': _L0_ffn_in['Wg'], 'L0_ffn_Wu': _L0_ffn_in['Wu'], 'L0_ffn_Wd': _L0_ffn_in['Wd']}
    _x0 = _d['L0_attn_hidden_states']
    _d['L0_attn_hidden_states'] = jax.random.normal(jax.random.fold_in(jax.random.key(seed), 1), (8, 512, 256), dtype=_x0.dtype)
    del _x0
    return _d

def reference(L0_attn_hidden_states, L0_attn_wq, L0_attn_bq, L0_attn_wk, L0_attn_bk, L0_attn_wv, L0_attn_bv, L0_attn_wo, L0_attn_bo, L0_ffn_Ws, L0_ffn_bs, L0_ffn_Wg, L0_ffn_Wu, L0_ffn_Wd):

    def _L0_attn_ref(hidden_states, wq, bq, wk, bk, wv, bv, wo, bo):
        import jax, jax.numpy as jnp
        import numpy as np
        EMBED_DIM = 256
        NUM_HEADS = 16
        HEAD_DIM = EMBED_DIM // NUM_HEADS
        BATCH = 2
        SEQ = 512
        B, T, E = hidden_states.shape
        H, D = (NUM_HEADS, HEAD_DIM)
        scaling = jnp.asarray(D ** (-0.5), dtype=hidden_states.dtype)

        def shape_heads(x):
            return x.reshape(B, T, H, D).transpose(0, 2, 1, 3)
        q = shape_heads((hidden_states @ wq.T + bq) * scaling)
        k = shape_heads(hidden_states @ wk.T + bk)
        v = shape_heads(hidden_states @ wv.T + bv)
        scores = jnp.einsum('bhtd,bhsd->bhts', q, k)
        mask = jnp.triu(jnp.full((T, T), -10000.0, dtype=jnp.float32), k=1)
        attn = jax.nn.softmax(scores.astype(jnp.float32) + mask, axis=-1).astype(jnp.float16)
        out = jnp.einsum('bhts,bhsd->bhtd', attn, v)
        out = out.transpose(0, 2, 1, 3).reshape(B, T, E)
        return out @ wo.T + bo

    def _L0_ffn_ref(x, Ws, bs, Wg, Wu, Wd):
        import jax, jax.numpy as jnp
        import numpy as np
        D, F, E, K = (256, 688, 8, 2)
        b, n, d = x.shape
        xt = x.reshape(-1, d)
        logits = xt @ Ws + bs
        topk_w, topk_idx = jax.lax.top_k(logits, K)
        topk_w = jax.nn.softmax(topk_w, axis=-1)
        combine = jnp.sum(jax.nn.one_hot(topk_idx, E, dtype=xt.dtype) * topk_w[..., None], axis=1)
        g = jnp.einsum('td,edf->tef', xt, Wg)
        u = jnp.einsum('td,edf->tef', xt, Wu)
        h = jax.nn.silu(g) * u
        y = jnp.einsum('tef,efd->ted', h, Wd)
        out = jnp.einsum('ted,te->td', y, combine)
        return out.reshape(b, n, d)
    x = L0_attn_hidden_states
    x = x + _layernorm(_L0_attn_ref(_layernorm(x, axis=-1), L0_attn_wq, L0_attn_bq, L0_attn_wk, L0_attn_bk, L0_attn_wv, L0_attn_bv, L0_attn_wo, L0_attn_bo), axis=-1)
    x = x + _layernorm(_L0_ffn_ref(_layernorm(x, axis=-1), L0_ffn_Ws, L0_ffn_bs, L0_ffn_Wg, L0_ffn_Wu, L0_ffn_Wd), axis=-1)
    return x

_drawn_inputs = setup_inputs


def setup_inputs(seed=0):
    import zlib

    import numpy as np

    out = dict(_drawn_inputs(seed))
    spreads = {'L0_ffn_bs': (0.0, 0.1)}
    factors = {}
    for name, (base, spread) in spreads.items():
        noise = np.random.default_rng([zlib.crc32(name.encode()), seed]).standard_normal(out[name].shape)
        drawn = base * np.exp(spread * noise) if base else spread * noise
        out[name] = jnp.asarray(drawn.astype(out[name].dtype))
    for name, factor in factors.items():
        out[name] = (out[name] * factor).astype(out[name].dtype)
    return out
```

```python
from contextlib import ExitStack

import concourse.bass as bass
from concourse import mybir

ALU = mybir.AluOpType
ACT = mybir.ActivationFunctionType
AX = mybir.AxisListType
F32 = mybir.dt.float32
F16 = mybir.dt.float16
BF16 = mybir.dt.bfloat16
U32 = mybir.dt.uint32

P = 128
B, T, D = 8, 512, 256
H, HD = 16, 16
KD = D // P
QT = T // P
G, J = 4, 4
NT = B * QT
E, F = 8, 688
FC = -(-F // P)
FR = F - (FC - 1) * P
UNITS = QT * J
P_AT = [sum(T - P * (n // J) for n in range(i)) for i in range(UNITS + 1)]
P_COLS = P_AT[UNITS]
TOP = 2
TS = 2 * P
REGION = B * T + TS
TILES = (TOP * B * T + E * (TS - 1)) // TS
SPARE_TILES = TILES - TOP * B * T // TS
ROWS = E * REGION + (SPARE_TILES + 1) * TS
PV_LAG = 3
LN_EPS = 1e-5
LN_EPS16 = 2.0 ** -24 * 168
WSCALE = 256.0
HSCALE = 64.0
MASK = -10000.0
INV_SCALE = float(HD) ** 0.5


def hold(eng, sem, value, spare):
    eng.wait_ge(sem, value)
    eng.sem_inc(spare, 1)


class Chain:

    def __init__(self, eng, sem, spare):
        self.eng, self.sem, self.spare, self.base, self.n = eng, sem, spare, 0, 0

    def link(self, ins):
        ins.then_inc(self.sem, 1)
        self.n += 1
        hold(self.eng, self.sem, self.base + self.n, self.spare)

    def rebase(self, base):
        self.base, self.n = base, 0


def build(nc, x, wq, wk, wv, wo, bq, bk, bv, bo, ws, bs, wg, wu, wd, out):
    x1_dram = nc.dram_tensor("x1_rows", [NT * P, D], F16).ap()
    xs_dram = nc.dram_tensor("dispatch_rows", [ROWS, D], F16).ap()
    ys_dram = nc.dram_tensor("expert_rows", [(TILES + TILES % 2) * TS, D], F32).ap()
    outer = ExitStack()
    with outer:
        def sb(stack, name, shape, dt):
            return stack.enter_context(nc.sbuf_tensor(name, shape, dt))

        def sem(name):
            return outer.enter_context(nc.semaphore(name))

        spare = sem("spare")
        bank = [outer.enter_context(nc.psum_tensor(f"bank{i}", [P, 512], F32)) for i in range(8)]
        keep = {
            "ident": sb(outer, "ident", [P, P], F16),
            "wg": [sb(outer, f"wg_part{i}", [P, E * KD * F + P], F16) for i in range(2)],
            "wu": [sb(outer, f"wu_part{i}", [P, E * KD * F + P], F16) for i in range(2)],
            "wd": [sb(outer, f"wd_part{i}", [P, E * FC * D], F16) for i in range(2)],
            "slots": sb(outer, "slots", [P, NT * TOP], U32),
            "weights": sb(outer, "weights", [P, NT * TOP], F32),
            "fill": sb(outer, "fill", [P, E], F32),
            "first": sb(outer, "first", [P, E], F32),
        }
        attention(nc, sb, sem, spare, bank, keep, x, wq, wk, wv, wo, bq, bk, bv, bo, ws, bs, wg, wu, wd,
                  x1_dram, xs_dram)
        experts(nc, sb, sem, spare, bank, keep, xs_dram, ys_dram)
        combine(nc, sb, sem, spare, keep, x1_dram, ys_dram, out)
    return nc


def attention(nc, sb, sem, spare, bank, keep, x, wq, wk, wv, wo, bq, bk, bv, bo, ws, bs, wg, wu, wd,
              x1_dram, xs_dram):
    x_v = x.rearrange("b (t p) d -> b p t d", p=P)
    x1_v = x1_dram.rearrange("(b t p) d -> b p t d", t=QT, p=P)
    ident = keep["ident"]
    stack = ExitStack()
    with stack:
        identf = sb(stack, "identf", [P, P], F32)
        wq_sb = sb(stack, "wq_sb", [P, KD, G, P], F16)
        wk_sb = sb(stack, "wk_sb", [P, KD, G, P], F16)
        wv_sb = sb(stack, "wv_sb", [P, KD, D], F16)
        wo_sb = sb(stack, "wo_sb", [P, KD, D], F16)
        bq16 = sb(stack, "bq16", [P, G], F16)
        bk16 = sb(stack, "bk16", [P, G], F16)
        bq_sb = sb(stack, "bq_sb", [P, G], F32)
        bk_sb = sb(stack, "bk_sb", [P, G], F32)
        bv_sb = sb(stack, "bv_sb", [P, D], F16)
        bo_sb = sb(stack, "bo_sb", [P, D], F16)
        ws_f = sb(stack, "ws_f", [P, KD, E], F32)
        ws_r = sb(stack, "ws_r", [P, KD, E], F32)
        ws_part = sb(stack, "ws_part", [P, KD, 3, E], BF16)
        bs_sb = sb(stack, "bs_sb", [P, E], F32)
        mask_qk = sb(stack, "mask_qk", [P, P], F16)
        mask_kq = sb(stack, "mask_kq", [P, P], F16)
        before = sb(stack, "before", [P, P], F16)
        ones = sb(stack, "ones", [P, P], F16)
        power = sb(stack, "power", [P, 2, QT], F32)
        wscale = sb(stack, "wscale", [P, 1], F32)
        iota8 = sb(stack, "iota8", [P, E], F32)
        x_sb = sb(stack, "x_sb", [P, QT, D], F16)
        xr_sb = sb(stack, "xr_sb", [P, QT, D], F16)
        xn = sb(stack, "xn", [P, QT, D], F16)
        xnT = sb(stack, "xnT", [P, KD, T], F16)
        qT = sb(stack, "qT", [P, G, T], F16)
        kT = sb(stack, "kT", [P, G, T], F16)
        va = sb(stack, "va", [P, G, QT, J, 32], F16)
        v16 = sb(stack, "v16", [P, QT, J * HD], F16)
        nmax = sb(stack, "nmax", [P, 2, QT, P], F16)
        pT = sb(stack, "pT", [P, P_COLS], F16)
        ov = sb(stack, "ov", [P, T], F32)
        rden = sb(stack, "rden", [P, QT, J], F32)
        att = sb(stack, "att", [P, QT, D], F16)
        attT = sb(stack, "attT", [P, KD, T], F16)
        y = sb(stack, "y", [P, QT, D], F16)
        x1 = sb(stack, "x1", [P, QT, D], F16)
        xn2 = sb(stack, "xn2", [P, QT, D], F16)
        stats = sb(stack, "stats", [P, QT, 6], F32)
        mv = sb(stack, "mv", [P, QT, 2], F16)
        veps = sb(stack, "veps", [P, QT], F16)
        std = sb(stack, "std", [P, QT], F16)
        cen = sb(stack, "cen", [P, QT, D], F16)
        rstd = sb(stack, "rstd", [P, QT], F32)
        st_gu = sb(stack, "st_gu", [P, KD * F], F32)
        st_d = sb(stack, "st_d", [P, FC * D], F32)
        logit = sb(stack, "logit", [P, QT, E], F32)
        top = sb(stack, "top", [P, QT, E], F32)
        topi = sb(stack, "topi", [P, QT, E], U32)
        topf = sb(stack, "topf", [P, QT, TOP], F32)
        pick = [sb(stack, f"pick{r}", [P, QT, E], F32) for r in range(TOP)]
        both = sb(stack, "both", [P, QT, E], F16)
        dif = sb(stack, "dif", [P, QT], F32)
        e1 = sb(stack, "e1", [P, QT], F32)
        den = sb(stack, "den", [P, QT], F32)
        wts = sb(stack, "wts", [P, QT, TOP], F32)
        row = sb(stack, "row", [P, QT, E], F32)
        prow = [sb(stack, f"prow{r}", [P, QT, E], F32) for r in range(TOP)]
        slotf = sb(stack, "slotf", [P, QT, TOP], F32)
        slot = sb(stack, "slot", [P, QT, TOP], U32)

        S_BANK, ST_BANK = (bank[0], bank[1]), (bank[2], bank[3])
        PV_BANK, Q_BANK, K_BANK, M_BANK = bank[4], bank[5], bank[6], bank[7]
        M16 = M_BANK[:, :].bitcast(F16)
        LOGITS = K_BANK[:, 0:QT * E].rearrange("p (t e) -> p t e", t=QT)
        RANKS = K_BANK[:, 64:64 + QT * E].rearrange("p (t e) -> p t e", t=QT)
        TOTAL = K_BANK[:, 128:128 + E]

        w_in = sem("w_in")
        x_in = sem("x_in")
        xr_in = sem("xr_in")
        pool_const = sem("pool_const")
        const_ready = sem("const_ready")
        zero_ready = sem("zero_ready")
        bias_ready = sem("bias_ready")
        var_ready = sem("var_ready")
        veps_ready = sem("veps_ready")
        std_ready = sem("std_ready")
        cen_ready = sem("cen_ready")
        rstd_ready = sem("rstd_ready")
        xn_ready = sem("xn_ready")
        xnT_mm = sem("xnT_mm")
        xnT_ready = sem("xnT_ready")
        q_mm = sem("q_mm")
        q_out = sem("q_out")
        k_mm = sem("k_mm")
        k_out = sem("k_out")
        v_mm = sem("v_mm")
        v_out = sem("v_out")
        s_mm = sem("s_mm")
        s_max = sem("s_max")
        st_mm = sem("st_mm")
        p_ready = sem("p_ready")
        pv_mm = sem("pv_mm")
        ov_out = sem("ov_out")
        ot_mm = sem("ot_mm")
        att_out = sem("att_out")
        attT_mm = sem("attT_mm")
        attT_out = sem("attT_out")
        y_mm = sem("y_mm")
        y_out = sem("y_out")
        x1_ready = sem("x1_ready")
        xn2_ready = sem("xn2_ready")
        x1_out = sem("x1_out")
        xn2T_mm = sem("xn2T_mm")
        xn2T_out = sem("xn2T_out")
        logit_mm = sem("logit_mm")
        logit_out = sem("logit_out")
        both_ready = sem("both_ready")
        dif_ready = sem("dif_ready")
        e1_ready = sem("e1_ready")
        rank_mm = sem("rank_mm")
        rank_out = sem("rank_out")
        slot_ready = sem("slot_ready")
        scattered = sem("scattered")
        xn2_free = sem("xn2_free")
        zeros_out = sem("zeros_out")
        dve_chain = sem("dve_chain")
        ws_chain = sem("ws_chain")
        v16_ready = sem("v16_ready")
        y16_ready = sem("y16_ready")
        g_in = sem("g_in")
        d_in = sem("d_in")
        u_in = sem("u_in")
        hi_ready = sem("hi_ready")
        mul_ready = sem("mul_ready")
        lo_ready = sem("lo_ready")

        AT_TRANSPOSE_O, AT_MAXIMA, AT_FIN = 7, 9, 14
        STEPS = 18

        LAST = G * (B - 1)

        def q_uses(grp, in_last):
            return 5 + 2 * grp if not in_last else 5 + 2 * LAST + (grp - LAST)

        with nc.Block() as block:
            @block.sync
            def _(sp):
                def load_x(dst, b, signal):
                    sp.dma_start(dst[:, :, :], x_v[b, :, :, :]).then_inc(signal, 16)

                def load_gu(src, e, signal):
                    sp.dma_start(st_gu[:, :].rearrange("p (k f) -> p k f", k=KD),
                                 src[e, :, :].rearrange("(k p) f -> p k f", p=P)).then_inc(signal, 16)

                def load_d(e):
                    sp.dma_start(st_d[:, 0:(FC - 1) * D].rearrange("p (c d) -> p c d", c=FC - 1),
                                 wd[e, 0:(FC - 1) * P, :].rearrange("(c p) d -> p c d", p=P)).then_inc(d_in, 16)
                    sp.dma_start(st_d[0:FR, (FC - 1) * D:FC * D], wd[e, (FC - 1) * P:F, :]).then_inc(d_in, 16)

                def batch(b, first, in_last, more_x):
                    hold(sp, lo_ready, 3 * b + 1, spare)
                    load_gu(wu, b, u_in)
                    if not first:
                        hold(sp, x1_ready, b, spare)
                        sp.dma_start(x1_v[b - 1, :, :, :], x1[:, :, :]).then_inc(x1_out, 16)
                    load_x(xr_sb, b, xr_in)
                    if not in_last:
                        hold(sp, xn_ready, b + 2, spare)
                        if more_x:
                            load_x(x_sb, b + 2, x_in)
                        hold(sp, lo_ready, 3 * b + 2, spare)
                        load_d(b + 1)
                        hold(sp, lo_ready, 3 * b + 3, spare)
                        load_gu(wg, b + 1, g_in)

                sp.sem_inc(x1_out, 16)
                load_x(x_sb, 0, x_in)
                for dst, src in ((wq_sb[:, :, :, :], wq), (wk_sb[:, :, :, :], wk), (wv_sb[:, :, :], wv),
                                 (wo_sb[:, :, :], wo), (bq16[:, :], bq), (bk16[:, :], bk),
                                 (bv_sb[:, :], bv.partition_broadcast(P)),
                                 (bo_sb[:, :], bo.partition_broadcast(P)),
                                 (ws_f[:, :, :], ws.rearrange("(k p) e -> p k e", p=P)),
                                 (bs_sb[:, :], bs.partition_broadcast(P))):
                    sp.dma_start(dst, src).then_inc(w_in, 16)
                load_gu(wg, 0, g_in)
                sp.wait_ge(zero_ready, 1)
                load_d(0)
                sp.wait_ge(xn_ready, 1)
                load_x(x_sb, 1, x_in)
                sp.wait_ge(zero_ready, 2)
                sp.dma_start(xs_dram[E * REGION:, :].rearrange("(p r) d -> p (r d)", p=P),
                             pT[:, 0:(SPARE_TILES + 1) * TS * D // P]).then_inc(zeros_out, 16)
                batch(0, True, False, True)
                with sp.Fori(1, B - 2) as b:
                    batch(b, False, False, True)
                batch(B - 2, False, False, False)
                batch(B - 1, False, True, False)
                sp.wait_ge(x1_ready, B)
                sp.dma_start(x1_v[B - 1, :, :, :], x1[:, :, :]).then_inc(x1_out, 16)
                sp.wait_ge(x1_out, 16 * B + 16)
                sp.wait_ge(zeros_out, 16)

            @block.gpsimd
            def _(pool):
                gp = nc.gpsimd
                ch = Chain(pool, pool_const, spare)
                ch.link(gp.memset(power[:, 0, :], 0.5))
                ch.link(gp.memset(power[:, 1, :], -1.0))
                ch.link(gp.memset(wscale[:, :], WSCALE))
                ch.link(gp.memset(ones[:, :], 1.0))
                ch.link(gp.iota(iota8[:, :], [[1, E]], base=0, channel_multiplier=0,
                                allow_small_or_imprecise_dtypes=True))
                ch.link(gp.iota(keep["fill"][:, :], [[REGION, E]], base=0, channel_multiplier=0,
                                allow_small_or_imprecise_dtypes=True))
                ch.link(gp.iota(keep["first"][:, :], [[REGION, E]], base=0, channel_multiplier=0,
                                allow_small_or_imprecise_dtypes=True))
                for m in (ident, identf):
                    ch.link(gp.memset(m[:, :], 0.0))
                    ch.link(gp.affine_select(out=m[:, :], in_=m[:, :], compare_op=ALU.not_equal, fill=1.0,
                                             base=0, pattern=[[-1, P]], channel_multiplier=1))
                ch.link(gp.memset(before[:, :], 0.0))
                ch.link(gp.affine_select(out=before[:, :], in_=before[:, :], compare_op=ALU.is_ge, fill=1.0,
                                         base=0, pattern=[[-1, P]], channel_multiplier=1))
                for m, row_is_query in ((mask_qk, 1), (mask_kq, -1)):
                    ch.link(gp.memset(m[:, :], 0.0))
                    ch.link(gp.affine_select(out=m[:, :], in_=m[:, :], compare_op=ALU.is_ge,
                                             fill=MASK * INV_SCALE, base=0, pattern=[[-row_is_query, P]],
                                             channel_multiplier=row_is_query))
                for part in (*keep["wg"], *keep["wu"]):
                    ch.link(gp.memset(part[:, E * KD * F:], 0.0))
                for g in range(G):
                    ch.link(gp.memset(va[:, g, :, :, HD:32], 0.0))
                    last = gp.memset(va[:, g, :, :, HD:HD + 1], 1.0)
                    if g < G - 1:
                        ch.link(last)
                last.then_inc(const_ready, 1)

                def rsqrt(n):
                    hold(pool, var_ready, n + 1, spare)
                    gp.tensor_scalar(veps[:, :], mv[:, :, 1], LN_EPS16, None, ALU.add).then_inc(veps_ready, 1)
                    pool.wait_ge(veps_ready, n + 1)
                    gp.tensor_tensor(std[:, :], veps[:, :], power[:, 0, :], ALU.pow).then_inc(std_ready, 1)
                    pool.wait_ge(std_ready, n + 1)
                    gp.tensor_tensor(rstd[:, :], std[:, :], power[:, 1, :], ALU.pow).then_inc(rstd_ready, 1)

                def rest(stage, parts, start, n, count):
                    pool.wait_ge(hi_ready, count + 1)
                    gp.tensor_tensor(stage[:, :], stage[:, :], wscale[:, 0:1].broadcast_to([P, n]),
                                     ALU.mult).then_inc(mul_ready, 1)
                    hold(pool, mul_ready, count + 1, spare)
                    gp.tensor_tensor(parts[1][:, bass.ds(start, n)], stage[:, :], parts[0][:, bass.ds(start, n)],
                                     ALU.subtract).then_inc(lo_ready, 1)

                def scatter(b):
                    hold(pool, slot_ready, b + 1, spare)
                    for t in range(QT):
                        for r in range(TOP):
                            gp.indirect_dma_start(
                                out=xs_dram[:, :], in_=xn2[:, t, :], in_offset=None,
                                out_offset=bass.IndirectOffsetOnAxis(ap=slot[:, t, r:r + 1], axis=0),
                            ).then_inc(scattered, 16)
                    pool.wait_ge(scattered, 16 * TOP * QT * (b + 1))
                    pool.sem_inc(xn2_free, 1)

                def batch(b, first, in_last):
                    if not in_last:
                        rsqrt(1 if first else 3 * b - 1)
                    rest(st_gu, keep["wg"], b * (KD * F), KD * F, 3 * b)
                    if not first:
                        rsqrt(3 * b - (1 if in_last else 0))
                        rsqrt(3 * b + 1 - (1 if in_last else 0))
                    rest(st_d, keep["wd"], b * (FC * D), FC * D, 3 * b + 1)
                    rest(st_gu, keep["wu"], b * (KD * F), KD * F, 3 * b + 2)
                    if not first:
                        scatter(b - 1)

                pool.sem_inc(xn2_free, 1)
                rsqrt(0)
                batch(0, True, False)
                with pool.Fori(1, B - 1) as b:
                    batch(b, False, False)
                batch(B - 1, False, True)
                rsqrt(3 * B - 2)
                rsqrt(3 * B - 1)
                scatter(B - 1)

            @block.scalar
            def _(act):
                sc = nc.scalar
                act.wait_ge(w_in, 16 * 10)
                sc.activation(bq_sb[:, :], bq16[:, :], ACT.Copy).then_inc(bias_ready, 1)
                sc.activation(bk_sb[:, :], bk16[:, :], ACT.Copy).then_inc(bias_ready, 1)
                act.wait_ge(bias_ready, 2)
                m16 = M16.rearrange("p (k t) -> p k t", k=KD)

                def take_xnT(b):
                    act.wait_ge(xnT_mm, b + 1)
                    sc.activation(xnT[:, :, :], m16, ACT.Copy).then_inc(xnT_ready, 1)

                def take_q(use, g):
                    act.wait_ge(q_mm, use + 1)
                    sc.activation(qT[:, g, :], Q_BANK[:, :], ACT.Identity, bias=bq_sb[:, g:g + 1]).then_inc(q_out, 1)

                def take_q_max(use, g):
                    act.wait_ge(q_mm, use + 1)
                    sc.activation(qT[:, g, :], Q_BANK[:, :], ACT.Copy).then_inc(q_out, 1)

                def take_ov(grp):
                    act.wait_ge(pv_mm, UNITS * (grp + 2))
                    act.wait_ge(ot_mm, grp + 1)
                    sc.activation(ov[:, :], PV_BANK[:, :], ACT.Copy).then_inc(ov_out, 1)

                def part(b, which):
                    stage, parts, width, signal, amount = (
                        (st_gu, keep["wg"], KD * F, g_in, 16), (st_d, keep["wd"], FC * D, d_in, 32),
                        (st_gu, keep["wu"], KD * F, u_in, 16))[which]
                    act.wait_ge(signal, amount * b + amount)
                    sc.activation(parts[0][:, bass.ds(b * width, width)], stage[:, :], ACT.Copy,
                                  scale=WSCALE).then_inc(hi_ready, 1)

                def take_attT(b):
                    act.wait_ge(attT_mm, b + 1)
                    sc.activation(attT[:, :, :], m16, ACT.Copy).then_inc(attT_out, 1)

                def take_xn2T(b):
                    act.wait_ge(xn2T_mm, b + 1)
                    sc.activation(attT[:, :, :], m16, ACT.Copy).then_inc(xn2T_out, 1)

                def weight(b):
                    act.wait_ge(dif_ready, b + 1)
                    sc.activation(e1[:, :], dif[:, :], ACT.Exp).then_inc(e1_ready, 1)

                def batch(b, first, in_last):
                    for g in range(G):
                        grp = G * b + g
                        for i in range(UNITS):
                            n = T - P * (i // J)
                            act.wait_ge(st_mm, UNITS * grp + i + 1)
                            act.wait_ge(pv_mm, UNITS * grp + i + 1)
                            sc.activation(pT[:, P_AT[i]:P_AT[i + 1]], ST_BANK[i % 2][:, 0:n], ACT.Exp,
                                          scale=1.0 / INV_SCALE).then_inc(p_ready, 1)
                            if i == AT_MAXIMA + 2 and not (in_last and g == G - 1):
                                take_q_max(q_uses(grp, in_last), (g + 1) % G)
                            if i == 4 and g == 1 and not first:
                                take_attT(b - 1)
                            if i == AT_FIN - 1 and g == 2 and not first:
                                take_xn2T(b - 1)
                            if i == 12 and g == 3 and not first:
                                weight(b - 1)
                            if i == 6 and g < 3:
                                part(b, g)
                        if not in_last:
                            if g == 0:
                                take_xnT(b + 1)
                            take_q(q_uses(grp, False) + 1, g)
                        take_ov(grp)

                take_xnT(0)
                act.wait_ge(zeros_out, 16)
                for g in range(G - 1):
                    take_q(g, g)
                take_q_max(3, 0)
                take_q(4, G - 1)
                batch(0, True, False)
                with act.Fori(1, B - 1) as b:
                    batch(b, False, False)
                batch(B - 1, False, True)
                take_attT(B - 1)
                take_xn2T(B - 1)
                weight(B - 1)

            @block.vector
            def _(dve):
                v = nc.vector
                ch = Chain(dve, dve_chain, spare)
                wch = Chain(dve, ws_chain, spare)
                v.memset(st_d[:, (FC - 1) * D:FC * D], 0.0).then_inc(zero_ready, 1)
                v.memset(pT[:, :], 0.0).then_inc(zero_ready, 1)
                v.memset(nmax[:, 0, :, :], 0.0).then_inc(p_ready, 2)
                v.memset(nmax[:, 1, :, :], 0.0).then_inc(pv_mm, UNITS)
                dve.sem_inc(ot_mm, 1)

                def norm(src, dst, n):
                    for t in range(QT):
                        last = v.bn_stats(stats[:, t, :], src[:, t, :])
                    ch.link(last)
                    for t in range(QT):
                        last = v.bn_aggr(mv[:, t, :], stats[:, t, :])
                    last.then_inc(var_ready, 1)
                    dve.wait_ge(var_ready, n + 1)
                    for t in range(QT):
                        last = v.tensor_scalar(cen[:, t, :], src[:, t, :], mv[:, t, 0:1], None, ALU.subtract)
                    last.then_inc(cen_ready, 1)
                    dve.wait_ge(cen_ready, n + 1)
                    dve.wait_ge(rstd_ready, n + 1)
                    for t in range(QT):
                        last = v.tensor_scalar(dst[:, t, :], cen[:, t, :], rstd[:, t:t + 1], None, ALU.mult)
                    return last

                def norm_x(b, n):
                    dve.wait_ge(x_in, 16 * b + 16)
                    norm(x_sb, xn, n).then_inc(xn_ready, 1)

                def take_k(grp, g):
                    dve.wait_ge(k_mm, grp + 1)
                    v.tensor_scalar(kT[:, g, :], K_BANK[:, :], bk_sb[:, g:g + 1], None, ALU.add).then_inc(k_out, 1)

                def take_v(grp, g):
                    dve.wait_ge(v_mm, grp + 1)
                    v.tensor_copy(v16[:, :, :], M_BANK[:, 0:QT * J * HD].rearrange("p (t c) -> p t c", t=QT)
                                  ).then_inc(v16_ready, 1)
                    dve.wait_ge(v16_ready, grp + 1)
                    for t in range(QT):
                        last = v.tensor_tensor(va[:, g, t, :, 0:HD],
                                               v16[:, t, :].rearrange("p (j d) -> p j d", j=J),
                                               bv_sb[:, 64 * g:64 * (g + 1)].rearrange("p (j d) -> p j d", j=J), ALU.add)
                    last.then_inc(v_out, 1)

                def maxima(grp, g, i):
                    qt, col = i // J, 32 * (i % J) + HD
                    dve.wait_ge(s_mm, UNITS * grp + i + 1)
                    v.reduce_max(nmax[:, g % 2, qt, col:col + 1], S_BANK[i % 2][:, 0:P * (qt + 1)], AX.X,
                                 negate=True).then_inc(s_max, 1)

                def take_att(grp, g):
                    dve.wait_ge(ot_mm, grp + 2)
                    o = M_BANK[:, :].rearrange("p (t j c) -> p t j c", t=QT, j=J)
                    ch.link(v.reciprocal(rden[:, :, :], o[:, :, :, HD]))
                    for t in range(QT):
                        last = v.tensor_tensor(att[:, t, 64 * g:64 * (g + 1)].rearrange("p (j d) -> p j d", j=J),
                                               o[:, t, :, 0:HD],
                                               rden[:, t, :].unsqueeze(2).broadcast_to([P, J, HD]), ALU.mult)
                    last.then_inc(att_out, 1)

                def finish(b, n):
                    for half in range(2):
                        dve.wait_ge(y_mm, 2 * b + half + 1)
                        v.tensor_copy(y[:, 2 * half:2 * half + 2, :],
                                      (Q_BANK, K_BANK)[half][:, :].rearrange("p (t d) -> p t d", t=2)
                                      ).then_inc(y_out, 1)
                    dve.wait_ge(y_out, 2 * b + 2)
                    for t in range(QT):
                        last = v.tensor_tensor(y[:, t, :], y[:, t, :], bo_sb[:, :], ALU.add)
                    last.then_inc(y16_ready, 1)
                    dve.wait_ge(y16_ready, b + 1)
                    ch.link(norm(y, y, n))
                    dve.wait_ge(xr_in, 16 * b + 16)
                    dve.wait_ge(x1_out, 16 * b + 16)
                    v.tensor_tensor(x1[:, :, :], xr_sb[:, :, :], y[:, :, :], ALU.add).then_inc(x1_ready, 1)
                    dve.wait_ge(x1_ready, b + 1)
                    dve.wait_ge(xn2_free, b + 1)
                    norm(x1, xn2, n + 1).then_inc(xn2_ready, 1)

                def route(b):
                    dve.wait_ge(logit_mm, b + 1)
                    v.tensor_tensor(logit[:, :, :], LOGITS, bs_sb[:, :].unsqueeze(1).broadcast_to([P, QT, E]),
                                    ALU.add).then_inc(logit_out, 1)
                    hold(dve, logit_out, b + 1, spare)
                    for t in range(QT):
                        last = v.max(top[:, t, :], logit[:, t, :])
                    ch.link(last)
                    v.tensor_tensor(dif[:, :], top[:, :, 1], top[:, :, 0], ALU.subtract).then_inc(dif_ready, 1)
                    for t in range(QT):
                        last = v.max_index(topi[:, t, :], top[:, t, :], logit[:, t, :])
                    ch.link(last)
                    ch.link(v.tensor_copy(topf[:, :, :], topi[:, :, 0:TOP]))
                    for r in range(TOP):
                        last = v.tensor_tensor(pick[r][:, :, :], iota8[:, :].unsqueeze(1).broadcast_to([P, QT, E]),
                                               topf[:, :, r:r + 1].broadcast_to([P, QT, E]), ALU.is_equal)
                    ch.link(last)
                    v.tensor_tensor(both[:, :, :], pick[0][:, :, :], pick[1][:, :, :], ALU.add).then_inc(both_ready, 1)

                def slots(b):
                    dve.wait_ge(rank_mm, b + 1)
                    ch.link(v.tensor_tensor(row[:, :, :], RANKS, keep["fill"][:, :].unsqueeze(1).broadcast_to([P, QT, E]),
                                            ALU.add))
                    v.tensor_tensor(keep["fill"][:, :], keep["fill"][:, :], TOTAL, ALU.add).then_inc(rank_out, 1)
                    for r in range(TOP):
                        last = v.tensor_tensor(prow[r][:, :, :], row[:, :, :], pick[r][:, :, :], ALU.mult)
                    ch.link(last)
                    for r in range(TOP):
                        last = v.reduce_sum(slotf[:, :, r], prow[r][:, :, :], AX.X)
                    ch.link(last)
                    v.tensor_copy(slot[:, :, :], slotf[:, :, :]).then_inc(slot_ready, 1)
                    at = bass.ds(b * (QT * TOP), QT * TOP)
                    v.tensor_copy(keep["slots"][:, at], slotf[:, :, :].rearrange("p t r -> p (t r)"))
                    dve.wait_ge(e1_ready, b + 1)
                    ch.link(v.tensor_scalar(den[:, :], e1[:, :], 1.0, None, ALU.add))
                    ch.link(v.reciprocal(wts[:, :, 0], den[:, :]))
                    ch.link(v.tensor_tensor(wts[:, :, 1], e1[:, :], wts[:, :, 0], ALU.mult))
                    v.tensor_copy(keep["weights"][:, at], wts[:, :, :].rearrange("p t r -> p (t r)"))

                def batch(b, first, in_last):
                    for g in range(G):
                        grp = G * b + g
                        ahead = not (in_last and g >= 2)
                        if ahead:
                            dve.wait_ge(q_mm, 4 + 2 * grp)
                        for i in range(UNITS):
                            if ahead:
                                maxima(grp + 2, (g + 2) % G, i)
                            if i == AT_TRANSPOSE_O + 1 and not (first and g == 0):
                                take_att(grp - 1, (g - 1) % G)
                            if i == 3 and g == 0 and not in_last:
                                dve.wait_ge(xnT_mm, b + 1)
                                norm_x(b + 1, 1 if first else 3 * b - 1)
                            if i == 6 and g == 3 and not first:
                                route(b - 1)
                        if g == 1 and not first:
                            finish(b - 1, 3 * b - (1 if in_last else 0))
                        if g == 3 and not first:
                            slots(b - 1)
                        if not in_last:
                            take_k(grp + G, g)
                            take_v(grp + G, g)

                norm_x(0, 0)
                dve.wait_ge(bias_ready, 2)
                dve.wait_ge(w_in, 16 * 10)
                dve.wait_ge(const_ready, 1)
                for g in range(G - 1):
                    take_k(g, g)
                    take_v(g, g)
                dve.wait_ge(pv_mm, UNITS)
                for i in range(UNITS):
                    maxima(0, 0, i)
                take_k(G - 1, G - 1)
                take_v(G - 1, G - 1)
                for i in range(UNITS):
                    maxima(1, 1, i)
                for n in range(3):
                    src = ws_f if n == 0 else ws_r
                    wch.link(v.tensor_copy(ws_part[:, :, n, :], src[:, :, :]))
                    if n < 2:
                        wch.link(v.tensor_tensor(ws_r[:, :, :], src[:, :, :], ws_part[:, :, n, :], ALU.subtract))
                batch(0, True, False)
                start = ch.n
                with dve.Fori(1, B - 1) as b:
                    ch.rebase(start + STEPS * (b - 1))
                    batch(b, False, False)
                    assert ch.n == STEPS, ch.n
                ch.rebase(start + STEPS * (B - 2))
                batch(B - 1, False, True)
                take_att(G * B - 1, G - 1)
                finish(B - 1, 3 * B - 2)
                route(B - 1)
                slots(B - 1)

            @block.tensor
            def _(pe):
                mm = nc.tensor.matmul

                def transpose4(src, signal):
                    for k in range(KD):
                        for t in range(QT):
                            last = nc.tensor.transpose(M16[:, T * k + P * t:T * k + P * (t + 1)],
                                                       src[:, t, P * k:P * (k + 1)], ident[:, :])
                    last.then_inc(signal, 1)

                def project_q(g):
                    for k in range(KD):
                        last = mm(Q_BANK[:, :], wq_sb[:, k, g, :], xnT[:, k, :], start=(k == 0), stop=(k == KD - 1))
                    last.then_inc(q_mm, 1)

                def project_k(g):
                    for k in range(KD):
                        last = mm(K_BANK[:, :], wk_sb[:, k, g, :], xnT[:, k, :], start=(k == 0), stop=(k == KD - 1))
                    last.then_inc(k_mm, 1)

                def project_v(g):
                    for t in range(QT):
                        for k in range(KD):
                            last = mm(M_BANK[:, 64 * t:64 * (t + 1)], xnT[:, k, P * t:P * (t + 1)],
                                      wv_sb[:, k, 64 * g:64 * (g + 1)], start=(k == 0), stop=(k == KD - 1))
                    last.then_inc(v_mm, 1)

                def scores_qk(g, i):
                    qt, r = i // J, 32 * (i % J)
                    n = P * (qt + 1)
                    out = S_BANK[i % 2]
                    mm(out[:, 0:n], qT[r:r + 32, g, P * qt:P * (qt + 1)], kT[r:r + 32, g, 0:n],
                       start=True, stop=False)
                    mm(out[:, n - P:n], ident[:, :], mask_qk[:, :], start=False, stop=True).then_inc(s_mm, 1)

                def scores_kq(g, i):
                    kt, r = i // J, 32 * (i % J)
                    out = ST_BANK[i % 2]
                    mm(out[:, 0:T - P * kt], kT[r:r + 32, g, P * kt:P * (kt + 1)], qT[r:r + 32, g, P * kt:T],
                       start=True, stop=False)
                    mm(out[:, 0:P], ident[:, :], mask_kq[:, :], start=False, stop=True).then_inc(st_mm, 1)

                def add_maxima(g):
                    mm(Q_BANK[:, :], ident[:, :], qT[:, g, :], start=True, stop=False)
                    for t in range(QT):
                        last = mm(Q_BANK[:, P * t:P * (t + 1)], nmax[:, g % 2, t, :], ident[:, :],
                                  start=False, stop=(t == QT - 1))
                    last.then_inc(q_mm, 1)

                def values(grp, g, i):
                    kt, j = i // J, i % J
                    pe.wait_ge(p_ready, UNITS * grp + i + 3)
                    mm(PV_BANK[32 * j:32 * j + 32, P * kt:T], va[:, g, kt, j, :], pT[:, P_AT[i]:P_AT[i + 1]],
                       start=(kt == 0), stop=(kt == QT - 1), tile_position=(0, 32 * j)).then_inc(pv_mm, 1)

                def transpose_o(grp):
                    pe.wait_ge(ov_out, grp + 1)
                    for t in range(QT):
                        last = nc.tensor.transpose(M_BANK[:, P * t:P * (t + 1)], ov[:, P * t:P * (t + 1)],
                                                   identf[:, :])
                    last.then_inc(ot_mm, 1)

                def project_out(b):
                    pe.wait_ge(attT_out, b + 1)
                    for t in range(QT):
                        for k in range(KD):
                            last = mm((Q_BANK, K_BANK)[t // 2][:, D * (t % 2):D * (t % 2 + 1)],
                                      attT[:, k, P * t:P * (t + 1)], wo_sb[:, k, :],
                                      start=(k == 0), stop=(k == KD - 1))
                        if t % 2:
                            last.then_inc(y_mm, 1)

                def logits(b):
                    pe.wait_ge(xn2T_out, b + 1)
                    for t in range(QT):
                        for s in range(3 * KD):
                            last = mm(LOGITS[:, t, :], attT[:, s // 3, P * t:P * (t + 1)], ws_part[:, s // 3, s % 3, :],
                                      start=(s == 0), stop=(s == 3 * KD - 1))
                    last.then_inc(logit_mm, 1)

                def ranks(b):
                    pe.wait_ge(both_ready, b + 1)
                    for t in range(QT):
                        for s in range(t + 1):
                            mm(RANKS[:, t, :], (before if s == t else ones)[:, :], both[:, s, :],
                               start=(s == 0), stop=(s == t))
                    for s in range(QT):
                        last = mm(TOTAL, ones[:, :], both[:, s, :], start=(s == 0), stop=(s == QT - 1))
                    last.then_inc(rank_mm, 1)

                def batch(b, first, in_last):
                    for g in range(G):
                        grp = G * b + g
                        ahead = not (in_last and g >= 2)
                        pe.wait_ge(q_out, 4 + 2 * grp if not (in_last and g) else q_uses(grp, True))
                        if ahead:
                            pe.wait_ge(k_out, grp + 3)
                        for i in range(UNITS):
                            pe.wait_ge(p_ready, UNITS * grp + i + 1)
                            scores_kq(g, i)
                            if ahead:
                                pe.wait_ge(s_max, UNITS * (grp + 2) + i - 1)
                                scores_qk((g + 2) % G, i)
                            if i == PV_LAG and not (first and g == 0):
                                pe.wait_ge(ov_out, grp)
                            if i >= PV_LAG:
                                values(grp, g, i - PV_LAG)
                            if i == 2 and g == 1 and not first:
                                pe.wait_ge(att_out, grp - 1)
                                if not in_last:
                                    pe.wait_ge(v_out, grp + 4)
                                transpose4(att, attT_mm)
                            if i == AT_TRANSPOSE_O and not (first and g == 0):
                                if g == 1 and not first:
                                    pe.wait_ge(attT_out, b)
                                elif g == 3 and in_last:
                                    pe.wait_ge(xn2T_out, b)
                                elif g and in_last:
                                    pe.wait_ge(att_out, grp - 1)
                                else:
                                    pe.wait_ge(v_out, grp + 4)
                                transpose_o(grp - 1)
                            if i == 11 and g == 2 and not first:
                                pe.wait_ge(att_out, grp)
                                pe.wait_ge(xn2_ready, b)
                                transpose4(xn2, xn2T_mm)
                            if i == 3 and g == 3 and not first:
                                if not in_last:
                                    pe.wait_ge(k_out, grp + 4)
                                logits(b - 1)
                            if i == 13 and g == 3 and not first:
                                ranks(b - 1)
                            if i == AT_MAXIMA and not (in_last and g == G - 1):
                                pe.wait_ge(s_max, UNITS * (grp + 2))
                                pe.wait_ge(q_out, q_uses(grp, in_last))
                                add_maxima((g + 1) % G)
                            if i == AT_FIN and g == 1 and not first:
                                pe.wait_ge(q_out, q_uses(grp, in_last) + 1)
                                pe.wait_ge(k_out, grp + 4 if not in_last else G * B)
                                project_out(b - 1)
                        if not in_last:
                            if g == 0:
                                pe.wait_ge(xn_ready, b + 2)
                                if first:
                                    pe.wait_ge(v_out, grp + 4)
                                else:
                                    pe.wait_ge(att_out, grp)
                                transpose4(xn, xnT_mm)
                                pe.wait_ge(xnT_ready, b + 2)
                            pe.wait_ge(q_out, q_uses(grp, False) + 1)
                            if g == 1 and not first:
                                pe.wait_ge(y_out, 2 * b)
                            project_q(g)
                            pe.wait_ge(k_out, grp + 4)
                            if g == 3 and not first:
                                pe.wait_ge(rank_out, b)
                            project_k(g)
                        for i in range(UNITS - PV_LAG, UNITS):
                            values(grp, g, i)
                        if not in_last:
                            if g > 0:
                                pe.wait_ge(att_out, grp)
                            if g == 2 and not first:
                                pe.wait_ge(xn2T_out, b)
                            project_v(g)
                        elif g == 1:
                            pe.wait_ge(y_out, 2 * b)

                pe.wait_ge(const_ready, 1)
                pe.wait_ge(xn_ready, 1)
                transpose4(xn, xnT_mm)
                pe.wait_ge(w_in, 16 * 10)
                pe.wait_ge(xnT_ready, 1)

                def first_projections(g, use):
                    if use:
                        pe.wait_ge(q_out, use)
                    project_q(g)
                    if g:
                        pe.wait_ge(k_out, g)
                    project_k(g)
                    if g:
                        pe.wait_ge(v_out, g)
                    project_v(g)

                def first_scores(grp):
                    pe.wait_ge(k_out, grp + 1)
                    for i in range(UNITS):
                        n = UNITS * grp + i
                        if n >= 2:
                            pe.wait_ge(s_max, n - 1)
                        scores_qk(grp, i)

                for g in range(G - 1):
                    first_projections(g, g)
                pe.wait_ge(q_out, G - 1)
                first_scores(0)
                pe.wait_ge(s_max, UNITS)
                add_maxima(0)
                first_projections(G - 1, G)
                first_scores(1)
                batch(0, True, False)
                with pe.Fori(1, B - 1) as b:
                    batch(b, False, False)
                batch(B - 1, False, True)
                pe.wait_ge(att_out, G * B - 1)
                transpose_o(G * B - 1)
                pe.wait_ge(att_out, G * B)
                transpose4(att, attT_mm)
                project_out(B - 1)
                pe.wait_ge(xn2_ready, B)
                transpose4(xn2, xn2T_mm)
                pe.wait_ge(y_out, 2 * B)
                logits(B - 1)
                ranks(B - 1)


def experts(nc, sb, sem, spare, bank, keep, xs_dram, ys_dram):
    NTILE = TILES + TILES % 2
    TT = TS // P
    CP = FC // 2
    M_MAX = B * T // TS
    ident, wg_part, wu_part, wd_part = keep["ident"], keep["wg"], keep["wu"], keep["wd"]
    stack = ExitStack()
    with stack:
        iota_m = sb(stack, "iota_m", [P, M_MAX], F32)
        iota_i = sb(stack, "iota_i", [P, NTILE], F32)
        iota_p = sb(stack, "iota_p", [P, TT], F32)
        one8 = sb(stack, "one8", [P, E], F32)
        zrow = sb(stack, "zrow", [P, D], F16)
        count = sb(stack, "count", [P, E], F32)
        over = sb(stack, "over", [P, E, M_MAX], F32)
        tiles = sb(stack, "tiles", [P, E], F32)
        cum = sb(stack, "cum", [P, E], F32)
        past = sb(stack, "past", [P, NTILE, E], F32)
        pastn = sb(stack, "pastn", [P, NTILE, E], F32)
        own = sb(stack, "own", [P, NTILE], F32)
        begun = sb(stack, "begun", [P, NTILE], F32)
        rowf = sb(stack, "rowf", [P, NTILE], F32)
        ownc = sb(stack, "ownc", [P, NTILE], F32)
        table = sb(stack, "table", [P, 3, NTILE], U32)
        shift = sb(stack, "shift", [P, E - 1], F32)
        beyond = sb(stack, "beyond", [P, NT * TOP, E - 1], F32)
        moved = sb(stack, "moved", [P, NT * TOP], F32)
        padf = sb(stack, "padf", [P, TT, E], F32)
        pad = sb(stack, "pad", [P, TT, E], U32)
        xin = [sb(stack, f"xin{j}", [P, TT, D], F16) for j in range(2)]
        xT = [sb(stack, f"xT{j}", [P, KD, TS], F16) for j in range(2)]
        act_g = sb(stack, "act_g", [P, CP, 2 * TS], F32)
        hid = sb(stack, "hid", [P, CP, 2 * TS], F32)
        h1 = sb(stack, "h1", [P, CP, 2 * TS], F16)
        h2 = sb(stack, "h2", [P, CP, 2 * TS], F16)
        y_sb = [sb(stack, f"y_sb{j}", [P, TT, D], F32) for j in range(2)]

        G_BANK, U_BANK, Y_BANK = bank[0:3], bank[3:6], bank[6:8]
        XT16 = Y_BANK[0][:, D:2 * D].bitcast(F16)

        consts = sem("consts")
        plan = sem("plan")
        table_ready = sem("table_ready")
        pad_ready = sem("pad_ready")
        padded = sem("padded")
        xin_in = [sem(f"xin_in{j}") for j in range(2)]
        xT_mm = sem("xT_mm")
        xT_ready = sem("xT_ready")
        up_mm = sem("up_mm")
        silu_ready = sem("silu_ready")
        hid_ready = sem("hid_ready")
        h1_ready = sem("h1_ready")
        h2_ready = sem("h2_ready")
        down_mm = sem("down_mm")
        y_ready = sem("y_ready")
        ys_out = [sem(f"ys_out{j}") for j in range(2)]

        def rows_of(dram, row):
            return dram[bass.ds(row, TS), :].rearrange("(t p) d -> p t d", p=P)

        with nc.Block() as block:
            @block.sync
            def _(sp):
                def load(h, j):
                    row = sp.value_load(table[0:1, 0, bass.ds(2 * h + j, 1)], min_val=0, max_val=ROWS - TS)
                    sp.dma_start(xin[j][:, :, :], rows_of(xs_dram, row)).then_inc(xin_in[j], 16)

                def store(h, j):
                    hold(sp, y_ready, 2 * h + j + 2, spare)
                    sp.dma_start(rows_of(ys_dram, (2 * h + j) * TS), y_sb[j][:, :, :]).then_inc(ys_out[j], 16)

                for j in range(2):
                    sp.sem_inc(ys_out[j], 16)
                sp.wait_ge(table_ready, 1)
                sp.wait_ge(padded, 16 * TT * E)
                for j in range(2):
                    load(0, j)
                with sp.Fori(0, NTILE // 2 - 1) as h:
                    for j in range(2):
                        store(h, j)
                        load(h + 1, j)
                for j in range(2):
                    store(NTILE // 2 - 1, j)
                for j in range(2):
                    sp.wait_ge(ys_out[j], 8 * NTILE + 16)

            @block.gpsimd
            def _(pool):
                gp = nc.gpsimd
                any_f = dict(allow_small_or_imprecise_dtypes=True)
                gp.iota(iota_m[:, :], [[TS, M_MAX]], base=0, channel_multiplier=0, **any_f).then_inc(consts, 1)
                gp.iota(iota_i[:, :], [[1, NTILE]], base=0, channel_multiplier=0, **any_f).then_inc(consts, 1)
                gp.iota(iota_p[:, :], [[P, TT]], base=0, channel_multiplier=1, **any_f).then_inc(consts, 1)
                gp.memset(one8[:, :], 1.0).then_inc(consts, 1)
                gp.memset(zrow[:, :], 0.0).then_inc(consts, 1)
                pool.wait_ge(consts, 5)
                pool.wait_ge(pad_ready, 1)
                for e in range(E):
                    for t in range(TT):
                        gp.indirect_dma_start(
                            out=xs_dram[:, :], in_=zrow[:, :], in_offset=None,
                            out_offset=bass.IndirectOffsetOnAxis(ap=pad[:, t, e:e + 1], axis=0),
                        ).then_inc(padded, 16)
                pool.wait_ge(padded, 16 * TT * E)

            @block.scalar
            def _(act):
                sc = nc.scalar

                def take_xT(i, j):
                    act.wait_ge(xT_mm, i + 1)
                    sc.activation(xT[j][:, :, :], XT16.rearrange("p (k t) -> p k t", k=KD), ACT.Copy
                                  ).then_inc(xT_ready, 1)

                def tile(i, j, is_last):
                    for c in range(CP):
                        act.wait_ge(up_mm, CP * i + c + 1)
                        sc.activation(act_g[:, c, :], G_BANK[c][:, :], ACT.Silu, scale=1.0 / WSCALE
                                      ).then_inc(silu_ready, 1)
                        if c == 1 and not is_last:
                            take_xT(i + 1, 1 - j)
                        act.wait_ge(hid_ready, CP * i + c + 1)
                        act.wait_ge(down_mm, i + 1)
                        sc.activation(h1[:, c, :], hid[:, c, :], ACT.Copy).then_inc(h1_ready, 1)

                take_xT(0, 0)
                with act.Fori(0, NTILE // 2 - 1) as h:
                    for j in range(2):
                        tile(2 * h + j, j, False)
                for j in range(2):
                    tile(NTILE - 2 + j, j, j == 1)

            @block.vector
            def _(dve):
                v = nc.vector
                dve.sem_inc(y_ready, 1)
                ch = Chain(dve, plan, spare)
                dve.wait_ge(consts, 5)
                ch.link(v.tensor_tensor(padf[:, :, :], keep["fill"][:, :].unsqueeze(1).broadcast_to([P, TT, E]),
                                        iota_p[:, :].unsqueeze(2).broadcast_to([P, TT, E]), ALU.add))
                v.tensor_copy(pad[:, :, :], padf[:, :, :]).then_inc(pad_ready, 1)
                ch.link(v.tensor_tensor(count[:, :], keep["fill"][:, :], keep["first"][:, :], ALU.subtract))
                ch.link(v.tensor_tensor(over[:, :, :], count[:, :].unsqueeze(2).broadcast_to([P, E, M_MAX]),
                                        iota_m[:, :].unsqueeze(1).broadcast_to([P, E, M_MAX]), ALU.is_gt))
                ch.link(v.reduce_sum(tiles[:, :], over[:, :, :], AX.X))
                ch.link(v.tensor_tensor_scan(cum[:, :], one8[:, :], tiles[:, :], 0.0, ALU.mult, ALU.add))
                ch.link(v.tensor_tensor(past[:, :, :], iota_i[:, :].unsqueeze(2).broadcast_to([P, NTILE, E]),
                                        cum[:, :].unsqueeze(1).broadcast_to([P, NTILE, E]), ALU.is_ge))
                v.tensor_tensor(pastn[:, :, :], past[:, :, :], tiles[:, :].unsqueeze(1).broadcast_to([P, NTILE, E]),
                                ALU.mult)
                ch.link(v.reduce_sum(own[:, :], past[:, :, :], AX.X))
                ch.link(v.reduce_sum(begun[:, :], pastn[:, :, :], AX.X))
                ch.link(v.tensor_tensor(rowf[:, :], iota_i[:, :], begun[:, :], ALU.subtract))
                ch.link(v.tensor_scalar(rowf[:, :], rowf[:, :], float(TS), None, ALU.mult))
                ch.link(v.scalar_tensor_tensor(rowf[:, :], own[:, :], float(REGION), rowf[:, :], ALU.mult, ALU.add))
                ch.link(v.tensor_scalar(ownc[:, :], own[:, :], float(E - 1), None, ALU.min))
                v.tensor_copy(table[:, 0, :], rowf[:, :])
                v.tensor_scalar(table[:, 1, :], ownc[:, :], float(KD * F), None, ALU.mult)
                v.tensor_scalar(table[:, 2, :], ownc[:, :], float(FC * D), None, ALU.mult).then_inc(table_ready, 1)
                n_slot = NT * TOP
                ch.link(v.tensor_scalar(shift[:, :], tiles[:, 0:E - 1], float(TS), -float(REGION), ALU.mult, ALU.add))
                ch.link(v.tensor_tensor(beyond[:, :, :], keep["slots"][:, :].unsqueeze(2).broadcast_to([P, n_slot, E - 1]),
                                        keep["first"][:, 1:E].unsqueeze(1).broadcast_to([P, n_slot, E - 1]), ALU.is_ge))
                ch.link(v.tensor_tensor(beyond[:, :, :], beyond[:, :, :],
                                        shift[:, :].unsqueeze(1).broadcast_to([P, n_slot, E - 1]), ALU.mult))
                ch.link(v.reduce_sum(moved[:, :], beyond[:, :, :], AX.X))
                v.tensor_tensor(keep["slots"][:, :], keep["slots"][:, :], moved[:, :], ALU.add)

                def tile(h, j):
                    i = 2 * h + j
                    for c in range(CP):
                        dve.wait_ge(silu_ready, CP * i + c + 1)
                        v.scalar_tensor_tensor(hid[:, c, :], U_BANK[c][:, :], HSCALE / WSCALE, act_g[:, c, :],
                                               ALU.mult, ALU.mult).then_inc(hid_ready, 1)
                        dve.wait_ge(h1_ready, CP * i + c + 1)
                        v.tensor_tensor(h2[:, c, :], hid[:, c, :], h1[:, c, :], ALU.subtract).then_inc(h2_ready, 1)
                    dve.wait_ge(down_mm, i + 2)
                    dve.wait_ge(ys_out[j], 16 * h + 16)
                    for t in range(TT):
                        last = v.tensor_scalar(y_sb[j][:, t, :], Y_BANK[t][:, 0:D], 1.0 / (WSCALE * HSCALE), None,
                                               ALU.mult)
                    last.then_inc(y_ready, 1)

                with dve.Fori(0, NTILE // 2) as h:
                    for j in range(2):
                        tile(h, j)

            @block.tensor
            def _(pe):
                mm = nc.tensor.matmul

                def transpose_rows(h, j):
                    pe.wait_ge(xin_in[j], 16 * h + 16)
                    for k in range(KD):
                        for t in range(TT):
                            last = nc.tensor.transpose(XT16[:, TS * k + P * t:TS * k + P * (t + 1)],
                                                       xin[j][:, t, P * k:P * (k + 1)], ident[:, :])
                    last.then_inc(xT_mm, 1)

                def up(i, j, c, col):
                    for parts, dst in ((wg_part, G_BANK[c]), (wu_part, U_BANK[c])):
                        for half in range(2):
                            at = (2 * c + half) * P
                            for s in range(2 * KD):
                                k, part = s // 2, s % 2
                                last = mm(dst[:, TS * half:TS * (half + 1)],
                                          parts[part][:, bass.ds(col + (k * F + at), P)], xT[j][:, k, :],
                                          start=(s == 0), stop=(s == 2 * KD - 1))
                    last.then_inc(up_mm, 1)

                def down(i, col):
                    for c in range(FC):
                        rows = P if c < FC - 1 else FR
                        if c % 2 == 0:
                            pe.wait_ge(h2_ready, CP * i + c // 2 + 1)
                        for t in range(TT):
                            at = (c % 2) * TS + t * P
                            for s, (h, w) in enumerate(((h1, 0), (h1, 1), (h2, 0))):
                                last = mm(Y_BANK[t][:, 0:D], h[0:rows, c // 2, at:at + P],
                                          wd_part[w][0:rows, bass.ds(col + c * D, D)],
                                          start=(c == 0 and s == 0), stop=(c == FC - 1 and s == 2))
                    last.then_inc(down_mm, 1)

                def tile(h, j, is_last):
                    i = 2 * h + j
                    col_gu = pe.value_load(table[0:1, 1, bass.ds(i, 1)], min_val=0, max_val=(E - 1) * KD * F)
                    col_d = pe.value_load(table[0:1, 2, bass.ds(i, 1)], min_val=0, max_val=(E - 1) * FC * D)
                    pe.wait_ge(xT_ready, i + 1)
                    up(i, j, 0, col_gu)
                    if not is_last:
                        pe.wait_ge(y_ready, i + 1)
                        transpose_rows(h + j, 1 - j)
                    up(i, j, 1, col_gu)
                    up(i, j, 2, col_gu)
                    if not is_last:
                        pe.wait_ge(xT_ready, i + 2)
                    down(i, col_d)

                pe.sem_inc(down_mm, 1)
                pe.wait_ge(table_ready, 1)
                transpose_rows(0, 0)
                with pe.Fori(0, NTILE // 2 - 1) as h:
                    for j in range(2):
                        tile(h, j, False)
                for j in range(2):
                    tile(NTILE // 2 - 1, j, j == 1)


def combine(nc, sb, sem, spare, keep, x1_dram, ys_dram, out):
    TT = 2
    N = NT // TT
    W = TT * TOP
    x1_v = x1_dram.rearrange("(i t p) d -> i p t d", t=TT, p=P)
    out_v = out.rearrange("b (h t p) d -> (b h) p t d", t=TT, p=P)
    stack = ExitStack()
    with stack:
        idx = [sb(stack, f"idx{j}", [P, W], U32) for j in range(2)]
        yg = [sb(stack, f"yg{j}", [P, W, D], F32) for j in range(2)]
        x1 = [sb(stack, f"x1c{j}", [P, TT, D], F16) for j in range(2)]
        wcur = sb(stack, "wcur", [P, W], F32)
        part = sb(stack, "part", [P, TT, D], F32)
        total = sb(stack, "total", [P, TT, D], F32)
        res = [sb(stack, f"res{j}", [P, TT, D], F32) for j in range(2)]
        nrm = sb(stack, "nrm", [P, TT, D], F32)
        stats = sb(stack, "stats3", [P, TT, 6], F32)
        mv = sb(stack, "mv3", [P, TT, 2], F32)
        std = sb(stack, "std3", [P, TT], F32)
        rstd = sb(stack, "rstd3", [P, TT], F32)
        eps = sb(stack, "eps", [P, 1], F32)

        idx_ready = sem("idx_ready")
        gathered = [sem(f"gathered{j}") for j in range(2)]
        x1_in = [sem(f"x1_in{j}") for j in range(2)]
        sum_ready = sem("sum_ready")
        eps_ready = sem("eps_ready")
        cchain = sem("cchain")
        var_ready = sem("var_ready3")
        std_ready = sem("std_ready3")
        fin = sem("fin")
        stored = [sem(f"stored{j}") for j in range(2)]

        with nc.Block() as block:
            @block.sync
            def _(sp):
                def load(h, j):
                    sp.dma_start(x1[j][:, :, :], x1_v[2 * h + j, :, :, :]).then_inc(x1_in[j], 16)

                def store(h, j):
                    hold(sp, fin, 2 * h + j + 1, spare)
                    sp.dma_start(out_v[2 * h + j, :, :, :], res[j][:, :, :]).then_inc(stored[j], 16)

                for j in range(2):
                    sp.sem_inc(stored[j], 16)
                for j in range(2):
                    load(0, j)
                with sp.Fori(0, N // 2 - 1) as h:
                    for j in range(2):
                        store(h, j)
                        load(h + 1, j)
                for j in range(2):
                    store(N // 2 - 1, j)
                for j in range(2):
                    sp.wait_ge(stored[j], 8 * N + 16)

            @block.gpsimd
            def _(pool):
                gp = nc.gpsimd
                gp.memset(eps[:, :], LN_EPS).then_inc(eps_ready, 1)
                with pool.Fori(0, N // 2) as h:
                    for j in range(2):
                        n = 2 * h + j
                        hold(pool, sum_ready, n + 1, spare)
                        gp.tensor_copy(idx[j][:, :], keep["slots"][:, bass.ds(n * W, W)]).then_inc(idx_ready, 1)
                        hold(pool, idx_ready, n + 1, spare)
                        for w in range(W):
                            gp.indirect_dma_start(
                                out=yg[j][:, w, :], out_offset=None, in_=ys_dram[:, :],
                                in_offset=bass.IndirectOffsetOnAxis(ap=idx[j][:, w:w + 1], axis=0),
                            ).then_inc(gathered[j], 16)

            @block.scalar
            def _(act):
                act.wait_ge(eps_ready, 1)
                with act.Fori(0, N) as i:
                    act.wait_ge(var_ready, i + 1)
                    nc.scalar.activation(std[:, :], mv[:, :, 1], ACT.Sqrt, bias=eps[:, 0:1]).then_inc(std_ready, 1)

            @block.vector
            def _(dve):
                v = nc.vector
                dve.sem_inc(sum_ready, 2)
                ch = Chain(dve, cchain, spare)
                with dve.Fori(0, N // 2) as h:
                    for j in range(2):
                        n = 2 * h + j
                        ch.rebase(6 * n)
                        ch.link(v.tensor_copy(wcur[:, :], keep["weights"][:, bass.ds(n * W, W)]))
                        dve.wait_ge(gathered[j], 16 * W * (h + 1))
                        for t in range(TT):
                            last = v.tensor_scalar(part[:, t, :], yg[j][:, TOP * t, :], wcur[:, TOP * t:TOP * t + 1],
                                                   None, ALU.mult)
                        ch.link(last)
                        for t in range(TT):
                            last = v.scalar_tensor_tensor(total[:, t, :], yg[j][:, TOP * t + 1, :],
                                                          wcur[:, TOP * t + 1:TOP * t + 2], part[:, t, :],
                                                          ALU.mult, ALU.add)
                        last.then_inc(sum_ready, 1)
                        dve.wait_ge(sum_ready, n + 3)
                        for t in range(TT):
                            last = v.bn_stats(stats[:, t, :], total[:, t, :])
                        ch.link(last)
                        for t in range(TT):
                            last = v.bn_aggr(mv[:, t, :], stats[:, t, :])
                        last.then_inc(var_ready, 1)
                        dve.wait_ge(var_ready, n + 1)
                        dve.wait_ge(std_ready, n + 1)
                        ch.link(v.reciprocal(rstd[:, :], std[:, :]))
                        for t in range(TT):
                            last = v.tensor_scalar(nrm[:, t, :], total[:, t, :], mv[:, t, 0:1], rstd[:, t:t + 1],
                                                   ALU.subtract, ALU.mult)
                        ch.link(last)
                        dve.wait_ge(x1_in[j], 16 * h + 16)
                        dve.wait_ge(stored[j], 16 * h + 16)
                        ch.link(v.tensor_tensor(res[j][:, :, :], nrm[:, :, :], x1[j][:, :, :], ALU.add))
                        dve.sem_inc(fin, 1)


_OUT = ("out_0", (B, T, D), "float32")


def kernel(**inputs):
    import numpy as np
    import concourse.bacc as bacc
    from concourse.bass_utils import run_bass_kernel_spmd

    a = {k: np.ascontiguousarray(v) for k, v in inputs.items()}

    def by_head(w):
        w = w.T.reshape(KD, P, G, J, HD)
        r = np.zeros((KD, P, G, J, 32), w.dtype)
        r[..., :HD] = w
        return np.ascontiguousarray(r.reshape(KD, P, G, P).transpose(1, 0, 2, 3))

    def bias_by_head(b, fill):
        r = np.zeros((G, J, 32), b.dtype)
        r[..., :HD] = b.reshape(G, J, HD)
        r[..., HD] = fill
        return np.ascontiguousarray(r.reshape(G, P).T)

    def by_slice(w):
        return np.ascontiguousarray(w.T.reshape(KD, P, D).transpose(1, 0, 2))

    arrays = {
        "x": a["L0_attn_hidden_states"],
        "wq": by_head(a["L0_attn_wq"]), "wk": by_head(a["L0_attn_wk"]),
        "wv": by_slice(a["L0_attn_wv"]), "wo": by_slice(a["L0_attn_wo"]),
        "bq": bias_by_head(a["L0_attn_bq"], 0), "bk": bias_by_head(a["L0_attn_bk"], 1),
        "bv": a["L0_attn_bv"], "bo": a["L0_attn_bo"],
        "ws": a["L0_ffn_Ws"], "bs": a["L0_ffn_bs"],
        "wg": a["L0_ffn_Wg"], "wu": a["L0_ffn_Wu"], "wd": a["L0_ffn_Wd"],
    }
    nc = bacc.Bacc("TRN2", target_bir_lowering=False, num_devices=1)
    args = [nc.dram_tensor(k, v.shape, mybir.dt.from_np(v.dtype), kind="ExternalInput").ap()
            for k, v in arrays.items()]
    out = nc.dram_tensor(_OUT[0], _OUT[1], mybir.dt.from_np(np.dtype(_OUT[2])), kind="ExternalOutput").ap()
    build(nc, *args, out)
    r = run_bass_kernel_spmd(nc, [arrays], core_ids=[0])
    return r.results[0][_OUT[0]]
```

```python
from contextlib import ExitStack

import concourse.bass as bass
from concourse import mybir

ALU = mybir.AluOpType
ACT = mybir.ActivationFunctionType
AX = mybir.AxisListType
F32 = mybir.dt.float32
F16 = mybir.dt.float16
BF16 = mybir.dt.bfloat16
U32 = mybir.dt.uint32

P = 128
B, T, D = 8, 512, 256
H, HD = 16, 16
KD = D // P
QT = T // P
G, J = 4, 4
NT = B * QT
E, F = 8, 688
FC = -(-F // P)
FR = F - (FC - 1) * P
TILES_OF = ((0,), (1, 3), (2,))
FILLS = [(j, tiles) for tiles in TILES_OF for j in range(J)]
S_FILLS = [(j, tiles) for tiles in ((1,), (2, 0), (3,)) for j in range(J)]
CUTS = len(TILES_OF)
NF = len(FILLS)


def width(key_tiles):
    return sum(T - P * kt for kt in key_tiles)


P_COL = {(kt, j): sum(width(tiles) for _, tiles in FILLS[:i]) + width(tiles[:m])
         for i, (j, tiles) in enumerate(FILLS) for m, kt in enumerate(tiles)}
P_COLS = sum(width(tiles) for _, tiles in FILLS)
TOP = 2
TS = 2 * P
REGION = B * T + TS
TILES = (TOP * B * T + E * (TS - 1)) // TS
SPARE_TILES = TILES - TOP * B * T // TS
ROWS = E * REGION + (SPARE_TILES + 1) * TS
GU_UP = (FC - 1) * P
GU_LAST = 2 * GU_UP
GU = GU_LAST + P // 2 + FR
PV_LAG = 7
LN_EPS = 1e-5
LN_EPS16 = 2.0 ** -24 * 168
WSCALE = 256.0
HSCALE = 64.0
MASK = -10000.0
INV_SCALE = float(HD) ** 0.5


def hold(eng, sem, value, spare):
    eng.wait_ge(sem, value)
    eng.sem_inc(spare, 1)


class Chain:

    def __init__(self, eng, sem, spare):
        self.eng, self.sem, self.spare, self.base, self.n = eng, sem, spare, 0, 0

    def link(self, ins):
        ins.then_inc(self.sem, 1)
        self.n += 1
        hold(self.eng, self.sem, self.base + self.n, self.spare)

    def mark(self, ins):
        ins.then_inc(self.sem, 1)
        self.n += 1

    def settle(self):
        hold(self.eng, self.sem, self.base + self.n, self.spare)

    def rebase(self, base):
        self.base, self.n = base, 0


def build(nc, x, wq, wk, wv, wo, bq, bk, bv, bo, ws, bs, wg, wu, wd, out):
    x1_dram = nc.dram_tensor("x1_rows", [NT * P, D], F16).ap()
    xs_dram = nc.dram_tensor("dispatch_rows", [ROWS, D], F16).ap()
    ys_dram = nc.dram_tensor("expert_rows", [TILES * TS, D], F32).ap()
    outer = ExitStack()
    with outer:
        def sb(stack, name, shape, dt):
            return stack.enter_context(nc.sbuf_tensor(name, shape, dt))

        def sem(name):
            return outer.enter_context(nc.semaphore(name))

        spare = sem("spare")
        bank = [outer.enter_context(nc.psum_tensor(f"bank{i}", [P, 512], F32)) for i in range(8)]
        keep = {
            "ident": sb(outer, "ident", [P, P], F16),
            "gu": [sb(outer, f"gu_part{i}", [P, E * KD * GU], F16) for i in range(2)],
            "wd": [sb(outer, f"wd_part{i}", [P, E * FC * D], F16) for i in range(2)],
            "slots": sb(outer, "slots", [P, NT * TOP], U32),
            "weights": sb(outer, "weights", [P, NT * TOP], F32),
            "slot": sb(outer, "slot", [P, QT, TOP], U32),
            "xn2": sb(outer, "xn2", [P, QT, D], F16),
            "scattered": sem("scattered"),
            "fill": sb(outer, "fill", [P, E], F32),
            "first": sb(outer, "first", [P, E], F32),
        }
        attention(nc, sb, sem, spare, bank, keep, x, wq, wk, wv, wo, bq, bk, bv, bo, ws, bs, wg, wu, wd,
                  x1_dram, xs_dram)
        experts(nc, sb, sem, spare, bank, keep, xs_dram, ys_dram)
        combine(nc, sb, sem, spare, keep, x1_dram, ys_dram, out)
    return nc


def scatter_rows(gp, keep, xs_dram, part, parts):
    n = TOP * QT
    for i in range(part * n // parts, (part + 1) * n // parts):
        t, r = i // TOP, i % TOP
        gp.indirect_dma_start(
            out=xs_dram[:, :], in_=keep["xn2"][:, t, :], in_offset=None,
            out_offset=bass.IndirectOffsetOnAxis(ap=keep["slot"][:, t, r:r + 1], axis=0),
        ).then_inc(keep["scattered"], 16)


def attention(nc, sb, sem, spare, bank, keep, x, wq, wk, wv, wo, bq, bk, bv, bo, ws, bs, wg, wu, wd,
              x1_dram, xs_dram):
    x_v = x.rearrange("b (t p) d -> b p t d", p=P)
    x1_v = x1_dram.rearrange("(b t p) d -> b p t d", t=QT, p=P)
    ident = keep["ident"]
    stack = ExitStack()
    with stack:
        wq_sb = sb(stack, "wq_sb", [P, KD, G, P], F16)
        wk_sb = sb(stack, "wk_sb", [P, KD, G, P], F16)
        wv_sb = sb(stack, "wv_sb", [P, KD, D], F16)
        wo_sb = sb(stack, "wo_sb", [P, KD, D], F16)
        bq16 = sb(stack, "bq16", [P, G], F16)
        bk16 = sb(stack, "bk16", [P, G], F16)
        bq_sb = sb(stack, "bq_sb", [P, G], F32)
        bk_sb = sb(stack, "bk_sb", [P, G], F32)
        bv_sb = sb(stack, "bv_sb", [P, D], F16)
        bo_sb = sb(stack, "bo_sb", [P, D], F16)
        ws_f = sb(stack, "ws_f", [P, KD, E], F32)
        ws_r = sb(stack, "ws_r", [P, KD, E], F32)
        ws_part = sb(stack, "ws_part", [P, KD, 3, E], BF16)
        bs_sb = sb(stack, "bs_sb", [P, E], F32)
        mask = sb(stack, "mask", [P, T], F16)
        before = sb(stack, "before", [P, P], F16)
        ones = sb(stack, "ones", [P, P], F16)
        power = sb(stack, "power", [P, 2, QT], F32)
        wscale = sb(stack, "wscale", [P, 1], F32)
        iota8 = sb(stack, "iota8", [P, E], F32)
        x_sb = sb(stack, "x_sb", [P, QT, D], F16)
        xr_sb = sb(stack, "xr_sb", [P, QT, D], F16)
        xn = sb(stack, "xn", [P, QT, D], F16)
        xnT = sb(stack, "xnT", [P, KD, T], F16)
        qT = sb(stack, "qT", [P, G, T], F16)
        kT = sb(stack, "kT", [P, G, T], F16)
        va = sb(stack, "va", [P, G, QT, J, HD + 1], F16)
        v16 = sb(stack, "v16", [P, QT, J * HD], F16)
        nmax = sb(stack, "nmax", [P, 2, QT, P], F16)
        pT = sb(stack, "pT", [P, P_COLS], F16)
        unused = sb(stack, "unused", [P, 2, T], F16)
        rden = sb(stack, "rden", [P, QT, J], F32)
        att = sb(stack, "att", [P, QT, D], F16)
        attT = sb(stack, "attT", [P, KD, T], F16)
        y = sb(stack, "y", [P, QT, D], F16)
        x1 = sb(stack, "x1", [P, QT, D], F16)
        stats = sb(stack, "stats", [P, QT, 6], F32)
        mv = sb(stack, "mv", [P, QT, 2], F16)
        veps = sb(stack, "veps", [P, QT], F16)
        std = sb(stack, "std", [P, QT], F16)
        cen = sb(stack, "cen", [P, QT, D], F16)
        rstd = sb(stack, "rstd", [P, QT], F32)
        st_gu = sb(stack, "st_gu", [P, KD * F], F32)
        st_d = sb(stack, "st_d", [P, FC * D], F32)
        logit = sb(stack, "logit", [P, QT, E], F32)
        top = sb(stack, "top", [P, QT, E], F32)
        topi = sb(stack, "topi", [P, QT, E], U32)
        topf = sb(stack, "topf", [P, QT, TOP], F32)
        pick = [sb(stack, f"pick{r}", [P, QT, E], F32) for r in range(TOP)]
        both = sb(stack, "both", [P, QT, E], F16)
        dif = sb(stack, "dif", [P, QT], F32)
        e1 = sb(stack, "e1", [P, QT], F32)
        den = sb(stack, "den", [P, QT], F32)
        wts = sb(stack, "wts", [P, QT, TOP], F32)
        row = sb(stack, "row", [P, QT, E], F32)
        prow = [sb(stack, f"prow{r}", [P, QT, E], F32) for r in range(TOP)]
        slotf = sb(stack, "slotf", [P, QT, TOP], F32)
        slot, xn2 = keep["slot"], keep["xn2"]

        S_BANK, ST_BANK = (bank[0], bank[1]), (bank[2], bank[3])
        PV_BANK, Q_BANK, K_BANK, M_BANK = bank[4], bank[5], bank[6], bank[7]
        M16 = M_BANK[:, :].bitcast(F16)
        OUT = PV_BANK[:, :].rearrange("p (t j c) -> p t j c", t=QT, j=J)
        LOGITS = K_BANK[:, 0:QT * E].rearrange("p (t e) -> p t e", t=QT)
        RANKS = K_BANK[:, 64:64 + QT * E].rearrange("p (t e) -> p t e", t=QT)
        TOTAL = K_BANK[:, 128:128 + E]

        w_in = sem("w_in")
        x_in = sem("x_in")
        xr_in = sem("xr_in")
        pool_const = sem("pool_const")
        const_ready = sem("const_ready")
        zero_ready = sem("zero_ready")
        bias_ready = sem("bias_ready")
        var_ready = sem("var_ready")
        veps_ready = sem("veps_ready")
        std_ready = sem("std_ready")
        cen_ready = sem("cen_ready")
        rstd_ready = sem("rstd_ready")
        xn_ready = sem("xn_ready")
        xnT_mm = sem("xnT_mm")
        xnT_ready = sem("xnT_ready")
        q_mm = sem("q_mm")
        q_out = sem("q_out")
        k_mm = sem("k_mm")
        k_out = sem("k_out")
        v_mm = sem("v_mm")
        v_out = sem("v_out")
        s_mm = sem("s_mm")
        s_max = sem("s_max")
        st_mm = sem("st_mm")
        p_ready = sem("p_ready")
        pv_mm = sem("pv_mm")
        att_out = sem("att_out")
        attT_mm = sem("attT_mm")
        attT_out = sem("attT_out")
        y_mm = sem("y_mm")
        y_out = sem("y_out")
        x1_ready = sem("x1_ready")
        xn2_ready = sem("xn2_ready")
        x1_out = sem("x1_out")
        xn2T_mm = sem("xn2T_mm")
        xn2T_out = sem("xn2T_out")
        logit_mm = sem("logit_mm")
        logit_out = sem("logit_out")
        both_ready = sem("both_ready")
        dif_ready = sem("dif_ready")
        e1_ready = sem("e1_ready")
        rank_mm = sem("rank_mm")
        rank_out = sem("rank_out")
        slot_ready = sem("slot_ready")
        xn2_free = sem("xn2_free")
        cut_ready = sem("cut_ready")
        zeros_out = sem("zeros_out")
        dve_chain = sem("dve_chain")
        ws_chain = sem("ws_chain")
        v16_ready = sem("v16_ready")
        y16_ready = sem("y16_ready")
        g_in = sem("g_in")
        d_in = sem("d_in")
        u_in = sem("u_in")
        hi_ready = sem("hi_ready")
        mul_ready = sem("mul_ready")
        lo_ready = sem("lo_ready")

        AT_TAKE_ATT, AT_MAXIMA, AT_PROJECT_OUT, AT_NEXT_T, AT_XN2_T, AT_RANKS = 5, 6, 4, 10, 8, 8
        AT_NEXT_NORM = ((0, 1), (0, 2), (0, 3), (0, 7))
        AT_FINISH = ((1, 4), (1, 6), (1, 7), (1, 8), (1, 9), (1, 10), (2, 0), (2, 1), (2, 2), (2, 3), (2, 4), (2, 7))
        AT_ROUTE = ((3, 1), (3, 2), (3, 3), (3, 4), (3, 6), (3, 7))
        AT_SLOTS = ((3, 8), (3, 9), (3, 10), (3, 11))
        AT_SCATTER = ((1, 0), (1, 1))
        STEPS = 16

        LAST = G * (B - 1)

        def places(b, which, part):
            if which == 1:
                return ((keep["wd"][part][:, bass.ds(b * (FC * D), FC * D)], st_d[:, :]),)
            dst = keep["gu"][part][:, bass.ds(b * (KD * GU), KD * GU)].rearrange("p (k c) -> p k c", k=KD)
            src = st_gu[:, :].rearrange("p (k f) -> p k f", k=KD)
            at, last_at = (0, GU_LAST) if which == 0 else (GU_UP, GU_LAST + P // 2)
            return ((dst[:, :, at:at + GU_UP], src[:, :, 0:GU_UP]), (dst[:, :, last_at:last_at + FR], src[:, :, GU_UP:F]))

        def q_uses(grp, in_last):
            return 5 + 2 * grp if not in_last else 5 + 2 * LAST + (grp - LAST)

        with nc.Block() as block:
            @block.sync
            def _(sp):
                def load_x(dst, b, signal):
                    sp.dma_start(dst[:, :, :], x_v[b, :, :, :]).then_inc(signal, 16)

                def load_gu(src, e, signal):
                    sp.dma_start(st_gu[:, :].rearrange("p (k f) -> p k f", k=KD),
                                 src[e, :, :].rearrange("(k p) f -> p k f", p=P)).then_inc(signal, 16)

                def load_d(e):
                    sp.dma_start(st_d[:, 0:(FC - 1) * D].rearrange("p (c d) -> p c d", c=FC - 1),
                                 wd[e, 0:(FC - 1) * P, :].rearrange("(c p) d -> p c d", p=P)).then_inc(d_in, 16)
                    sp.dma_start(st_d[0:FR, (FC - 1) * D:FC * D], wd[e, (FC - 1) * P:F, :]).then_inc(d_in, 16)

                def batch(b, first, in_last, more_x):
                    hold(sp, lo_ready, 3 * b + 1, spare)
                    load_gu(wu, b, u_in)
                    if not first:
                        hold(sp, x1_ready, b, spare)
                        sp.dma_start(x1_v[b - 1, :, :, :], x1[:, :, :]).then_inc(x1_out, 16)
                    load_x(xr_sb, b, xr_in)
                    if not in_last:
                        hold(sp, xn_ready, b + 2, spare)
                        if more_x:
                            load_x(x_sb, b + 2, x_in)
                        hold(sp, lo_ready, 3 * b + 2, spare)
                        load_d(b + 1)
                        hold(sp, lo_ready, 3 * b + 3, spare)
                        load_gu(wg, b + 1, g_in)

                sp.sem_inc(x1_out, 16)
                load_x(x_sb, 0, x_in)
                for dst, src in ((wq_sb[:, :, :, :], wq), (wk_sb[:, :, :, :], wk), (wv_sb[:, :, :], wv),
                                 (wo_sb[:, :, :], wo), (bq16[:, :], bq), (bk16[:, :], bk),
                                 (bv_sb[:, :], bv.partition_broadcast(P)),
                                 (bo_sb[:, :], bo.partition_broadcast(P)),
                                 (ws_f[:, :, :], ws.rearrange("(k p) e -> p k e", p=P)),
                                 (bs_sb[:, :], bs.partition_broadcast(P))):
                    sp.dma_start(dst, src).then_inc(w_in, 16)
                load_gu(wg, 0, g_in)
                sp.wait_ge(zero_ready, 1)
                load_d(0)
                sp.wait_ge(xn_ready, 1)
                load_x(x_sb, 1, x_in)
                sp.wait_ge(zero_ready, 2)
                sp.dma_start(xs_dram[E * REGION:, :].rearrange("(p r) d -> p (r d)", p=P),
                             pT[:, 0:(SPARE_TILES + 1) * TS * D // P]).then_inc(zeros_out, 16)
                batch(0, True, False, True)
                with sp.Fori(1, B - 2) as b:
                    batch(b, False, False, True)
                batch(B - 2, False, False, False)
                batch(B - 1, False, True, False)
                sp.wait_ge(x1_ready, B)
                sp.dma_start(x1_v[B - 1, :, :, :], x1[:, :, :]).then_inc(x1_out, 16)
                sp.wait_ge(x1_out, 16 * B + 16)
                sp.wait_ge(zeros_out, 16)

            @block.gpsimd
            def _(pool):
                gp = nc.gpsimd
                ch = Chain(pool, pool_const, spare)
                ch.link(gp.memset(power[:, 0, :], 0.5))
                ch.link(gp.memset(power[:, 1, :], -1.0))
                ch.link(gp.memset(wscale[:, :], WSCALE))
                ch.link(gp.memset(ones[:, :], 1.0))
                ch.link(gp.iota(iota8[:, :], [[1, E]], base=0, channel_multiplier=0,
                                allow_small_or_imprecise_dtypes=True))
                ch.link(gp.iota(keep["fill"][:, :], [[REGION, E]], base=0, channel_multiplier=0,
                                allow_small_or_imprecise_dtypes=True))
                ch.link(gp.iota(keep["first"][:, :], [[REGION, E]], base=0, channel_multiplier=0,
                                allow_small_or_imprecise_dtypes=True))
                for part in keep["gu"]:
                    ch.link(gp.memset(part[:, :].rearrange("p (r c) -> p r c", c=GU)[:, :, GU_LAST + FR:GU_LAST + P // 2],
                                      0.0))
                ch.link(gp.memset(ident[:, :], 0.0))
                ch.link(gp.affine_select(out=ident[:, :], in_=ident[:, :], compare_op=ALU.not_equal, fill=1.0,
                                         base=0, pattern=[[-1, P]], channel_multiplier=1))
                ch.link(gp.memset(before[:, :], 0.0))
                ch.link(gp.affine_select(out=before[:, :], in_=before[:, :], compare_op=ALU.is_ge, fill=1.0,
                                         base=0, pattern=[[-1, P]], channel_multiplier=1))
                ch.link(gp.memset(mask[:, :], 0.0))
                diagonal = mask[:, T - P:T]
                ch.link(gp.affine_select(out=diagonal, in_=diagonal, compare_op=ALU.is_ge,
                                         fill=MASK * INV_SCALE, base=0, pattern=[[-1, P]], channel_multiplier=1))
                for g in range(G):
                    last = gp.memset(va[:, g, :, :, HD:HD + 1], 1.0)
                    if g < G - 1:
                        ch.link(last)
                last.then_inc(const_ready, 1)

                def rsqrt(n):
                    hold(pool, var_ready, n + 1, spare)
                    gp.tensor_scalar(veps[:, :], mv[:, :, 1], LN_EPS16, None, ALU.add).then_inc(veps_ready, 1)
                    pool.wait_ge(veps_ready, n + 1)
                    gp.tensor_tensor(std[:, :], veps[:, :], power[:, 0, :], ALU.pow).then_inc(std_ready, 1)
                    pool.wait_ge(std_ready, n + 1)
                    gp.tensor_tensor(rstd[:, :], std[:, :], power[:, 1, :], ALU.pow).then_inc(rstd_ready, 1)

                def scale_stage(b, which):
                    stage, n, count = (st_gu, st_d, st_gu)[which], (KD * F, FC * D, KD * F)[which], 3 * b + which
                    pool.wait_ge(hi_ready, count + 1)
                    gp.tensor_tensor(stage[:, :], stage[:, :], wscale[:, 0:1].broadcast_to([P, n]),
                                     ALU.mult).then_inc(mul_ready, 1)

                def rest(b, which):
                    hold(pool, mul_ready, 3 * b + which + 1, spare)
                    for (dst, src), (high, _) in zip(places(b, which, 1), places(b, which, 0)):
                        last = gp.tensor_tensor(dst, src, high, ALU.subtract)
                    last.then_inc(lo_ready, 1)

                def cut(grp, c):
                    hold(pool, p_ready, NF * grp + J * (c + 1) + 2, spare)
                    tiles = TILES_OF[c]
                    at = P_COL[tiles[0], 0]
                    banks = pT[:, at:at + J * width(tiles)].rearrange("p (j n) -> p j n", j=J)
                    for kt in tiles:
                        at = P_COL[kt, 0] - P_COL[tiles[0], 0]
                        diagonal = banks[:, :, at:at + P]
                        last = gp.affine_select(out=diagonal, in_=diagonal, compare_op=ALU.is_ge, fill=0.0, base=0,
                                                pattern=[[0, J], [1, P]], channel_multiplier=-1)
                    last.then_inc(cut_ready, 1)

                def batch(b, first, in_last, scattering):
                    for g in range(G):
                        for c in range(CUTS):
                            cut(G * b + g, c)
                            at = (g, c)
                            if at == (0, 0) and not in_last:
                                rsqrt(1 if first else 3 * b - 1)
                            if at == (0, 1):
                                scale_stage(b, 0)
                            if at == (0, 2):
                                rest(b, 0)
                            if at == (1, 0) and scattering:
                                hold(pool, slot_ready, b - 1, spare)
                            if at in AT_SCATTER and scattering:
                                scatter_rows(gp, keep, xs_dram, AT_SCATTER.index(at), len(AT_SCATTER))
                            if at == (1, 2) and not first:
                                rsqrt(3 * b - (1 if in_last else 0))
                            if at == (2, 0):
                                if scattering:
                                    pool.wait_ge(keep["scattered"], 16 * TOP * QT * (b - 1))
                                    pool.sem_inc(xn2_free, 1)
                                scale_stage(b, 1)
                            if at == (2, 1) and not first:
                                rsqrt(3 * b + 1 - (1 if in_last else 0))
                            if at == (2, 2):
                                rest(b, 1)
                            if at == (3, 0):
                                scale_stage(b, 2)
                            if at == (3, 1):
                                rest(b, 2)

                pool.sem_inc(xn2_free, 1)
                rsqrt(0)
                batch(0, True, False, False)
                batch(1, False, False, False)
                with pool.Fori(2, B - 1) as b:
                    batch(b, False, False, True)
                batch(B - 1, False, True, True)
                hold(pool, slot_ready, B - 1, spare)
                scatter_rows(gp, keep, xs_dram, 0, 1)
                rsqrt(3 * B - 2)
                pool.wait_ge(keep["scattered"], 16 * TOP * QT * (B - 1))
                pool.sem_inc(xn2_free, 1)
                rsqrt(3 * B - 1)

            @block.scalar
            def _(act):
                sc = nc.scalar
                act.wait_ge(w_in, 16 * 10)
                sc.activation(bq_sb[:, :], bq16[:, :], ACT.Copy).then_inc(bias_ready, 1)
                sc.activation(bk_sb[:, :], bk16[:, :], ACT.Copy).then_inc(bias_ready, 1)
                act.wait_ge(bias_ready, 2)
                m16 = M16.rearrange("p (k t) -> p k t", k=KD)

                def take_xnT(b):
                    act.wait_ge(xnT_mm, b + 1)
                    sc.activation(xnT[:, :, :], m16, ACT.Copy).then_inc(xnT_ready, 1)

                def take_q(use, g):
                    act.wait_ge(q_mm, use + 1)
                    sc.activation(qT[:, g, :], Q_BANK[:, :], ACT.Identity, bias=bq_sb[:, g:g + 1]).then_inc(q_out, 1)

                def take_k(grp, g):
                    act.wait_ge(k_mm, grp + 1)
                    sc.activation(kT[:, g, :], K_BANK[:, :], ACT.Identity, bias=bk_sb[:, g:g + 1]).then_inc(k_out, 1)

                def take_q_max(use, g):
                    act.wait_ge(q_mm, use + 1)
                    sc.activation(qT[:, g, :], Q_BANK[:, :], ACT.Copy).then_inc(q_out, 1)

                def part(b, which):
                    signal, amount = ((g_in, 16), (d_in, 32), (u_in, 16))[which]
                    act.wait_ge(signal, amount * b + amount)
                    for dst, src in places(b, which, 0):
                        last = sc.activation(dst, src, ACT.Copy, scale=WSCALE)
                    last.then_inc(hi_ready, 1)

                def take_attT(b):
                    act.wait_ge(attT_mm, b + 1)
                    sc.activation(attT[:, :, :], m16, ACT.Copy).then_inc(attT_out, 1)

                def take_xn2T(b):
                    act.wait_ge(xn2T_mm, b + 1)
                    sc.activation(attT[:, :, :], m16, ACT.Copy).then_inc(xn2T_out, 1)

                def weight(b):
                    act.wait_ge(dif_ready, b + 1)
                    sc.activation(e1[:, :], dif[:, :], ACT.Exp).then_inc(e1_ready, 1)

                def batch(b, first, in_last):
                    for g in range(G):
                        grp = G * b + g
                        for i, (j, tiles) in enumerate(FILLS):
                            lo, hi = P_COL[tiles[0], j], P_COL[tiles[0], j] + width(tiles)
                            act.wait_ge(st_mm, NF * grp + i + 1)
                            act.wait_ge(pv_mm, NF * grp + i + 1)
                            sc.activation(pT[:, lo:hi], ST_BANK[i % 2][:, 0:hi - lo], ACT.Exp,
                                          scale=1.0 / INV_SCALE).then_inc(p_ready, 1)
                            if i == AT_MAXIMA + 1 and not (in_last and g == G - 1):
                                take_q_max(q_uses(grp, in_last), (g + 1) % G)
                            if i == 2 and g == 1 and not first:
                                take_attT(b - 1)
                            if i == AT_XN2_T + 1 and g == 2 and not first:
                                take_xn2T(b - 1)
                            if i == AT_NEXT_T + 1 and g == 0 and not in_last:
                                take_xnT(b + 1)
                            if i == 6 and g == 3 and not first:
                                weight(b - 1)
                            if i == 4 and g < 3:
                                part(b, g)
                        if not in_last:
                            take_q(q_uses(grp, False) + 1, g)
                            take_k(grp + G, g)

                take_xnT(0)
                act.wait_ge(zeros_out, 16)
                for g in range(G - 1):
                    take_q(g, g)
                    take_k(g, g)
                take_q_max(3, 0)
                take_q(4, G - 1)
                take_k(G - 1, G - 1)
                batch(0, True, False)
                with act.Fori(1, B - 1) as b:
                    batch(b, False, False)
                batch(B - 1, False, True)
                take_attT(B - 1)
                take_xn2T(B - 1)
                weight(B - 1)

            @block.vector
            def _(dve):
                v = nc.vector
                ch = Chain(dve, dve_chain, spare)
                wch = Chain(dve, ws_chain, spare)
                v.memset(st_d[:, (FC - 1) * D:FC * D], 0.0).then_inc(zero_ready, 1)
                v.memset(pT[:, :], 0.0).then_inc(zero_ready, 1)
                v.memset(nmax[:, 0, :, :], 0.0).then_inc(p_ready, 2)
                v.memset(nmax[:, 1, :, :], 0.0).then_inc(pv_mm, NF)

                def norm_stats(src):
                    for t in range(QT):
                        last = v.bn_stats(stats[:, t, :], src[:, t, :])
                    ch.mark(last)

                def norm_moments(n):
                    ch.settle()
                    for t in range(QT):
                        last = v.bn_aggr(mv[:, t, :], stats[:, t, :])
                    last.then_inc(var_ready, 1)

                def norm_centre(src, n):
                    dve.wait_ge(var_ready, n + 1)
                    for t in range(QT):
                        last = v.tensor_scalar(cen[:, t, :], src[:, t, :], mv[:, t, 0:1], None, ALU.subtract)
                    last.then_inc(cen_ready, 1)

                def norm_scale(dst, n):
                    dve.wait_ge(cen_ready, n + 1)
                    dve.wait_ge(rstd_ready, n + 1)
                    for t in range(QT):
                        last = v.tensor_scalar(dst[:, t, :], cen[:, t, :], rstd[:, t:t + 1], None, ALU.mult)
                    return last

                def take_v(grp, g):
                    dve.wait_ge(v_mm, grp + 1)
                    v.tensor_copy(v16[:, :, :], M_BANK[:, 0:QT * J * HD].rearrange("p (t c) -> p t c", t=QT)
                                  ).then_inc(v16_ready, 1)
                    dve.wait_ge(v16_ready, grp + 1)
                    for t in range(QT):
                        last = v.tensor_tensor(va[:, g, t, :, 0:HD],
                                               v16[:, t, :].rearrange("p (j d) -> p j d", j=J),
                                               bv_sb[:, 64 * g:64 * (g + 1)].rearrange("p (j d) -> p j d", j=J), ALU.add)
                    last.then_inc(v_out, 1)

                def maxima(grp, g, i):
                    j, tiles = S_FILLS[i]
                    at = 0
                    hold(dve, s_mm, NF * grp + i + 1, spare)
                    for qt in tiles:
                        n = P * (qt + 1)
                        last = v.tensor_tensor_reduce(
                            out=unused[:, i % 2, at:at + n], in0=S_BANK[i % 2][:, at:at + n], in1=mask[:, T - n:T],
                            scale=-1.0, scalar=3.0e38, op0=ALU.add, op1=ALU.min,
                            accum_out=nmax[:, g % 2, qt, 32 * j + HD:32 * j + HD + 1])
                        at += n
                    last.then_inc(s_max, 1)

                def take_att(grp, g):
                    dve.wait_ge(pv_mm, NF * (grp + 2))
                    o = PV_BANK[:, :].rearrange("p (t j c) -> p t j c", t=QT, j=J)
                    ch.link(v.reciprocal(rden[:, :, :], o[:, :, :, HD]))
                    for t in range(QT):
                        last = v.tensor_tensor(att[:, t, 64 * g:64 * (g + 1)].rearrange("p (j d) -> p j d", j=J),
                                               o[:, t, :, 0:HD],
                                               rden[:, t, :].unsqueeze(2).broadcast_to([P, J, HD]), ALU.mult)
                    last.then_inc(att_out, 1)

                def take_y(b, half):
                    dve.wait_ge(y_mm, 2 * b + half + 1)
                    v.tensor_copy(y[:, 2 * half:2 * half + 2, :],
                                  (Q_BANK, K_BANK)[half][:, :].rearrange("p (t d) -> p t d", t=2)
                                  ).then_inc(y_out, 1)

                def bias_y(b):
                    dve.wait_ge(y_out, 2 * b + 2)
                    for t in range(QT):
                        last = v.tensor_tensor(y[:, t, :], y[:, t, :], bo_sb[:, :], ALU.add)
                    last.then_inc(y16_ready, 1)

                def add_x(b):
                    ch.settle()
                    dve.wait_ge(xr_in, 16 * b + 16)
                    dve.wait_ge(x1_out, 16 * b + 16)
                    v.tensor_tensor(x1[:, :, :], xr_sb[:, :, :], y[:, :, :], ALU.add).then_inc(x1_ready, 1)

                def finish(b, n, at):
                    if at == 0:
                        take_y(b, 0)
                    elif at == 1:
                        take_y(b, 1)
                    elif at == 2:
                        bias_y(b)
                    elif at == 3:
                        dve.wait_ge(y16_ready, b + 1)
                        norm_stats(y)
                    elif at == 4:
                        norm_moments(n)
                    elif at == 5:
                        norm_centre(y, n)
                    elif at == 6:
                        ch.mark(norm_scale(y, n))
                    elif at == 7:
                        add_x(b)
                    elif at == 8:
                        dve.wait_ge(x1_ready, b + 1)
                        norm_stats(x1)
                    elif at == 9:
                        norm_moments(n + 1)
                    elif at == 10:
                        norm_centre(x1, n + 1)
                    elif at == 11:
                        dve.wait_ge(xn2_free, b + 1)
                        norm_scale(xn2, n + 1).then_inc(xn2_ready, 1)

                def route(b, at):
                    if at == 0:
                        dve.wait_ge(logit_mm, b + 1)
                        v.tensor_tensor(logit[:, :, :], LOGITS, bs_sb[:, :].unsqueeze(1).broadcast_to([P, QT, E]),
                                        ALU.add).then_inc(logit_out, 1)
                    elif at == 1:
                        hold(dve, logit_out, b + 1, spare)
                        for t in range(QT):
                            last = v.max(top[:, t, :], logit[:, t, :])
                        ch.mark(last)
                    elif at == 2:
                        ch.settle()
                        v.tensor_tensor(dif[:, :], top[:, :, 1], top[:, :, 0], ALU.subtract).then_inc(dif_ready, 1)
                        for t in range(QT):
                            last = v.max_index(topi[:, t, :], top[:, t, :], logit[:, t, :])
                        ch.mark(last)
                    elif at == 3:
                        ch.settle()
                        ch.mark(v.tensor_copy(topf[:, :, :], topi[:, :, 0:TOP]))
                    elif at == 4:
                        ch.settle()
                        for r in range(TOP):
                            last = v.tensor_tensor(pick[r][:, :, :], iota8[:, :].unsqueeze(1).broadcast_to([P, QT, E]),
                                                   topf[:, :, r:r + 1].broadcast_to([P, QT, E]), ALU.is_equal)
                        ch.mark(last)
                    elif at == 5:
                        ch.settle()
                        v.tensor_tensor(both[:, :, :], pick[0][:, :, :], pick[1][:, :, :], ALU.add
                                        ).then_inc(both_ready, 1)

                def slots(b, at):
                    at_b = bass.ds(b * (QT * TOP), QT * TOP)
                    if at == 0:
                        dve.wait_ge(rank_mm, b + 1)
                        ch.mark(v.tensor_tensor(row[:, :, :], RANKS,
                                                keep["fill"][:, :].unsqueeze(1).broadcast_to([P, QT, E]), ALU.add))
                        dve.wait_ge(e1_ready, b + 1)
                        ch.mark(v.tensor_scalar(den[:, :], e1[:, :], 1.0, None, ALU.add))
                    elif at == 1:
                        ch.settle()
                        v.tensor_tensor(keep["fill"][:, :], keep["fill"][:, :], TOTAL, ALU.add).then_inc(rank_out, 1)
                        v.reciprocal(wts[:, :, 0], den[:, :])
                        for r in range(TOP):
                            last = v.tensor_tensor(prow[r][:, :, :], row[:, :, :], pick[r][:, :, :], ALU.mult)
                        ch.mark(last)
                    elif at == 2:
                        ch.settle()
                        v.tensor_tensor(wts[:, :, 1], e1[:, :], wts[:, :, 0], ALU.mult)
                        for r in range(TOP):
                            last = v.reduce_sum(slotf[:, :, r], prow[r][:, :, :], AX.X)
                        ch.mark(last)
                    elif at == 3:
                        ch.settle()
                        v.tensor_copy(slot[:, :, :], slotf[:, :, :]).then_inc(slot_ready, 1)
                        v.tensor_copy(keep["slots"][:, at_b], slotf[:, :, :].rearrange("p t r -> p (t r)"))
                        v.tensor_copy(keep["weights"][:, at_b], wts[:, :, :].rearrange("p t r -> p (t r)"))

                def next_norm(b, n, at, first=False):
                    if at == 0:
                        dve.wait_ge(x_in, 16 * b + 16)
                        norm_stats(x_sb)
                    elif at == 1:
                        norm_moments(n)
                    elif at == 2:
                        norm_centre(x_sb, n)
                    elif at == 3:
                        if not first:
                            dve.wait_ge(xnT_mm, b)
                        norm_scale(xn, n).then_inc(xn_ready, 1)

                def batch(b, first, in_last):
                    for g in range(G):
                        grp = G * b + g
                        ahead = not (in_last and g >= 2)
                        if ahead:
                            dve.wait_ge(q_mm, 4 + 2 * grp)
                        for i in range(NF):
                            if ahead:
                                maxima(grp + 2, (g + 2) % G, i)
                            if i == AT_TAKE_ATT and not (first and g == 0):
                                if g == 1 and not first:
                                    dve.wait_ge(attT_mm, b)
                                take_att(grp - 1, (g - 1) % G)
                            for n, at in enumerate(AT_NEXT_NORM):
                                if at == (g, i) and not in_last:
                                    next_norm(b + 1, 1 if first else 3 * b - 1, n)
                            for n, at in enumerate(AT_FINISH):
                                if at == (g, i) and not first:
                                    finish(b - 1, 3 * b - (1 if in_last else 0), n)
                            for n, at in enumerate(AT_ROUTE):
                                if at == (g, i) and not first:
                                    route(b - 1, n)
                            for n, at in enumerate(AT_SLOTS):
                                if at == (g, i) and not first:
                                    slots(b - 1, n)
                        if not in_last:
                            take_v(grp + G, g)

                for at in range(len(AT_NEXT_NORM)):
                    next_norm(0, 0, at, first=True)
                dve.wait_ge(bias_ready, 2)
                dve.wait_ge(w_in, 16 * 10)
                dve.wait_ge(const_ready, 1)
                for g in range(G - 1):
                    take_v(g, g)
                dve.wait_ge(pv_mm, NF)
                for i in range(NF):
                    maxima(0, 0, i)
                take_v(G - 1, G - 1)
                for i in range(NF):
                    maxima(1, 1, i)
                for n in range(3):
                    src = ws_f if n == 0 else ws_r
                    wch.link(v.tensor_copy(ws_part[:, :, n, :], src[:, :, :]))
                    if n < 2:
                        wch.link(v.tensor_tensor(ws_r[:, :, :], src[:, :, :], ws_part[:, :, n, :], ALU.subtract))
                batch(0, True, False)
                start = ch.n
                with dve.Fori(1, B - 1) as b:
                    ch.rebase(start + STEPS * (b - 1))
                    batch(b, False, False)
                    assert ch.n == STEPS, ch.n
                ch.rebase(start + STEPS * (B - 2))
                batch(B - 1, False, True)
                take_att(G * B - 1, G - 1)
                for at in range(len(AT_FINISH)):
                    finish(B - 1, 3 * B - 2, at)
                for at in range(len(AT_ROUTE)):
                    route(B - 1, at)
                for at in range(len(AT_SLOTS)):
                    slots(B - 1, at)

            @block.tensor
            def _(pe):
                mm = nc.tensor.matmul

                def transpose4(src, signal):
                    for k in range(KD):
                        for t in range(QT):
                            last = nc.tensor.transpose(M16[:, T * k + P * t:T * k + P * (t + 1)],
                                                       src[:, t, P * k:P * (k + 1)], ident[:, :])
                    last.then_inc(signal, 1)

                def project_q(g):
                    for k in range(KD):
                        last = mm(Q_BANK[:, :], wq_sb[:, k, g, :], xnT[:, k, :], start=(k == 0), stop=(k == KD - 1))
                    last.then_inc(q_mm, 1)

                def project_k(g):
                    for k in range(KD):
                        last = mm(K_BANK[:, :], wk_sb[:, k, g, :], xnT[:, k, :], start=(k == 0), stop=(k == KD - 1))
                    last.then_inc(k_mm, 1)

                def project_v(g):
                    for t in range(QT):
                        for k in range(KD):
                            last = mm(M_BANK[:, 64 * t:64 * (t + 1)], xnT[:, k, P * t:P * (t + 1)],
                                      wv_sb[:, k, 64 * g:64 * (g + 1)], start=(k == 0), stop=(k == KD - 1))
                    last.then_inc(v_mm, 1)

                def scores_qk(g, i):
                    (j, tiles), at = S_FILLS[i], 0
                    for qt in tiles:
                        n = P * (qt + 1)
                        last = mm(S_BANK[i % 2][:, at:at + n], qT[32 * j:32 * j + 32, g, P * qt:P * (qt + 1)],
                                  kT[32 * j:32 * j + 32, g, 0:n], start=True, stop=True)
                        at += n
                    last.then_inc(s_mm, 1)

                def scores_kq(g, i):
                    (j, tiles), at = FILLS[i], 0
                    for kt in tiles:
                        n = T - P * kt
                        last = mm(ST_BANK[i % 2][:, at:at + n], kT[32 * j:32 * j + 32, g, P * kt:P * (kt + 1)],
                                  qT[32 * j:32 * j + 32, g, P * kt:T], start=True, stop=True)
                        at += n
                    last.then_inc(st_mm, 1)

                def add_maxima(g):
                    mm(Q_BANK[:, :], ident[:, :], qT[:, g, :], start=True, stop=False)
                    for t in range(QT):
                        last = mm(Q_BANK[:, P * t:P * (t + 1)], nmax[:, g % 2, t, :], ident[:, :],
                                  start=False, stop=(t == QT - 1))
                    last.then_inc(q_mm, 1)

                def values(grp, g, i):
                    j, tiles = FILLS[i]
                    if j == 0:
                        pe.wait_ge(cut_ready, CUTS * grp + i // J + 1)
                    for kt in tiles:
                        for qt in range(kt, QT):
                            at = P_COL[kt, j] + P * (qt - kt)
                            last = mm(OUT[:, qt, j, 0:HD + 1], pT[:, at:at + P], va[:, g, kt, j, :],
                                      start=(i == 0 and qt == 0), stop=(i == NF - 1 and qt == QT - 1))
                    last.then_inc(pv_mm, 1)

                def project_out(b):
                    pe.wait_ge(attT_out, b + 1)
                    for t in range(QT):
                        for k in range(KD):
                            last = mm((Q_BANK, K_BANK)[t // 2][:, D * (t % 2):D * (t % 2 + 1)],
                                      attT[:, k, P * t:P * (t + 1)], wo_sb[:, k, :],
                                      start=(k == 0), stop=(k == KD - 1))
                        if t % 2:
                            last.then_inc(y_mm, 1)

                def logits(b):
                    pe.wait_ge(xn2T_out, b + 1)
                    for t in range(QT):
                        for s in range(3 * KD):
                            last = mm(LOGITS[:, t, :], attT[:, s // 3, P * t:P * (t + 1)], ws_part[:, s // 3, s % 3, :],
                                      start=(s == 0), stop=(s == 3 * KD - 1))
                    last.then_inc(logit_mm, 1)

                def ranks(b):
                    pe.wait_ge(both_ready, b + 1)
                    for t in range(QT):
                        for s in range(t + 1):
                            mm(RANKS[:, t, :], (before if s == t else ones)[:, :], both[:, s, :],
                               start=(s == 0), stop=(s == t))
                    for s in range(QT):
                        last = mm(TOTAL, ones[:, :], both[:, s, :], start=(s == 0), stop=(s == QT - 1))
                    last.then_inc(rank_mm, 1)

                def batch(b, first, in_last):
                    for g in range(G):
                        grp = G * b + g
                        ahead = not (in_last and g >= 2)
                        pe.wait_ge(q_out, 4 + 2 * grp if not (in_last and g) else q_uses(grp, True))
                        if ahead:
                            pe.wait_ge(k_out, grp + 3)
                        for i in range(NF):
                            pe.wait_ge(p_ready, NF * grp + i + 1)
                            scores_kq(g, i)
                            if ahead:
                                pe.wait_ge(s_max, NF * (grp + 2) + i - 1)
                                scores_qk((g + 2) % G, i)
                            if i == PV_LAG and not (first and g == 0):
                                pe.wait_ge(att_out, grp)
                            if i >= PV_LAG:
                                values(grp, g, i - PV_LAG)
                            if i == 1 and g == 1 and not first:
                                pe.wait_ge(att_out, grp - 1)
                                if not in_last:
                                    pe.wait_ge(v_out, grp + 4)
                                transpose4(att, attT_mm)
                            if i == AT_XN2_T and g == 2 and not first:
                                if not in_last:
                                    pe.wait_ge(v_out, grp + 4)
                                pe.wait_ge(xn2_ready, b)
                                transpose4(xn2, xn2T_mm)
                            if i == 0 and g == 3 and not first:
                                if not in_last:
                                    pe.wait_ge(k_out, grp + 4)
                                else:
                                    pe.wait_ge(y_out, 2 * b)
                                logits(b - 1)
                            if i == AT_RANKS and g == 3 and not first:
                                ranks(b - 1)
                            if i == AT_PROJECT_OUT and g == 1 and not first:
                                pe.wait_ge(q_out, q_uses(grp, in_last))
                                pe.wait_ge(k_out, grp + 4 if not in_last else G * B)
                                project_out(b - 1)
                            if i == AT_MAXIMA and not (in_last and g == G - 1):
                                if g == 1 and not first:
                                    pe.wait_ge(y_out, 2 * b - 1)
                                pe.wait_ge(s_max, NF * (grp + 2))
                                pe.wait_ge(q_out, q_uses(grp, in_last))
                                add_maxima((g + 1) % G)
                            if i == AT_NEXT_T and g == 0 and not in_last:
                                pe.wait_ge(xn_ready, b + 2)
                                pe.wait_ge(v_out, grp + 4)
                                transpose4(xn, xnT_mm)
                        if not in_last:
                            if g == 0:
                                pe.wait_ge(xnT_ready, b + 2)
                            pe.wait_ge(q_out, q_uses(grp, False) + 1)
                            project_q(g)
                            pe.wait_ge(k_out, grp + 4)
                            if g == 1 and not first:
                                pe.wait_ge(y_out, 2 * b)
                            if g == 3 and not first:
                                pe.wait_ge(rank_out, b)
                            project_k(g)
                        for i in range(NF - PV_LAG, NF):
                            values(grp, g, i)
                        if not in_last:
                            if g > 0:
                                pe.wait_ge(v_out, grp + 4)
                            if g == 1 and not first:
                                pe.wait_ge(attT_out, b)
                            if g == 2 and not first:
                                pe.wait_ge(xn2T_out, b)
                            project_v(g)

                pe.wait_ge(const_ready, 1)
                pe.wait_ge(xn_ready, 1)
                transpose4(xn, xnT_mm)
                pe.wait_ge(w_in, 16 * 10)
                pe.wait_ge(xnT_ready, 1)

                def first_projections(g, use):
                    if use:
                        pe.wait_ge(q_out, use)
                    project_q(g)
                    if g:
                        pe.wait_ge(k_out, g)
                    project_k(g)
                    if g:
                        pe.wait_ge(v_out, g)
                    project_v(g)

                def first_scores(grp):
                    pe.wait_ge(k_out, grp + 1)
                    for i in range(NF):
                        n = NF * grp + i
                        if n >= 2:
                            pe.wait_ge(s_max, n - 1)
                        scores_qk(grp, i)

                for g in range(G - 1):
                    first_projections(g, g)
                pe.wait_ge(q_out, G - 1)
                first_scores(0)
                pe.wait_ge(s_max, NF)
                add_maxima(0)
                first_projections(G - 1, G)
                first_scores(1)
                batch(0, True, False)
                with pe.Fori(1, B - 1) as b:
                    batch(b, False, False)
                batch(B - 1, False, True)
                pe.wait_ge(att_out, G * B)
                transpose4(att, attT_mm)
                project_out(B - 1)
                pe.wait_ge(xn2_ready, B)
                transpose4(xn2, xn2T_mm)
                pe.wait_ge(y_out, 2 * B)
                logits(B - 1)
                ranks(B - 1)


def experts(nc, sb, sem, spare, bank, keep, xs_dram, ys_dram):
    NTILE = TILES
    PAIRS = (NTILE - 1) // 2
    TAIL = [(i // 2, i % 2) for i in range(2 * PAIRS, NTILE)]
    TT = TS // P
    CP = FC // 2
    M_MAX = B * T // TS
    ident, gu_part, wd_part = keep["ident"], keep["gu"], keep["wd"]
    stack = ExitStack()
    with stack:
        iota_m = sb(stack, "iota_m", [P, M_MAX], F32)
        iota_i = sb(stack, "iota_i", [P, NTILE], F32)
        one8 = sb(stack, "one8", [P, E], F32)
        zeros = sb(stack, "zeros", [P, TT * D], F16)
        fill_u = sb(stack, "fill_u", [P, E], U32)
        count = sb(stack, "count", [P, E], F32)
        over = sb(stack, "over", [P, E, M_MAX], F32)
        tiles = sb(stack, "tiles", [P, E], F32)
        cum = sb(stack, "cum", [P, E], F32)
        past = sb(stack, "past", [P, NTILE, E], F32)
        pastn = sb(stack, "pastn", [P, NTILE, E], F32)
        own = sb(stack, "own", [P, NTILE], F32)
        begun = sb(stack, "begun", [P, NTILE], F32)
        rowf = sb(stack, "rowf", [P, NTILE], F32)
        ownc = sb(stack, "ownc", [P, NTILE], F32)
        table = sb(stack, "table", [P, 2, NTILE], U32)
        shift = sb(stack, "shift", [P, E - 1], F32)
        beyond = sb(stack, "beyond", [P, NT * TOP, E - 1], F32)
        moved = sb(stack, "moved", [P, NT * TOP], F32)
        xin = [sb(stack, f"xin{j}", [P, TT, D], F16) for j in range(2)]
        xT = [sb(stack, f"xT{j}", [P, KD, TS], F16) for j in range(2)]
        act_g = sb(stack, "act_g", [P, CP, 2 * TS], F32)
        hid = sb(stack, "hid", [P, CP, 2 * TS], F32)
        h1 = sb(stack, "h1", [P, CP, 2 * TS], F16)
        h2 = sb(stack, "h2", [P, CP, 2 * TS], F16)
        y_sb = [sb(stack, f"y_sb{j}", [P, TT, D], F32) for j in range(2)]

        G_BANK, U_BANK, Y_BANK = bank[0:3], bank[3:6], bank[6:8]
        XT16 = G_BANK[0][:, 0:KD * TS // 2].bitcast(F16)

        consts = sem("consts")
        plan = sem("plan")
        table_ready = sem("table_ready")
        pad_ready = sem("pad_ready")
        padded = sem("padded")
        xin_in = [sem(f"xin_in{j}") for j in range(2)]
        xT_mm = sem("xT_mm")
        xT_ready = sem("xT_ready")
        up_mm = sem("up_mm")
        silu_ready = sem("silu_ready")
        hid_ready = sem("hid_ready")
        h1_ready = sem("h1_ready")
        h2_ready = sem("h2_ready")
        down_mm = sem("down_mm")
        y_ready = sem("y_ready")
        ys_out = [sem(f"ys_out{j}") for j in range(2)]

        def blocks(c):
            if 2 * (c + 1) * P <= F:
                return ((slice(0, P), slice(0, 2 * TS), G_BANK[c][:, :], U_BANK[c][:, :]),)
            g_last = G_BANK[c][:, TS:2 * TS]
            return ((slice(0, P), slice(0, TS), G_BANK[c][:, 0:TS], U_BANK[c][:, 0:TS]),
                    (slice(0, FR), slice(TS, 2 * TS), g_last[0:FR, :], g_last[P // 2:P // 2 + FR, :]))

        def rows_of(dram, row):
            return dram[bass.ds(row, TS), :].rearrange("(t p) d -> p t d", p=P)

        with nc.Block() as block:
            @block.sync
            def _(sp):
                def load(h, j):
                    row = sp.value_load(table[0:1, 0, bass.ds(2 * h + j, 1)], min_val=0, max_val=ROWS - TS)
                    sp.dma_start(xin[j][:, :, :], rows_of(xs_dram, row)).then_inc(xin_in[j], 16)

                def store(h, j):
                    hold(sp, y_ready, 2 * h + j + 2, spare)
                    sp.dma_start(rows_of(ys_dram, (2 * h + j) * TS), y_sb[j][:, :, :]).then_inc(ys_out[j], 16)

                for j in range(2):
                    sp.sem_inc(ys_out[j], 16)
                sp.wait_ge(pad_ready, 1)
                sp.wait_ge(consts, 4)
                for e in range(E):
                    row = sp.value_load(fill_u[0:1, e:e + 1], min_val=0, max_val=ROWS - TS)
                    sp.dma_start(xs_dram[bass.ds(row, TS), :].rearrange("(p r) d -> p (r d)", p=P),
                                 zeros[:, :]).then_inc(padded, 16)
                sp.wait_ge(table_ready, 1)
                sp.wait_ge(padded, 16 * E)
                sp.wait_ge(keep["scattered"], 16 * TOP * QT * B)
                for j in range(2):
                    load(0, j)
                with sp.Fori(0, (NTILE - 2) // 2) as h:
                    for j in range(2):
                        hold(sp, xT_mm, 2 * h + j + 1, spare)
                        load(h + 1, j)
                        store(h, j)
                for i in range((NTILE - 2) // 2 * 2, NTILE):
                    if i + 2 < NTILE:
                        sp.wait_ge(xT_mm, i + 1)
                        load(i // 2 + 1, i % 2)
                    store(i // 2, i % 2)
                for j in range(2):
                    sp.wait_ge(ys_out[j], 16 * ((NTILE - j + 1) // 2) + 16)

            @block.gpsimd
            def _(pool):
                gp = nc.gpsimd
                any_f = dict(allow_small_or_imprecise_dtypes=True)
                gp.iota(iota_m[:, :], [[TS, M_MAX]], base=0, channel_multiplier=0, **any_f).then_inc(consts, 1)
                gp.iota(iota_i[:, :], [[1, NTILE]], base=0, channel_multiplier=0, **any_f).then_inc(consts, 1)
                gp.memset(one8[:, :], 1.0).then_inc(consts, 1)
                gp.memset(zeros[:, :], 0.0).then_inc(consts, 1)
                scatter_rows(gp, keep, xs_dram, 0, 1)

            @block.scalar
            def _(act):
                sc = nc.scalar

                def take_xT(i, j):
                    act.wait_ge(xT_mm, i + 1)
                    sc.activation(xT[j][:, :, :], XT16.rearrange("p (k t) -> p k t", k=KD), ACT.Copy
                                  ).then_inc(xT_ready, 1)

                def tile(i, j, is_last):
                    for c in range(CP):
                        act.wait_ge(up_mm, CP * i + c + 1)
                        for rows, cols, gate, _ in blocks(c):
                            last = sc.activation(act_g[rows, c, cols], gate, ACT.Silu,
                                                 scale=1.0 / WSCALE)
                        last.then_inc(silu_ready, 1)
                        act.wait_ge(hid_ready, CP * i + c + 1)
                        act.wait_ge(down_mm, i + 1)
                        for rows, cols, _, _ in blocks(c):
                            last = sc.activation(h1[rows, c, cols], hid[rows, c, cols], ACT.Copy)
                        last.then_inc(h1_ready, 1)
                    if not is_last:
                        take_xT(i + 1, 1 - j)

                take_xT(0, 0)
                with act.Fori(0, PAIRS) as h:
                    for j in range(2):
                        tile(2 * h + j, j, False)
                for h, j in TAIL:
                    tile(2 * h + j, j, 2 * h + j == NTILE - 1)

            @block.vector
            def _(dve):
                v = nc.vector
                dve.sem_inc(y_ready, 1)
                ch = Chain(dve, plan, spare)
                v.tensor_copy(fill_u[:, :], keep["fill"][:, :]).then_inc(pad_ready, 1)
                dve.wait_ge(consts, 4)
                ch.link(v.tensor_tensor(count[:, :], keep["fill"][:, :], keep["first"][:, :], ALU.subtract))
                ch.link(v.tensor_tensor(over[:, :, :], count[:, :].unsqueeze(2).broadcast_to([P, E, M_MAX]),
                                        iota_m[:, :].unsqueeze(1).broadcast_to([P, E, M_MAX]), ALU.is_gt))
                ch.link(v.reduce_sum(tiles[:, :], over[:, :, :], AX.X))
                ch.link(v.tensor_tensor_scan(cum[:, :], one8[:, :], tiles[:, :], 0.0, ALU.mult, ALU.add))
                ch.link(v.tensor_tensor(past[:, :, :], iota_i[:, :].unsqueeze(2).broadcast_to([P, NTILE, E]),
                                        cum[:, :].unsqueeze(1).broadcast_to([P, NTILE, E]), ALU.is_ge))
                v.tensor_tensor(pastn[:, :, :], past[:, :, :], tiles[:, :].unsqueeze(1).broadcast_to([P, NTILE, E]),
                                ALU.mult)
                ch.link(v.reduce_sum(own[:, :], past[:, :, :], AX.X))
                ch.link(v.reduce_sum(begun[:, :], pastn[:, :, :], AX.X))
                ch.link(v.tensor_tensor(rowf[:, :], iota_i[:, :], begun[:, :], ALU.subtract))
                ch.link(v.tensor_scalar(rowf[:, :], rowf[:, :], float(TS), None, ALU.mult))
                ch.link(v.scalar_tensor_tensor(rowf[:, :], own[:, :], float(REGION), rowf[:, :], ALU.mult, ALU.add))
                ch.link(v.tensor_scalar(ownc[:, :], own[:, :], float(E - 1), None, ALU.min))
                v.tensor_copy(table[:, 0, :], rowf[:, :])
                v.tensor_copy(table[:, 1, :], ownc[:, :]).then_inc(table_ready, 1)
                n_slot = NT * TOP
                ch.link(v.tensor_scalar(shift[:, :], tiles[:, 0:E - 1], float(TS), -float(REGION), ALU.mult, ALU.add))
                ch.link(v.tensor_tensor(beyond[:, :, :], keep["slots"][:, :].unsqueeze(2).broadcast_to([P, n_slot, E - 1]),
                                        keep["first"][:, 1:E].unsqueeze(1).broadcast_to([P, n_slot, E - 1]), ALU.is_ge))
                ch.link(v.tensor_tensor(beyond[:, :, :], beyond[:, :, :],
                                        shift[:, :].unsqueeze(1).broadcast_to([P, n_slot, E - 1]), ALU.mult))
                ch.link(v.reduce_sum(moved[:, :], beyond[:, :, :], AX.X))
                v.tensor_tensor(keep["slots"][:, :], keep["slots"][:, :], moved[:, :], ALU.add)

                def tile(h, j):
                    i = 2 * h + j
                    for c in range(CP):
                        dve.wait_ge(silu_ready, CP * i + c + 1)
                        for rows, cols, _, other in blocks(c):
                            last = v.scalar_tensor_tensor(hid[rows, c, cols], other, HSCALE / WSCALE,
                                                          act_g[rows, c, cols], ALU.mult, ALU.mult)
                        last.then_inc(hid_ready, 1)
                        dve.wait_ge(h1_ready, CP * i + c + 1)
                        for rows, cols, _, _ in blocks(c):
                            last = v.tensor_tensor(h2[rows, c, cols], hid[rows, c, cols], h1[rows, c, cols],
                                                   ALU.subtract)
                        last.then_inc(h2_ready, 1)
                    dve.wait_ge(down_mm, i + 2)
                    dve.wait_ge(ys_out[j], 16 * h + 16)
                    for t in range(TT):
                        last = v.tensor_scalar(y_sb[j][:, t, :], Y_BANK[t][:, 0:D], 1.0 / (WSCALE * HSCALE), None,
                                               ALU.mult)
                    last.then_inc(y_ready, 1)

                with dve.Fori(0, PAIRS) as h:
                    for j in range(2):
                        tile(h, j)
                for h, j in TAIL:
                    tile(h, j)

            @block.tensor
            def _(pe):
                mm = nc.tensor.matmul

                def transpose_rows(h, j):
                    pe.wait_ge(xin_in[j], 16 * h + 16)
                    for k in range(KD):
                        for t in range(TT):
                            last = nc.tensor.transpose(XT16[:, TS * k + P * t:TS * k + P * (t + 1)],
                                                       xin[j][:, t, P * k:P * (k + 1)], ident[:, :])
                    last.then_inc(xT_mm, 1)

                def up(i, j, c, col):
                    for half in range(2):
                        n, cols = 2 * c + half, slice(TS * half, TS * (half + 1))
                        if n < FC - 1:
                            sources = ((G_BANK[c], n * P, P), (U_BANK[c], GU_UP + n * P, P))
                        else:
                            sources = ((G_BANK[c], GU_LAST, GU - GU_LAST),)
                        for dst, at, width in sources:
                            for s in range(2 * KD):
                                k, part = s // 2, s % 2
                                last = mm(dst[0:width, cols], gu_part[part][:, bass.ds(col + (k * GU + at), width)],
                                          xT[j][:, k, :], start=(s == 0), stop=(s == 2 * KD - 1))
                    last.then_inc(up_mm, 1)

                def down(i, col):
                    for c in range(FC):
                        rows = P if c < FC - 1 else FR
                        if c % 2 == 0:
                            pe.wait_ge(h1_ready, CP * i + c // 2 + 1)
                        for s, (h, w) in enumerate(((h1, 0), (h1, 1), (h2, 0))):
                            if c % 2 == 0 and s == 2:
                                pe.wait_ge(h2_ready, CP * i + c // 2 + 1)
                            for t in range(TT):
                                at = (c % 2) * TS + t * P
                                last = mm(Y_BANK[t][:, 0:D], h[0:rows, c // 2, at:at + P],
                                          wd_part[w][0:rows, bass.ds(col + c * D, D)],
                                          start=(c == 0 and s == 0), stop=(c == FC - 1 and s == 2))
                    last.then_inc(down_mm, 1)

                def tile(h, j, is_last):
                    i = 2 * h + j
                    expert = pe.value_load(table[0:1, 1, bass.ds(i, 1)], min_val=0, max_val=E - 1)
                    col_gu, col_d = expert * (KD * GU), expert * (FC * D)
                    pe.wait_ge(xT_ready, i + 1)
                    for c in range(CP):
                        up(i, j, c, col_gu)
                    if not is_last:
                        pe.wait_ge(silu_ready, CP * i + 1)
                        transpose_rows(h + j, 1 - j)
                    pe.wait_ge(y_ready, i + 1)
                    down(i, col_d)

                pe.sem_inc(down_mm, 1)
                pe.wait_ge(table_ready, 1)
                transpose_rows(0, 0)
                with pe.Fori(0, PAIRS) as h:
                    for j in range(2):
                        tile(h, j, False)
                for h, j in TAIL:
                    tile(h, j, 2 * h + j == NTILE - 1)


def combine(nc, sb, sem, spare, keep, x1_dram, ys_dram, out):
    TT = 2
    N = NT // TT
    W = TT * TOP
    x1_v = x1_dram.rearrange("(i t p) d -> i p t d", t=TT, p=P)
    out_v = out.rearrange("b (h t p) d -> (b h) p t d", t=TT, p=P)
    stack = ExitStack()
    with stack:
        idx = [sb(stack, f"idx{j}", [P, W], U32) for j in range(2)]
        yg = [sb(stack, f"yg{j}", [P, W, D], F32) for j in range(2)]
        x1 = [sb(stack, f"x1c{j}", [P, TT, D], F16) for j in range(2)]
        wcur = sb(stack, "wcur", [P, W], F32)
        part = sb(stack, "part", [P, TT, D], F32)
        total = sb(stack, "total", [P, TT, D], F32)
        res = [sb(stack, f"res{j}", [P, TT, D], F32) for j in range(2)]
        nrm = sb(stack, "nrm", [P, TT, D], F32)
        stats = sb(stack, "stats3", [P, TT, 6], F32)
        mv = sb(stack, "mv3", [P, TT, 2], F32)
        std = sb(stack, "std3", [P, TT], F32)
        rstd = sb(stack, "rstd3", [P, TT], F32)
        eps = sb(stack, "eps", [P, 1], F32)

        idx_ready = sem("idx_ready")
        gathered = [sem(f"gathered{j}") for j in range(2)]
        x1_in = [sem(f"x1_in{j}") for j in range(2)]
        sum_ready = sem("sum_ready")
        eps_ready = sem("eps_ready")
        cchain = sem("cchain")
        var_ready = sem("var_ready3")
        std_ready = sem("std_ready3")
        fin = sem("fin")
        stored = [sem(f"stored{j}") for j in range(2)]

        with nc.Block() as block:
            @block.sync
            def _(sp):
                def load(h, j):
                    sp.dma_start(x1[j][:, :, :], x1_v[2 * h + j, :, :, :]).then_inc(x1_in[j], 16)

                def store(h, j):
                    hold(sp, fin, 2 * h + j + 1, spare)
                    sp.dma_start(out_v[2 * h + j, :, :, :], res[j][:, :, :]).then_inc(stored[j], 16)

                for j in range(2):
                    sp.sem_inc(stored[j], 16)
                for j in range(2):
                    load(0, j)
                with sp.Fori(0, N // 2 - 1) as h:
                    for j in range(2):
                        store(h, j)
                        load(h + 1, j)
                for j in range(2):
                    store(N // 2 - 1, j)
                for j in range(2):
                    sp.wait_ge(stored[j], 8 * N + 16)

            @block.gpsimd
            def _(pool):
                gp = nc.gpsimd
                gp.memset(eps[:, :], LN_EPS).then_inc(eps_ready, 1)
                with pool.Fori(0, N // 2) as h:
                    for j in range(2):
                        n = 2 * h + j
                        hold(pool, sum_ready, n + 1, spare)
                        gp.tensor_copy(idx[j][:, :], keep["slots"][:, bass.ds(n * W, W)]).then_inc(idx_ready, 1)
                        hold(pool, idx_ready, n + 1, spare)
                        for w in range(W):
                            gp.indirect_dma_start(
                                out=yg[j][:, w, :], out_offset=None, in_=ys_dram[:, :],
                                in_offset=bass.IndirectOffsetOnAxis(ap=idx[j][:, w:w + 1], axis=0),
                            ).then_inc(gathered[j], 16)

            @block.scalar
            def _(act):
                act.wait_ge(eps_ready, 1)
                with act.Fori(0, N) as i:
                    act.wait_ge(var_ready, i + 1)
                    nc.scalar.activation(std[:, :], mv[:, :, 1], ACT.Sqrt, bias=eps[:, 0:1]).then_inc(std_ready, 1)

            @block.vector
            def _(dve):
                v = nc.vector
                dve.sem_inc(sum_ready, 2)
                ch = Chain(dve, cchain, spare)
                with dve.Fori(0, N // 2) as h:
                    for j in range(2):
                        n = 2 * h + j
                        ch.rebase(6 * n)
                        ch.link(v.tensor_copy(wcur[:, :], keep["weights"][:, bass.ds(n * W, W)]))
                        dve.wait_ge(gathered[j], 16 * W * (h + 1))
                        for t in range(TT):
                            last = v.tensor_scalar(part[:, t, :], yg[j][:, TOP * t, :], wcur[:, TOP * t:TOP * t + 1],
                                                   None, ALU.mult)
                        ch.link(last)
                        for t in range(TT):
                            last = v.scalar_tensor_tensor(total[:, t, :], yg[j][:, TOP * t + 1, :],
                                                          wcur[:, TOP * t + 1:TOP * t + 2], part[:, t, :],
                                                          ALU.mult, ALU.add)
                        last.then_inc(sum_ready, 1)
                        dve.wait_ge(sum_ready, n + 3)
                        for t in range(TT):
                            last = v.bn_stats(stats[:, t, :], total[:, t, :])
                        ch.link(last)
                        for t in range(TT):
                            last = v.bn_aggr(mv[:, t, :], stats[:, t, :])
                        last.then_inc(var_ready, 1)
                        dve.wait_ge(var_ready, n + 1)
                        dve.wait_ge(std_ready, n + 1)
                        ch.link(v.reciprocal(rstd[:, :], std[:, :]))
                        for t in range(TT):
                            last = v.tensor_scalar(nrm[:, t, :], total[:, t, :], mv[:, t, 0:1], rstd[:, t:t + 1],
                                                   ALU.subtract, ALU.mult)
                        ch.link(last)
                        dve.wait_ge(x1_in[j], 16 * h + 16)
                        dve.wait_ge(stored[j], 16 * h + 16)
                        ch.link(v.tensor_tensor(res[j][:, :, :], nrm[:, :, :], x1[j][:, :, :], ALU.add))
                        dve.sem_inc(fin, 1)


_OUT = ("out_0", (B, T, D), "float32")


def kernel(**inputs):
    import numpy as np
    import concourse.bacc as bacc
    from concourse.bass_utils import run_bass_kernel_spmd

    a = {k: np.ascontiguousarray(v) for k, v in inputs.items()}

    def by_head(w):
        w = w.T.reshape(KD, P, G, J, HD)
        r = np.zeros((KD, P, G, J, 32), w.dtype)
        r[..., :HD] = w
        return np.ascontiguousarray(r.reshape(KD, P, G, P).transpose(1, 0, 2, 3))

    def bias_by_head(b, fill):
        r = np.zeros((G, J, 32), b.dtype)
        r[..., :HD] = b.reshape(G, J, HD)
        r[..., HD] = fill
        return np.ascontiguousarray(r.reshape(G, P).T)

    def by_slice(w):
        return np.ascontiguousarray(w.T.reshape(KD, P, D).transpose(1, 0, 2))

    arrays = {
        "x": a["L0_attn_hidden_states"],
        "wq": by_head(a["L0_attn_wq"]), "wk": by_head(a["L0_attn_wk"]),
        "wv": by_slice(a["L0_attn_wv"]), "wo": by_slice(a["L0_attn_wo"]),
        "bq": bias_by_head(a["L0_attn_bq"], 0), "bk": bias_by_head(a["L0_attn_bk"], 1),
        "bv": a["L0_attn_bv"], "bo": a["L0_attn_bo"],
        "ws": a["L0_ffn_Ws"], "bs": a["L0_ffn_bs"],
        "wg": a["L0_ffn_Wg"], "wu": a["L0_ffn_Wu"], "wd": a["L0_ffn_Wd"],
    }
    nc = bacc.Bacc("TRN2", target_bir_lowering=False, num_devices=1)
    args = [nc.dram_tensor(k, v.shape, mybir.dt.from_np(v.dtype), kind="ExternalInput").ap()
            for k, v in arrays.items()]
    out = nc.dram_tensor(_OUT[0], _OUT[1], mybir.dt.from_np(np.dtype(_OUT[2])), kind="ExternalOutput").ap()
    build(nc, *args, out)
    r = run_bass_kernel_spmd(nc, [arrays], core_ids=[0])
    return r.results[0][_OUT[0]]
```

```python
from contextlib import ExitStack

import concourse.bass as bass
from concourse import mybir

ALU = mybir.AluOpType
ACT = mybir.ActivationFunctionType
AX = mybir.AxisListType
F32 = mybir.dt.float32
F16 = mybir.dt.float16
BF16 = mybir.dt.bfloat16
U32 = mybir.dt.uint32

P = 128
B, T, D = 8, 512, 256
H, HD = 16, 16
KD = D // P
QT = T // P
G, J = 4, 4
NT = B * QT
E, F = 8, 688
FC = -(-F // P)
FR = F - (FC - 1) * P
TILES_OF = ((0,), (1, 3), (2,))
FILLS = [(j, tiles) for tiles in TILES_OF for j in range(J)]
S_FILLS = [(j, tiles) for tiles in ((2, 0), (1,), (3,)) for j in range(J)]
CUTS = len(TILES_OF)
NF = len(FILLS)


def width(key_tiles):
    return sum(T - P * kt for kt in key_tiles)


P_COL = {(kt, j): sum(width(tiles) for _, tiles in FILLS[:i]) + width(tiles[:m])
         for i, (j, tiles) in enumerate(FILLS) for m, kt in enumerate(tiles)}
P_COLS = sum(width(tiles) for _, tiles in FILLS)
TOP = 2
TS = 2 * P
REGION = B * T + TS
TILES = (TOP * B * T + E * (TS - 1)) // TS
SPARE_TILES = TILES - TOP * B * T // TS
ROWS = E * REGION + (SPARE_TILES + 1) * TS
RESULTS = TOP * B * T + (E + SPARE_TILES + 1) * TS
W = D + 4
GU_UP = (FC - 1) * P
GU_LAST = 2 * GU_UP
GU = GU_LAST + P // 2 + FR
PV_LAG = 7
LN_EPS = 1e-5
LN_EPS16 = 2.0 ** -24 * 168
WSCALE = 256.0
HSCALE = 64.0
MASK = -10000.0
INV_SCALE = float(HD) ** 0.5


def hold(eng, sem, value, spare):
    eng.wait_ge(sem, value)
    eng.sem_inc(spare, 1)


class Chain:

    def __init__(self, eng, sem, spare):
        self.eng, self.sem, self.spare, self.base, self.n = eng, sem, spare, 0, 0

    def link(self, ins):
        ins.then_inc(self.sem, 1)
        self.n += 1
        hold(self.eng, self.sem, self.base + self.n, self.spare)

    def mark(self, ins):
        ins.then_inc(self.sem, 1)
        self.n += 1

    def settle(self):
        hold(self.eng, self.sem, self.base + self.n, self.spare)

    def rebase(self, base):
        self.base, self.n = base, 0


def build(nc, x, wq, wk, wv, wo, bq, bk, bv, bo, ws, bs, wg, wu, wd, out):
    x1_dram = nc.dram_tensor("x1_rows", [NT * P, D], F16).ap()
    xs_dram = nc.dram_tensor("dispatch_rows", [ROWS, W // 2], F32).ap()
    ys_dram = nc.dram_tensor("expert_rows", [RESULTS, D], F32).ap()
    outer = ExitStack()
    with outer:
        def sb(stack, name, shape, dt):
            return stack.enter_context(nc.sbuf_tensor(name, shape, dt))

        def sem(name):
            return outer.enter_context(nc.semaphore(name))

        spare = sem("spare")
        bank = [outer.enter_context(nc.psum_tensor(f"bank{i}", [P, 512], F32)) for i in range(8)]
        keep = {
            "ident": sb(outer, "ident", [P, P], F16),
            "gu": [sb(outer, f"gu_part{i}", [P, E * KD * GU], F16) for i in range(2)],
            "wd": [sb(outer, f"wd_part{i}", [P, E * FC * D], F16) for i in range(2)],
            "slot": sb(outer, "slot", [P, QT, TOP], U32),
            "rows": sb(outer, "rows", [P, QT, TOP, W // 2], F32),
            "scattered": sem("scattered"),
            "fill": sb(outer, "fill", [P, E], F32),
            "first": sb(outer, "first", [P, E], F32),
        }
        attention(nc, sb, sem, spare, bank, keep, x, wq, wk, wv, wo, bq, bk, bv, bo, ws, bs, wg, wu, wd,
                  x1_dram, xs_dram)
        x1_all = sb(outer, "x1_all", [P, NT, D], F16)
        x1_in = sem("x1_in")
        experts(nc, sb, sem, spare, bank, keep, x1_all, x1_in, x1_dram, xs_dram, ys_dram)
        combine(nc, sb, sem, spare, x1_all, x1_in, ys_dram, out)
    return nc


def scatter_rows(gp, keep, xs_dram, part, parts):
    n = TOP * QT
    for i in range(part * n // parts, (part + 1) * n // parts):
        t, r = i // TOP, i % TOP
        gp.indirect_dma_start(
            out=xs_dram[:, :], in_=keep["rows"][:, t, r, :], in_offset=None,
            out_offset=bass.IndirectOffsetOnAxis(ap=keep["slot"][:, t, r:r + 1], axis=0),
        ).then_inc(keep["scattered"], 16)


def attention(nc, sb, sem, spare, bank, keep, x, wq, wk, wv, wo, bq, bk, bv, bo, ws, bs, wg, wu, wd,
              x1_dram, xs_dram):
    x_v = x.rearrange("b (t p) d -> b p t d", p=P)
    x1_v = x1_dram.rearrange("(b t p) d -> b p t d", t=QT, p=P)
    ident = keep["ident"]
    stack = ExitStack()
    with stack:
        wq_sb = sb(stack, "wq_sb", [P, KD, G, P], F16)
        wk_sb = sb(stack, "wk_sb", [P, KD, G, P], F16)
        wv_sb = sb(stack, "wv_sb", [P, KD, D], F16)
        wo_sb = sb(stack, "wo_sb", [P, KD, D], F16)
        bq16 = sb(stack, "bq16", [P, G], F16)
        bk16 = sb(stack, "bk16", [P, G], F16)
        bq_sb = sb(stack, "bq_sb", [P, G], F32)
        bk_sb = sb(stack, "bk_sb", [P, G], F32)
        bv_sb = sb(stack, "bv_sb", [P, D], F16)
        bo_sb = sb(stack, "bo_sb", [P, D], F16)
        ws_f = sb(stack, "ws_f", [P, KD, E], F32)
        ws_r = sb(stack, "ws_r", [P, KD, E], F32)
        ws_part = sb(stack, "ws_part", [P, KD, 3, E], BF16)
        bs_sb = sb(stack, "bs_sb", [P, E], F32)
        mask = sb(stack, "mask", [P, T], F16)
        before = sb(stack, "before", [P, P], F16)
        ones = sb(stack, "ones", [P, P], F16)
        power = sb(stack, "power", [P, 2, QT], F32)
        wscale = sb(stack, "wscale", [P, 1], F32)
        iota8 = sb(stack, "iota8", [P, E], F32)
        x_sb = sb(stack, "x_sb", [P, QT, D], F16)
        xr_sb = sb(stack, "xr_sb", [P, QT, D], F16)
        xn = sb(stack, "xn", [P, QT, D], F16)
        xnT = sb(stack, "xnT", [P, KD, T], F16)
        qT = sb(stack, "qT", [P, G, T], F16)
        kT = sb(stack, "kT", [P, G, T], F16)
        va = sb(stack, "va", [P, G, QT, J, HD + 1], F16)
        v16 = sb(stack, "v16", [P, QT, J * HD], F16)
        nmax = sb(stack, "nmax", [P, 2, QT, P], F16)
        pT = sb(stack, "pT", [P, P_COLS], F16)
        unused = sb(stack, "unused", [P, 2, T], F16)
        rden = sb(stack, "rden", [P, QT, J], F32)
        att = sb(stack, "att", [P, QT, D], F16)
        attT = sb(stack, "attT", [P, KD, T], F16)
        y = sb(stack, "y", [P, QT, D], F16)
        x1 = sb(stack, "x1", [P, QT, D], F16)
        stats = sb(stack, "stats", [P, QT, 6], F32)
        mv = sb(stack, "mv", [P, QT, 2], F16)
        veps = sb(stack, "veps", [P, QT], F16)
        std = sb(stack, "std", [P, QT], F16)
        cen = sb(stack, "cen", [P, QT, D], F16)
        rstd = sb(stack, "rstd", [P, QT], F32)
        st_gu = sb(stack, "st_gu", [P, KD * F], F32)
        st_d = sb(stack, "st_d", [P, FC * D], F32)
        logit = sb(stack, "logit", [P, QT, E], F32)
        top = sb(stack, "top", [P, QT, E], F32)
        topi = sb(stack, "topi", [P, QT, E], U32)
        topf = sb(stack, "topf", [P, QT, TOP], F32)
        pick = [sb(stack, f"pick{r}", [P, QT, E], F32) for r in range(TOP)]
        both = sb(stack, "both", [P, QT, E], F16)
        dif = sb(stack, "dif", [P, QT], F32)
        e1 = sb(stack, "e1", [P, QT], F32)
        den = sb(stack, "den", [P, QT], F32)
        wts = sb(stack, "wts", [P, QT, TOP], F32)
        row = sb(stack, "row", [P, QT, E], F32)
        prow = [sb(stack, f"prow{r}", [P, QT, E], F32) for r in range(TOP)]
        slotf = sb(stack, "slotf", [P, QT, TOP], F32)
        rows16 = keep["rows"][:, :, :, :].bitcast(F16)
        slot, xn2 = keep["slot"], rows16[:, :, 0, 0:D]
        ids = sb(stack, "ids", [P, QT, TOP], F32)
        spare_ids = sb(stack, "spare_ids", [P, SPARE_TILES + 1, TS // P], F32)

        S_BANK, ST_BANK = (bank[0], bank[1]), (bank[2], bank[3])
        PV_BANK, Q_BANK, K_BANK, M_BANK = bank[4], bank[5], bank[6], bank[7]
        M16 = M_BANK[:, :].bitcast(F16)
        spares = pT[:, 0:(SPARE_TILES + 1) * (TS // P) * W].rearrange("p (e t w) -> p e t w", t=TS // P, w=W)
        OUT = PV_BANK[:, :].rearrange("p (t j c) -> p t j c", t=QT, j=J)
        LOGITS = K_BANK[:, 0:QT * E].rearrange("p (t e) -> p t e", t=QT)
        RANKS = K_BANK[:, 64:64 + QT * E].rearrange("p (t e) -> p t e", t=QT)
        TOTAL = K_BANK[:, 128:128 + E]

        w_in = sem("w_in")
        x_in = sem("x_in")
        xr_in = sem("xr_in")
        pool_const = sem("pool_const")
        const_ready = sem("const_ready")
        zero_ready = sem("zero_ready")
        bias_ready = sem("bias_ready")
        var_ready = sem("var_ready")
        veps_ready = sem("veps_ready")
        std_ready = sem("std_ready")
        cen_ready = sem("cen_ready")
        rstd_ready = sem("rstd_ready")
        xn_ready = sem("xn_ready")
        xnT_mm = sem("xnT_mm")
        xnT_ready = sem("xnT_ready")
        q_mm = sem("q_mm")
        q_out = sem("q_out")
        k_mm = sem("k_mm")
        k_out = sem("k_out")
        v_mm = sem("v_mm")
        v_out = sem("v_out")
        s_mm = sem("s_mm")
        s_max = sem("s_max")
        st_mm = sem("st_mm")
        p_ready = sem("p_ready")
        pv_mm = sem("pv_mm")
        att_out = sem("att_out")
        attT_mm = sem("attT_mm")
        attT_out = sem("attT_out")
        y_mm = sem("y_mm")
        y_out = sem("y_out")
        x1_ready = sem("x1_ready")
        xn2_ready = sem("xn2_ready")
        x1_out = sem("x1_out")
        xn2T_mm = sem("xn2T_mm")
        xn2T_out = sem("xn2T_out")
        logit_mm = sem("logit_mm")
        logit_out = sem("logit_out")
        both_ready = sem("both_ready")
        dif_ready = sem("dif_ready")
        e1_ready = sem("e1_ready")
        rank_mm = sem("rank_mm")
        rank_out = sem("rank_out")
        slot_ready = sem("slot_ready")
        xn2_free = sem("xn2_free")
        cut_ready = sem("cut_ready")
        ids_ready = sem("ids_ready")
        spare_ready = sem("spare_ready")
        copy_ready = sem("copy_ready")
        zeros_out = sem("zeros_out")
        dve_chain = sem("dve_chain")
        ws_chain = sem("ws_chain")
        v16_ready = sem("v16_ready")
        y16_ready = sem("y16_ready")
        g_in = sem("g_in")
        d_in = sem("d_in")
        u_in = sem("u_in")
        hi_ready = sem("hi_ready")
        mul_ready = sem("mul_ready")
        lo_ready = sem("lo_ready")

        AT_TAKE_ATT, AT_MAXIMA, AT_PROJECT_OUT, AT_NEXT_T, AT_XN2_T, AT_RANKS = 4, 6, 4, 9, 0, 9
        AT_NEXT_NORM = ((0, 0), (0, 1), (0, 2), (0, 3), (0, 4), (0, 6), (0, 7))
        AT_FINISH = ((1, 4), (1, 6), (1, 7), (1, 8), (1, 9), (1, 10), (1, 10), (1, 11),
                     (2, 0), (2, 1), (2, 2), (2, 3), (2, 4), (2, 5), (2, 6), (2, 7), (2, 10), (2, 11))
        AT_ROUTE = ((3, 4), (3, 5), (3, 6), (3, 6), (3, 7), (3, 8))
        AT_SLOTS = ((3, 9), (3, 10), (3, 11), (3, 11))
        AT_SCATTER = ((1, 0), (1, 1))
        STEPS = 17

        LAST = G * (B - 1)

        def places(b, which, part):
            if which == 1:
                return ((keep["wd"][part][:, bass.ds(b * (FC * D), FC * D)], st_d[:, :]),)
            dst = keep["gu"][part][:, bass.ds(b * (KD * GU), KD * GU)].rearrange("p (k c) -> p k c", k=KD)
            src = st_gu[:, :].rearrange("p (k f) -> p k f", k=KD)
            at, last_at = (0, GU_LAST) if which == 0 else (GU_UP, GU_LAST + P // 2)
            return ((dst[:, :, at:at + GU_UP], src[:, :, 0:GU_UP]),
                    (dst[:, :, last_at:last_at + FR], src[:, :, GU_UP:F]))

        def q_uses(grp, in_last):
            return 5 + 2 * grp if not in_last else 5 + 2 * LAST + (grp - LAST)

        with nc.Block() as block:
            @block.sync
            def _(sp):
                def load_x(dst, b, signal):
                    sp.dma_start(dst[:, :, :], x_v[b, :, :, :]).then_inc(signal, 16)

                def load_gu(src, e, signal):
                    sp.dma_start(st_gu[:, :].rearrange("p (k f) -> p k f", k=KD),
                                 src[e, :, :].rearrange("(k p) f -> p k f", p=P)).then_inc(signal, 16)

                def load_d(e):
                    sp.dma_start(st_d[:, 0:(FC - 1) * D].rearrange("p (c d) -> p c d", c=FC - 1),
                                 wd[e, 0:(FC - 1) * P, :].rearrange("(c p) d -> p c d", p=P)).then_inc(d_in, 16)
                    sp.dma_start(st_d[0:FR, (FC - 1) * D:FC * D], wd[e, (FC - 1) * P:F, :]).then_inc(d_in, 16)

                def batch(b, first, in_last, more_x):
                    hold(sp, lo_ready, 3 * b + 1, spare)
                    load_gu(wu, b, u_in)
                    if not first:
                        hold(sp, x1_ready, b, spare)
                        sp.dma_start(x1_v[b - 1, :, :, :], x1[:, :, :]).then_inc(x1_out, 16)
                    load_x(xr_sb, b, xr_in)
                    if not in_last:
                        hold(sp, xn_ready, b + 2, spare)
                        if more_x:
                            load_x(x_sb, b + 2, x_in)
                        hold(sp, lo_ready, 3 * b + 2, spare)
                        load_d(b + 1)
                        hold(sp, lo_ready, 3 * b + 3, spare)
                        load_gu(wg, b + 1, g_in)

                sp.sem_inc(x1_out, 16)
                load_x(x_sb, 0, x_in)
                for dst, src in ((wq_sb[:, :, :, :], wq), (wk_sb[:, :, :, :], wk), (wv_sb[:, :, :], wv),
                                 (wo_sb[:, :, :], wo), (bq16[:, :], bq), (bk16[:, :], bk),
                                 (bv_sb[:, :], bv.partition_broadcast(P)),
                                 (bo_sb[:, :], bo.partition_broadcast(P)),
                                 (ws_f[:, :, :], ws.rearrange("(k p) e -> p k e", p=P)),
                                 (bs_sb[:, :], bs.partition_broadcast(P))):
                    sp.dma_start(dst, src).then_inc(w_in, 16)
                load_gu(wg, 0, g_in)
                sp.wait_ge(zero_ready, 1)
                load_d(0)
                sp.wait_ge(xn_ready, 1)
                load_x(x_sb, 1, x_in)
                sp.wait_ge(spare_ready, 1)
                sp.dma_start(xs_dram[E * REGION:, :].rearrange("(e p t) w -> p e (t w)", p=P, t=TS // P),
                             spares.bitcast(F32).rearrange("p e t w -> p e (t w)")).then_inc(zeros_out, 16)
                batch(0, True, False, True)
                with sp.Fori(1, B - 2) as b:
                    batch(b, False, False, True)
                batch(B - 2, False, False, False)
                batch(B - 1, False, True, False)
                sp.wait_ge(x1_ready, B)
                sp.dma_start(x1_v[B - 1, :, :, :], x1[:, :, :]).then_inc(x1_out, 16)
                sp.wait_ge(x1_out, 16 * B + 16)
                sp.wait_ge(zeros_out, 16)

            @block.gpsimd
            def _(pool):
                gp = nc.gpsimd
                ch = Chain(pool, pool_const, spare)
                ch.link(gp.memset(power[:, 0, :], 0.5))
                ch.link(gp.memset(power[:, 1, :], -1.0))
                ch.link(gp.memset(wscale[:, :], WSCALE))
                ch.link(gp.memset(ones[:, :], 1.0))
                any_f = dict(allow_small_or_imprecise_dtypes=True)
                ch.link(gp.iota(spare_ids[:, :, :], [[TS, SPARE_TILES + 1], [1, TS // P]],
                                base=TOP * B * T + E * TS, channel_multiplier=TS // P, **any_f))
                ch.link(gp.iota(ids[:, :, :], [[TOP * P, QT], [1, TOP]], base=0, channel_multiplier=TOP, **any_f))
                pool.sem_inc(ids_ready, 1)
                ch.link(gp.iota(iota8[:, :], [[1, E]], base=0, channel_multiplier=0,
                                allow_small_or_imprecise_dtypes=True))
                ch.link(gp.iota(keep["fill"][:, :], [[REGION, E]], base=0, channel_multiplier=0,
                                allow_small_or_imprecise_dtypes=True))
                ch.link(gp.iota(keep["first"][:, :], [[REGION, E]], base=0, channel_multiplier=0,
                                allow_small_or_imprecise_dtypes=True))
                for part in keep["gu"]:
                    ch.link(gp.memset(part[:, :].rearrange("p (r c) -> p r c", c=GU)[:, :, GU_LAST + FR:GU_LAST + P // 2],
                                      0.0))
                ch.link(gp.memset(ident[:, :], 0.0))
                ch.link(gp.affine_select(out=ident[:, :], in_=ident[:, :], compare_op=ALU.not_equal, fill=1.0,
                                         base=0, pattern=[[-1, P]], channel_multiplier=1))
                ch.link(gp.memset(before[:, :], 0.0))
                ch.link(gp.affine_select(out=before[:, :], in_=before[:, :], compare_op=ALU.is_ge, fill=1.0,
                                         base=0, pattern=[[-1, P]], channel_multiplier=1))
                ch.link(gp.memset(mask[:, :], 0.0))
                diagonal = mask[:, T - P:T]
                ch.link(gp.affine_select(out=diagonal, in_=diagonal, compare_op=ALU.is_ge,
                                         fill=MASK * INV_SCALE, base=0, pattern=[[-1, P]], channel_multiplier=1))
                for g in range(G):
                    last = gp.memset(va[:, g, :, :, HD:HD + 1], 1.0)
                    if g < G - 1:
                        ch.link(last)
                last.then_inc(const_ready, 1)

                def rsqrt(n):
                    hold(pool, var_ready, n + 1, spare)
                    gp.tensor_scalar(veps[:, :], mv[:, :, 1], LN_EPS16, None, ALU.add).then_inc(veps_ready, 1)
                    pool.wait_ge(veps_ready, n + 1)
                    gp.tensor_tensor(std[:, :], veps[:, :], power[:, 0, :], ALU.pow).then_inc(std_ready, 1)
                    pool.wait_ge(std_ready, n + 1)
                    gp.tensor_tensor(rstd[:, :], std[:, :], power[:, 1, :], ALU.pow).then_inc(rstd_ready, 1)

                def scale_stage(b, which):
                    stage, n, count = (st_gu, st_d, st_gu)[which], (KD * F, FC * D, KD * F)[which], 3 * b + which
                    pool.wait_ge(hi_ready, count + 1)
                    gp.tensor_tensor(stage[:, :], stage[:, :], wscale[:, 0:1].broadcast_to([P, n]),
                                     ALU.mult).then_inc(mul_ready, 1)

                def rest(b, which):
                    hold(pool, mul_ready, 3 * b + which + 1, spare)
                    for (dst, src), (high, _) in zip(places(b, which, 1), places(b, which, 0)):
                        last = gp.tensor_tensor(dst, src, high, ALU.subtract)
                    last.then_inc(lo_ready, 1)

                def cut(grp, c):
                    hold(pool, p_ready, NF * grp + J * (c + 1) + 2, spare)
                    tiles = TILES_OF[c]
                    at = P_COL[tiles[0], 0]
                    banks = pT[:, at:at + J * width(tiles)].rearrange("p (j n) -> p j n", j=J)
                    for kt in tiles:
                        at = P_COL[kt, 0] - P_COL[tiles[0], 0]
                        diagonal = banks[:, :, at:at + P]
                        last = gp.affine_select(out=diagonal, in_=diagonal, compare_op=ALU.is_ge, fill=0.0, base=0,
                                                pattern=[[0, J], [1, P]], channel_multiplier=-1)
                    last.then_inc(cut_ready, 1)

                def batch(b, first, in_last, scattering):
                    for g in range(G):
                        for c in range(CUTS):
                            cut(G * b + g, c)
                            at = (g, c)
                            if at == (0, 0) and not in_last:
                                rsqrt(1 if first else 3 * b - 1)
                            if at == (0, 1):
                                scale_stage(b, 0)
                            if at == (0, 2):
                                rest(b, 0)
                            if at == (1, 0) and scattering:
                                hold(pool, slot_ready, b - 1, spare)
                                hold(pool, copy_ready, b - 1, spare)
                            if at in AT_SCATTER and scattering:
                                scatter_rows(gp, keep, xs_dram, AT_SCATTER.index(at), len(AT_SCATTER))
                            if at == (1, 2) and not first:
                                rsqrt(3 * b - (1 if in_last else 0))
                            if at == (2, 0):
                                if scattering:
                                    pool.wait_ge(keep["scattered"], 16 * TOP * QT * (b - 1))
                                    pool.sem_inc(xn2_free, 1)
                                scale_stage(b, 1)
                            if at == (2, 1) and not first:
                                rsqrt(3 * b + 1 - (1 if in_last else 0))
                            if at == (2, 2):
                                rest(b, 1)
                            if at == (3, 0):
                                scale_stage(b, 2)
                            if at == (3, 1):
                                rest(b, 2)

                pool.sem_inc(xn2_free, 1)
                rsqrt(0)
                batch(0, True, False, False)
                batch(1, False, False, False)
                with pool.Fori(2, B - 1) as b:
                    batch(b, False, False, True)
                batch(B - 1, False, True, True)
                hold(pool, slot_ready, B - 1, spare)
                hold(pool, copy_ready, B - 1, spare)
                scatter_rows(gp, keep, xs_dram, 0, 1)
                rsqrt(3 * B - 2)
                pool.wait_ge(keep["scattered"], 16 * TOP * QT * (B - 1))
                pool.sem_inc(xn2_free, 1)
                rsqrt(3 * B - 1)

            @block.scalar
            def _(act):
                sc = nc.scalar
                act.wait_ge(w_in, 16 * 10)
                sc.activation(bq_sb[:, :], bq16[:, :], ACT.Copy).then_inc(bias_ready, 1)
                sc.activation(bk_sb[:, :], bk16[:, :], ACT.Copy).then_inc(bias_ready, 1)
                act.wait_ge(bias_ready, 2)
                m16 = M16.rearrange("p (k t) -> p k t", k=KD)

                def take_xnT(b):
                    act.wait_ge(xnT_mm, b + 1)
                    sc.activation(xnT[:, :, :], m16, ACT.Copy).then_inc(xnT_ready, 1)

                def take_q(use, g):
                    act.wait_ge(q_mm, use + 1)
                    sc.activation(qT[:, g, :], Q_BANK[:, :], ACT.Identity, bias=bq_sb[:, g:g + 1]).then_inc(q_out, 1)

                def take_k(grp, g):
                    act.wait_ge(k_mm, grp + 1)
                    sc.activation(kT[:, g, :], K_BANK[:, :], ACT.Identity, bias=bk_sb[:, g:g + 1]).then_inc(k_out, 1)

                def take_q_max(use, g):
                    act.wait_ge(q_mm, use + 1)
                    sc.activation(qT[:, g, :], Q_BANK[:, :], ACT.Copy).then_inc(q_out, 1)

                def part(b, which):
                    signal, amount = ((g_in, 16), (d_in, 32), (u_in, 16))[which]
                    act.wait_ge(signal, amount * b + amount)
                    for dst, src in places(b, which, 0):
                        last = sc.activation(dst, src, ACT.Copy, scale=WSCALE)
                    last.then_inc(hi_ready, 1)

                def take_attT(b):
                    act.wait_ge(attT_mm, b + 1)
                    sc.activation(attT[:, :, :], m16, ACT.Copy).then_inc(attT_out, 1)

                def take_xn2T(b):
                    act.wait_ge(xn2T_mm, b + 1)
                    sc.activation(attT[:, :, :], m16, ACT.Copy).then_inc(xn2T_out, 1)

                def copy_rows(b):
                    act.wait_ge(xn2_ready, b + 1)
                    sc.activation(rows16[:, :, 1, 0:D], xn2, ACT.Copy).then_inc(copy_ready, 1)

                def weight(b):
                    act.wait_ge(dif_ready, b + 1)
                    sc.activation(e1[:, :], dif[:, :], ACT.Exp).then_inc(e1_ready, 1)

                def batch(b, first, in_last):
                    for g in range(G):
                        grp = G * b + g
                        for i, (j, tiles) in enumerate(FILLS):
                            lo, hi = P_COL[tiles[0], j], P_COL[tiles[0], j] + width(tiles)
                            act.wait_ge(st_mm, NF * grp + i + 1)
                            act.wait_ge(pv_mm, NF * grp + i + 1)
                            sc.activation(pT[:, lo:hi], ST_BANK[i % 2][:, 0:hi - lo], ACT.Exp,
                                          scale=1.0 / INV_SCALE).then_inc(p_ready, 1)
                            if i == AT_MAXIMA + 1 and not (in_last and g == G - 1):
                                take_q_max(q_uses(grp, in_last), (g + 1) % G)
                            if i == 2 and g == 1 and not first:
                                take_attT(b - 1)
                            if i == AT_XN2_T + 1 and g == 3 and not first:
                                take_xn2T(b - 1)
                            if i == AT_XN2_T + 3 and g == 3 and not first:
                                copy_rows(b - 1)
                            if i == AT_NEXT_T + 1 and g == 0 and not in_last:
                                take_xnT(b + 1)
                            if i == 7 and g == 3 and not first:
                                weight(b - 1)
                            if i == 4 and g < 3:
                                part(b, g)
                        if not in_last:
                            take_q(q_uses(grp, False) + 1, g)
                            take_k(grp + G, g)

                take_xnT(0)
                act.wait_ge(zeros_out, 16)
                for g in range(G - 1):
                    take_q(g, g)
                    take_k(g, g)
                take_q_max(3, 0)
                take_q(4, G - 1)
                take_k(G - 1, G - 1)
                batch(0, True, False)
                with act.Fori(1, B - 1) as b:
                    batch(b, False, False)
                batch(B - 1, False, True)
                take_attT(B - 1)
                take_xn2T(B - 1)
                copy_rows(B - 1)
                weight(B - 1)

            @block.vector
            def _(dve):
                v = nc.vector
                ch = Chain(dve, dve_chain, spare)
                wch = Chain(dve, ws_chain, spare)
                v.memset(st_d[:, (FC - 1) * D:FC * D], 0.0).then_inc(zero_ready, 1)
                v.memset(spares, 0.0).then_inc(zero_ready, 1)
                dve.wait_ge(zero_ready, 2)
                dve.wait_ge(ids_ready, 1)
                v.tensor_copy(spares.bitcast(U32)[:, :, :, D // 2], spare_ids[:, :, :]).then_inc(spare_ready, 1)
                v.memset(nmax[:, 0, :, :], 0.0).then_inc(p_ready, 2)
                v.memset(nmax[:, 1, :, :], 0.0).then_inc(pv_mm, NF)

                HALVES = (range(QT // 2), range(QT // 2, QT))

                def norm_stats(src, half):
                    for t in HALVES[half]:
                        last = v.bn_stats(stats[:, t, :], src[:, t, :])
                    if half:
                        ch.mark(last)

                def norm_moments(n):
                    ch.settle()
                    for t in range(QT):
                        last = v.bn_aggr(mv[:, t, :], stats[:, t, :])
                    last.then_inc(var_ready, 1)

                def norm_centre(src, n, half):
                    if half == 0:
                        dve.wait_ge(var_ready, n + 1)
                    for t in HALVES[half]:
                        last = v.tensor_scalar(cen[:, t, :], src[:, t, :], mv[:, t, 0:1], None, ALU.subtract)
                    if half:
                        last.then_inc(cen_ready, 1)

                def norm_scale(dst, n, half):
                    if half == 0:
                        dve.wait_ge(cen_ready, n + 1)
                        dve.wait_ge(rstd_ready, n + 1)
                    for t in HALVES[half]:
                        last = v.tensor_scalar(dst[:, t, :], cen[:, t, :], rstd[:, t:t + 1], None, ALU.mult)
                    return last

                def take_v(grp, g):
                    dve.wait_ge(v_mm, grp + 1)
                    v.tensor_copy(v16[:, :, :], M_BANK[:, 0:QT * J * HD].rearrange("p (t c) -> p t c", t=QT)
                                  ).then_inc(v16_ready, 1)
                    dve.wait_ge(v16_ready, grp + 1)
                    for t in range(QT):
                        last = v.tensor_tensor(va[:, g, t, :, 0:HD],
                                               v16[:, t, :].rearrange("p (j d) -> p j d", j=J),
                                               bv_sb[:, 64 * g:64 * (g + 1)].rearrange("p (j d) -> p j d", j=J), ALU.add)
                    last.then_inc(v_out, 1)

                def maxima(grp, g, i):
                    j, tiles = S_FILLS[i]
                    at = 0
                    hold(dve, s_mm, NF * grp + i + 1, spare)
                    for qt in tiles:
                        n = P * (qt + 1)
                        last = v.tensor_tensor_reduce(
                            out=unused[:, i % 2, at:at + n], in0=S_BANK[i % 2][:, at:at + n], in1=mask[:, T - n:T],
                            scale=-1.0, scalar=3.0e38, op0=ALU.add, op1=ALU.min,
                            accum_out=nmax[:, g % 2, qt, 32 * j + HD:32 * j + HD + 1])
                        at += n
                    last.then_inc(s_max, 1)

                def take_att(grp, g):
                    dve.wait_ge(pv_mm, NF * (grp + 2))
                    o = PV_BANK[:, :].rearrange("p (t j c) -> p t j c", t=QT, j=J)
                    ch.link(v.reciprocal(rden[:, :, :], o[:, :, :, HD]))
                    for t in range(QT):
                        last = v.tensor_tensor(att[:, t, 64 * g:64 * (g + 1)].rearrange("p (j d) -> p j d", j=J),
                                               o[:, t, :, 0:HD],
                                               rden[:, t, :].unsqueeze(2).broadcast_to([P, J, HD]), ALU.mult)
                    last.then_inc(att_out, 1)

                def take_y(b, half):
                    dve.wait_ge(y_mm, 2 * b + half + 1)
                    v.tensor_copy(y[:, 2 * half:2 * half + 2, :],
                                  (Q_BANK, K_BANK)[half][:, :].rearrange("p (t d) -> p t d", t=2)
                                  ).then_inc(y_out, 1)

                def bias_y(b):
                    dve.wait_ge(y_out, 2 * b + 2)
                    for t in range(QT):
                        last = v.tensor_tensor(y[:, t, :], y[:, t, :], bo_sb[:, :], ALU.add)
                    last.then_inc(y16_ready, 1)

                def add_x(b):
                    ch.settle()
                    dve.wait_ge(xr_in, 16 * b + 16)
                    dve.wait_ge(x1_out, 16 * b + 16)
                    v.tensor_tensor(x1[:, :, :], xr_sb[:, :, :], y[:, :, :], ALU.add).then_inc(x1_ready, 1)

                def finish(b, n, at):
                    if at in (0, 1):
                        take_y(b, at)
                    elif at == 2:
                        bias_y(b)
                    elif at in (3, 4):
                        if at == 3:
                            dve.wait_ge(y16_ready, b + 1)
                        norm_stats(y, at - 3)
                    elif at == 5:
                        norm_moments(n)
                    elif at in (6, 7):
                        norm_centre(y, n, at - 6)
                    elif at in (8, 9):
                        last = norm_scale(y, n, at - 8)
                        if at == 9:
                            ch.mark(last)
                    elif at == 10:
                        add_x(b)
                    elif at in (11, 12):
                        if at == 11:
                            dve.wait_ge(x1_ready, b + 1)
                        norm_stats(x1, at - 11)
                    elif at == 13:
                        norm_moments(n + 1)
                    elif at in (14, 15):
                        norm_centre(x1, n + 1, at - 14)
                    elif at in (16, 17):
                        if at == 16:
                            dve.wait_ge(xn2_free, b + 1)
                        last = norm_scale(xn2, n + 1, at - 16)
                        if at == 17:
                            last.then_inc(xn2_ready, 1)

                def route(b, at):
                    if at == 0:
                        dve.wait_ge(logit_mm, b + 1)
                        v.tensor_tensor(logit[:, :, :], LOGITS, bs_sb[:, :].unsqueeze(1).broadcast_to([P, QT, E]),
                                        ALU.add).then_inc(logit_out, 1)
                    elif at == 1:
                        hold(dve, logit_out, b + 1, spare)
                        for t in range(QT):
                            last = v.max(top[:, t, :], logit[:, t, :])
                        ch.mark(last)
                    elif at == 2:
                        ch.settle()
                        v.tensor_tensor(dif[:, :], top[:, :, 1], top[:, :, 0], ALU.subtract).then_inc(dif_ready, 1)
                        for t in range(QT):
                            last = v.max_index(topi[:, t, :], top[:, t, :], logit[:, t, :])
                        ch.mark(last)
                    elif at == 3:
                        ch.settle()
                        ch.mark(v.tensor_copy(topf[:, :, :], topi[:, :, 0:TOP]))
                    elif at == 4:
                        ch.settle()
                        for r in range(TOP):
                            last = v.tensor_tensor(pick[r][:, :, :], iota8[:, :].unsqueeze(1).broadcast_to([P, QT, E]),
                                                   topf[:, :, r:r + 1].broadcast_to([P, QT, E]), ALU.is_equal)
                        ch.mark(last)
                    elif at == 5:
                        ch.settle()
                        v.tensor_tensor(both[:, :, :], pick[0][:, :, :], pick[1][:, :, :], ALU.add
                                        ).then_inc(both_ready, 1)

                def slots(b, at):
                    if at == 0:
                        dve.wait_ge(rank_mm, b + 1)
                        ch.mark(v.tensor_tensor(row[:, :, :], RANKS,
                                                keep["fill"][:, :].unsqueeze(1).broadcast_to([P, QT, E]), ALU.add))
                        dve.wait_ge(e1_ready, b + 1)
                        ch.mark(v.tensor_scalar(den[:, :], e1[:, :], 1.0, None, ALU.add))
                    elif at == 1:
                        ch.settle()
                        v.tensor_tensor(keep["fill"][:, :], keep["fill"][:, :], TOTAL, ALU.add).then_inc(rank_out, 1)
                        v.reciprocal(wts[:, :, 0], den[:, :])
                        for r in range(TOP):
                            last = v.tensor_tensor(prow[r][:, :, :], row[:, :, :], pick[r][:, :, :], ALU.mult)
                        ch.mark(last)
                    elif at == 2:
                        ch.settle()
                        v.tensor_tensor(wts[:, :, 1], e1[:, :], wts[:, :, 0], ALU.mult)
                        for r in range(TOP):
                            last = v.reduce_sum(slotf[:, :, r], prow[r][:, :, :], AX.X)
                        ch.mark(last)
                    elif at == 3:
                        ch.settle()
                        v.tensor_copy(slot[:, :, :], slotf[:, :, :])
                        v.tensor_copy(keep["rows"][:, :, :, :].bitcast(U32)[:, :, :, D // 2], ids[:, :, :])
                        v.tensor_copy(keep["rows"][:, :, :, D // 2 + 1], wts[:, :, :]
                                      ).then_inc(slot_ready, 1)
                        ch.mark(v.tensor_scalar(ids[:, :, :], ids[:, :, :], float(TOP * T), None, ALU.add))

                def next_norm(b, n, at, first=False):
                    if at in (0, 1):
                        if at == 0:
                            dve.wait_ge(x_in, 16 * b + 16)
                        norm_stats(x_sb, at)
                    elif at == 2:
                        norm_moments(n)
                    elif at in (3, 4):
                        norm_centre(x_sb, n, at - 3)
                    elif at in (5, 6):
                        if at == 5 and not first:
                            dve.wait_ge(xnT_mm, b)
                        last = norm_scale(xn, n, at - 5)
                        if at == 6:
                            last.then_inc(xn_ready, 1)

                def batch(b, first, in_last):
                    for g in range(G):
                        grp = G * b + g
                        ahead = not (in_last and g >= 2)
                        if ahead:
                            dve.wait_ge(q_mm, 4 + 2 * grp)
                        for i in range(NF):
                            if ahead:
                                maxima(grp + 2, (g + 2) % G, i)
                            if i == AT_TAKE_ATT and not (first and g == 0):
                                if g == 1 and not first:
                                    dve.wait_ge(attT_mm, b)
                                take_att(grp - 1, (g - 1) % G)
                            for n, at in enumerate(AT_NEXT_NORM):
                                if at == (g, i) and not in_last:
                                    next_norm(b + 1, 1 if first else 3 * b - 1, n)
                            for n, at in enumerate(AT_FINISH):
                                if at == (g, i) and not first:
                                    finish(b - 1, 3 * b - (1 if in_last else 0), n)
                            for n, at in enumerate(AT_ROUTE):
                                if at == (g, i) and not first:
                                    route(b - 1, n)
                            for n, at in enumerate(AT_SLOTS):
                                if at == (g, i) and not first:
                                    slots(b - 1, n)
                        if not in_last:
                            take_v(grp + G, g)

                for at in range(len(AT_NEXT_NORM)):
                    next_norm(0, 0, at, first=True)
                dve.wait_ge(bias_ready, 2)
                dve.wait_ge(w_in, 16 * 10)
                dve.wait_ge(const_ready, 1)
                for g in range(G - 1):
                    take_v(g, g)
                dve.wait_ge(pv_mm, NF)
                for i in range(NF):
                    maxima(0, 0, i)
                take_v(G - 1, G - 1)
                for i in range(NF):
                    maxima(1, 1, i)
                for n in range(3):
                    src = ws_f if n == 0 else ws_r
                    wch.link(v.tensor_copy(ws_part[:, :, n, :], src[:, :, :]))
                    if n < 2:
                        wch.link(v.tensor_tensor(ws_r[:, :, :], src[:, :, :], ws_part[:, :, n, :], ALU.subtract))
                batch(0, True, False)
                start = ch.n
                with dve.Fori(1, B - 1) as b:
                    ch.rebase(start + STEPS * (b - 1))
                    batch(b, False, False)
                    assert ch.n == STEPS, ch.n
                ch.rebase(start + STEPS * (B - 2))
                batch(B - 1, False, True)
                take_att(G * B - 1, G - 1)
                for at in range(len(AT_FINISH)):
                    finish(B - 1, 3 * B - 2, at)
                for at in range(len(AT_ROUTE)):
                    route(B - 1, at)
                for at in range(len(AT_SLOTS)):
                    slots(B - 1, at)

            @block.tensor
            def _(pe):
                mm = nc.tensor.matmul

                def transpose4(src, signal):
                    for k in range(KD):
                        for t in range(QT):
                            last = nc.tensor.transpose(M16[:, T * k + P * t:T * k + P * (t + 1)],
                                                       src[:, t, P * k:P * (k + 1)], ident[:, :])
                    last.then_inc(signal, 1)

                def project_q(g):
                    for k in range(KD):
                        last = mm(Q_BANK[:, :], wq_sb[:, k, g, :], xnT[:, k, :], start=(k == 0), stop=(k == KD - 1))
                    last.then_inc(q_mm, 1)

                def project_k(g):
                    for k in range(KD):
                        last = mm(K_BANK[:, :], wk_sb[:, k, g, :], xnT[:, k, :], start=(k == 0), stop=(k == KD - 1))
                    last.then_inc(k_mm, 1)

                def project_v(g):
                    for t in range(QT):
                        for k in range(KD):
                            last = mm(M_BANK[:, 64 * t:64 * (t + 1)], xnT[:, k, P * t:P * (t + 1)],
                                      wv_sb[:, k, 64 * g:64 * (g + 1)], start=(k == 0), stop=(k == KD - 1))
                    last.then_inc(v_mm, 1)

                def scores_qk(g, i):
                    (j, tiles), at = S_FILLS[i], 0
                    for qt in tiles:
                        n = P * (qt + 1)
                        last = mm(S_BANK[i % 2][:, at:at + n], qT[32 * j:32 * j + 32, g, P * qt:P * (qt + 1)],
                                  kT[32 * j:32 * j + 32, g, 0:n], start=True, stop=True)
                        at += n
                    last.then_inc(s_mm, 1)

                def scores_kq(g, i):
                    (j, tiles), at = FILLS[i], 0
                    for kt in tiles:
                        n = T - P * kt
                        last = mm(ST_BANK[i % 2][:, at:at + n], kT[32 * j:32 * j + 32, g, P * kt:P * (kt + 1)],
                                  qT[32 * j:32 * j + 32, g, P * kt:T], start=True, stop=True)
                        at += n
                    last.then_inc(st_mm, 1)

                def add_maxima(g):
                    mm(Q_BANK[:, :], ident[:, :], qT[:, g, :], start=True, stop=False)
                    for t in range(QT):
                        last = mm(Q_BANK[:, P * t:P * (t + 1)], nmax[:, g % 2, t, :], ident[:, :],
                                  start=False, stop=(t == QT - 1))
                    last.then_inc(q_mm, 1)

                def values(grp, g, i):
                    j, tiles = FILLS[i]
                    if j == 0:
                        pe.wait_ge(cut_ready, CUTS * grp + i // J + 1)
                    for kt in tiles:
                        for qt in range(kt, QT):
                            at = P_COL[kt, j] + P * (qt - kt)
                            last = mm(OUT[:, qt, j, 0:HD + 1], pT[:, at:at + P], va[:, g, kt, j, :],
                                      start=(i == 0 and qt == 0), stop=(i == NF - 1 and qt == QT - 1))
                    last.then_inc(pv_mm, 1)

                def project_out(b):
                    pe.wait_ge(attT_out, b + 1)
                    for t in range(QT):
                        for k in range(KD):
                            last = mm((Q_BANK, K_BANK)[t // 2][:, D * (t % 2):D * (t % 2 + 1)],
                                      attT[:, k, P * t:P * (t + 1)], wo_sb[:, k, :],
                                      start=(k == 0), stop=(k == KD - 1))
                        if t % 2:
                            last.then_inc(y_mm, 1)

                def logits(b):
                    pe.wait_ge(xn2T_out, b + 1)
                    for t in range(QT):
                        for s in range(3 * KD):
                            last = mm(LOGITS[:, t, :], attT[:, s // 3, P * t:P * (t + 1)], ws_part[:, s // 3, s % 3, :],
                                      start=(s == 0), stop=(s == 3 * KD - 1))
                    last.then_inc(logit_mm, 1)

                def ranks(b):
                    pe.wait_ge(both_ready, b + 1)
                    for t in range(QT):
                        for s in range(t + 1):
                            mm(RANKS[:, t, :], (before if s == t else ones)[:, :], both[:, s, :],
                               start=(s == 0), stop=(s == t))
                    for s in range(QT):
                        last = mm(TOTAL, ones[:, :], both[:, s, :], start=(s == 0), stop=(s == QT - 1))
                    last.then_inc(rank_mm, 1)

                def batch(b, first, in_last):
                    for g in range(G):
                        grp = G * b + g
                        ahead = not (in_last and g >= 2)
                        pe.wait_ge(q_out, 4 + 2 * grp if not (in_last and g) else q_uses(grp, True))
                        if ahead:
                            pe.wait_ge(k_out, grp + 3)
                        for i in range(NF):
                            pe.wait_ge(p_ready, NF * grp + i + 1)
                            scores_kq(g, i)
                            if ahead:
                                pe.wait_ge(s_max, NF * (grp + 2) + i - 1)
                                scores_qk((g + 2) % G, i)
                            if i == PV_LAG and not (first and g == 0):
                                pe.wait_ge(att_out, grp)
                            if i >= PV_LAG:
                                values(grp, g, i - PV_LAG)
                            if i == 1 and g == 1 and not first:
                                pe.wait_ge(att_out, grp - 1)
                                if not in_last:
                                    pe.wait_ge(v_out, grp + 4)
                                transpose4(att, attT_mm)
                            if i == AT_XN2_T and g == 3 and not first:
                                if not in_last:
                                    pe.wait_ge(v_out, grp + 4)
                                pe.wait_ge(xn2_ready, b)
                                transpose4(xn2, xn2T_mm)
                            if i == AT_XN2_T + 3 and g == 3 and not first:
                                if not in_last:
                                    pe.wait_ge(k_out, grp + 4)
                                else:
                                    pe.wait_ge(y_out, 2 * b)
                                logits(b - 1)
                            if i == AT_RANKS and g == 3 and not first:
                                ranks(b - 1)
                            if i == AT_PROJECT_OUT and g == 1 and not first:
                                pe.wait_ge(q_out, q_uses(grp, in_last))
                                pe.wait_ge(k_out, grp + 4 if not in_last else G * B)
                                project_out(b - 1)
                            if i == AT_MAXIMA and not (in_last and g == G - 1):
                                if g == 1 and not first:
                                    pe.wait_ge(y_out, 2 * b - 1)
                                pe.wait_ge(s_max, NF * (grp + 2))
                                pe.wait_ge(q_out, q_uses(grp, in_last))
                                add_maxima((g + 1) % G)
                            if i == AT_NEXT_T and g == 0 and not in_last:
                                pe.wait_ge(xn_ready, b + 2)
                                pe.wait_ge(v_out, grp + 4)
                                transpose4(xn, xnT_mm)
                        if not in_last:
                            if g == 0:
                                pe.wait_ge(xnT_ready, b + 2)
                            pe.wait_ge(q_out, q_uses(grp, False) + 1)
                            project_q(g)
                            pe.wait_ge(k_out, grp + 4)
                            if g == 1 and not first:
                                pe.wait_ge(y_out, 2 * b)
                            if g == 3 and not first:
                                pe.wait_ge(rank_out, b)
                            project_k(g)
                        for i in range(NF - PV_LAG, NF):
                            values(grp, g, i)
                        if not in_last:
                            if g > 0:
                                pe.wait_ge(v_out, grp + 4)
                            if g == 1 and not first:
                                pe.wait_ge(attT_out, b)
                            if g == 3 and not first:
                                pe.wait_ge(xn2T_out, b)
                            project_v(g)

                pe.wait_ge(const_ready, 1)
                pe.wait_ge(xn_ready, 1)
                transpose4(xn, xnT_mm)
                pe.wait_ge(w_in, 16 * 10)
                pe.wait_ge(xnT_ready, 1)

                def first_projections(g, use):
                    if use:
                        pe.wait_ge(q_out, use)
                    project_q(g)
                    if g:
                        pe.wait_ge(k_out, g)
                    project_k(g)
                    if g:
                        pe.wait_ge(v_out, g)
                    project_v(g)

                def first_scores(grp):
                    pe.wait_ge(k_out, grp + 1)
                    for i in range(NF):
                        n = NF * grp + i
                        if n >= 2:
                            pe.wait_ge(s_max, n - 1)
                        scores_qk(grp, i)

                for g in range(G - 1):
                    first_projections(g, g)
                pe.wait_ge(q_out, G - 1)
                first_scores(0)
                pe.wait_ge(s_max, NF)
                add_maxima(0)
                first_projections(G - 1, G)
                first_scores(1)
                batch(0, True, False)
                with pe.Fori(1, B - 1) as b:
                    batch(b, False, False)
                batch(B - 1, False, True)
                pe.wait_ge(att_out, G * B)
                transpose4(att, attT_mm)
                project_out(B - 1)
                pe.wait_ge(xn2_ready, B)
                transpose4(xn2, xn2T_mm)
                pe.wait_ge(y_out, 2 * B)
                logits(B - 1)
                ranks(B - 1)


def experts(nc, sb, sem, spare, bank, keep, x1_all, x1_in, x1_dram, xs_dram, ys_dram):
    NTILE = TILES
    PAIRS = (NTILE - 1) // 2
    UNROLL = 4
    TAIL = [(i // 2, i % 2) for i in range(2 * PAIRS, NTILE)]
    TT = TS // P
    CP = FC // 2
    M_MAX = B * T // TS
    ident, gu_part, wd_part = keep["ident"], keep["gu"], keep["wd"]
    stack = ExitStack()
    with stack:
        iota_m = sb(stack, "iota_m", [P, M_MAX], F32)
        iota_i = sb(stack, "iota_i", [P, NTILE], F32)
        one8 = sb(stack, "one8", [P, E], F32)
        pads = sb(stack, "pads", [P, E, TT, W // 2], F32)
        pad_ids = sb(stack, "pad_ids", [P, E, TT], F32)
        fill_u = sb(stack, "fill_u", [P, E], U32)
        count = sb(stack, "count", [P, E], F32)
        over = sb(stack, "over", [P, E, M_MAX], F32)
        tiles = sb(stack, "tiles", [P, E], F32)
        cum = sb(stack, "cum", [P, E], F32)
        past = sb(stack, "past", [P, NTILE, E], F32)
        pastn = sb(stack, "pastn", [P, NTILE, E], F32)
        own = sb(stack, "own", [P, NTILE], F32)
        begun = sb(stack, "begun", [P, NTILE], F32)
        rowf = sb(stack, "rowf", [P, NTILE], F32)
        ownc = sb(stack, "ownc", [P, NTILE], F32)
        table = sb(stack, "table", [P, 2, NTILE], U32)
        xin = [sb(stack, f"xin{j}", [P, TT, W // 2], F32) for j in range(2)]
        xin16 = [x[:, :, :].bitcast(F16) for x in xin]
        dest = [sb(stack, f"dest{j}", [P, TT], U32) for j in range(2)]
        share = [sb(stack, f"share{j}", [P, TT], F32) for j in range(2)]
        xT = [sb(stack, f"xT{j}", [P, KD, TS], F16) for j in range(2)]
        act_g = sb(stack, "act_g", [P, CP, 2 * TS], F32)
        hid = sb(stack, "hid", [P, CP, 2 * TS], F32)
        h1 = sb(stack, "h1", [P, CP, 2 * TS], F16)
        h2 = sb(stack, "h2", [P, CP, 2 * TS], F16)
        y_sb = [sb(stack, f"y_sb{j}", [P, TT, D], F32) for j in range(2)]

        G_BANK, U_BANK, Y_BANK = bank[0:3], bank[3:6], bank[6:8]
        XT16 = G_BANK[0][:, 0:KD * TS // 2].bitcast(F16)

        consts = sem("consts")
        plan = sem("plan")
        table_ready = sem("table_ready")
        pad_ready = sem("pad_ready")
        padded = sem("padded")
        xin_in = [sem(f"xin_in{j}") for j in range(2)]
        xT_mm = sem("xT_mm")
        xT_ready = sem("xT_ready")
        up_mm = sem("up_mm")
        silu_ready = sem("silu_ready")
        hid_ready = sem("hid_ready")
        h1_ready = sem("h1_ready")
        h2_ready = sem("h2_ready")
        down_mm = sem("down_mm")
        y_ready = sem("y_ready")
        taken = sem("taken")
        ys_out = [sem(f"ys_out{j}") for j in range(2)]

        def block_of(n):
            if n < CP - 1:
                return slice(0, P), n, slice(0, 2 * TS), G_BANK[n][:, :], U_BANK[n][:, :]
            c = CP - 1
            if n == c:
                return slice(0, P), c, slice(0, TS), G_BANK[c][:, 0:TS], G_BANK[c][:, TS:2 * TS]
            both = U_BANK[c][:, 0:TS]
            return slice(0, FR), c, slice(TS, 2 * TS), both[0:FR, :], both[P // 2:P // 2 + FR, :]

        NB = CP + 1

        def rows_of(dram, row):
            return dram[bass.ds(row, TS), :].rearrange("(t p) d -> p t d", p=P)

        with nc.Block() as block:
            @block.sync
            def _(sp):
                def load(h, j):
                    row = sp.value_load(table[0:1, 0, bass.ds(2 * h + j, 1)], min_val=0, max_val=ROWS - TS)
                    sp.dma_start(xin[j][:, :, :], rows_of(xs_dram, row)).then_inc(xin_in[j], 16)

                sp.wait_ge(pad_ready, 1)
                for e in range(E):
                    row = sp.value_load(fill_u[0:1, e:e + 1], min_val=0, max_val=ROWS - TS)
                    sp.dma_start(xs_dram[bass.ds(row, TS), :].rearrange("(p t) w -> p (t w)", p=P),
                                 pads[:, e, :, :].rearrange("p t w -> p (t w)")).then_inc(padded, 16)
                sp.wait_ge(table_ready, 1)
                sp.wait_ge(padded, 16 * E)
                sp.wait_ge(keep["scattered"], 16 * TOP * QT * B)
                for j in range(2):
                    load(0, j)
                sp.dma_start(x1_all[:, :, :], x1_dram.rearrange("(t p) d -> p t d", p=P)).then_inc(x1_in, 16)
                def reload(h, j):
                    hold(sp, xT_mm, 2 * h + j + 1, spare)
                    hold(sp, taken, 2 * h + j + 1, spare)
                    load(h + 1, j)

                with sp.Fori(0, (NTILE - 2) // 2) as h:
                    for j in range(2):
                        reload(h, j)
                for i in range((NTILE - 2) // 2 * 2, NTILE - 2):
                    reload(i // 2, i % 2)

            @block.gpsimd
            def _(pool):
                gp = nc.gpsimd
                any_f = dict(allow_small_or_imprecise_dtypes=True)
                gp.iota(iota_m[:, :], [[TS, M_MAX]], base=0, channel_multiplier=0, **any_f).then_inc(consts, 1)
                gp.iota(iota_i[:, :], [[1, NTILE]], base=0, channel_multiplier=0, **any_f).then_inc(consts, 1)
                gp.memset(one8[:, :], 1.0).then_inc(consts, 1)
                gp.iota(pad_ids[:, :, :], [[TS, E], [1, TT]], base=TOP * B * T, channel_multiplier=TT, **any_f
                        ).then_inc(consts, 1)
                scatter_rows(gp, keep, xs_dram, 0, 1)

                def store(h, j):
                    hold(pool, y_ready, 2 * h + j + 2, spare)
                    for t in range(TT):
                        gp.indirect_dma_start(
                            out=ys_dram[:, :], in_=y_sb[j][:, t, :], in_offset=None,
                            out_offset=bass.IndirectOffsetOnAxis(ap=dest[j][:, t:t + 1], axis=0),
                        ).then_inc(ys_out[j], 16)

                with pool.Fori(0, PAIRS) as h:
                    for j in range(2):
                        store(h, j)
                for h, j in TAIL:
                    store(h, j)
                for j in range(2):
                    pool.wait_ge(ys_out[j], 16 * TT * ((NTILE - j + 1) // 2))

            @block.scalar
            def _(act):
                sc = nc.scalar

                def take_xT(i, j):
                    act.wait_ge(xT_mm, i + 1)
                    sc.activation(xT[j][:, :, :], XT16.rearrange("p (k t) -> p k t", k=KD), ACT.Copy
                                  ).then_inc(xT_ready, 1)

                def tile(i, j, is_last):
                    def silu(n):
                        rows, c, cols, gate, _ = block_of(n)
                        act.wait_ge(up_mm, NB * i + n + 1)
                        sc.activation(act_g[rows, c, cols], gate, ACT.Silu, scale=1.0 / WSCALE
                                      ).then_inc(silu_ready, 1)

                    def high(n):
                        rows, c, cols, _, _ = block_of(n)
                        act.wait_ge(hid_ready, NB * i + n + 1)
                        act.wait_ge(down_mm, i + 1)
                        sc.activation(h1[rows, c, cols], hid[rows, c, cols], ACT.Copy).then_inc(h1_ready, 1)

                    for n in range(NB - 2):
                        silu(n)
                        high(n)
                    silu(NB - 2)
                    silu(NB - 1)
                    high(NB - 2)
                    high(NB - 1)
                    if not is_last:
                        take_xT(i + 1, 1 - j)

                take_xT(0, 0)
                with act.Fori(0, PAIRS) as h:
                    for j in range(2):
                        tile(2 * h + j, j, False)
                for h, j in TAIL:
                    tile(2 * h + j, j, 2 * h + j == NTILE - 1)

            @block.vector
            def _(dve):
                v = nc.vector
                dve.sem_inc(y_ready, 1)
                ch = Chain(dve, plan, spare)
                v.tensor_copy(fill_u[:, :], keep["fill"][:, :])
                ch.link(v.memset(pads[:, :, :, :], 0.0))
                dve.wait_ge(consts, 4)
                v.tensor_copy(pads[:, :, :, :].bitcast(U32)[:, :, :, D // 2], pad_ids[:, :, :]).then_inc(pad_ready, 1)
                ch.link(v.tensor_tensor(count[:, :], keep["fill"][:, :], keep["first"][:, :], ALU.subtract))
                ch.link(v.tensor_tensor(over[:, :, :], count[:, :].unsqueeze(2).broadcast_to([P, E, M_MAX]),
                                        iota_m[:, :].unsqueeze(1).broadcast_to([P, E, M_MAX]), ALU.is_gt))
                ch.link(v.reduce_sum(tiles[:, :], over[:, :, :], AX.X))
                ch.link(v.tensor_tensor_scan(cum[:, :], one8[:, :], tiles[:, :], 0.0, ALU.mult, ALU.add))
                ch.link(v.tensor_tensor(past[:, :, :], iota_i[:, :].unsqueeze(2).broadcast_to([P, NTILE, E]),
                                        cum[:, :].unsqueeze(1).broadcast_to([P, NTILE, E]), ALU.is_ge))
                v.tensor_tensor(pastn[:, :, :], past[:, :, :], tiles[:, :].unsqueeze(1).broadcast_to([P, NTILE, E]),
                                ALU.mult)
                ch.link(v.reduce_sum(own[:, :], past[:, :, :], AX.X))
                ch.link(v.reduce_sum(begun[:, :], pastn[:, :, :], AX.X))
                ch.link(v.tensor_tensor(rowf[:, :], iota_i[:, :], begun[:, :], ALU.subtract))
                ch.link(v.tensor_scalar(rowf[:, :], rowf[:, :], float(TS), None, ALU.mult))
                ch.link(v.scalar_tensor_tensor(rowf[:, :], own[:, :], float(REGION), rowf[:, :], ALU.mult, ALU.add))
                ch.link(v.tensor_scalar(ownc[:, :], own[:, :], float(E - 1), None, ALU.min))
                v.tensor_copy(table[:, 0, :], rowf[:, :])
                v.tensor_copy(table[:, 1, :], ownc[:, :]).then_inc(table_ready, 1)

                def tile(h, j, first):
                    i = 2 * h + j
                    dve.wait_ge(xin_in[j], 16 * h + 16)
                    if not first:
                        dve.wait_ge(ys_out[j], 16 * TT * h)
                    v.tensor_copy(dest[j][:, :], xin[j][:, :, :].bitcast(U32)[:, :, D // 2])
                    v.tensor_copy(share[j][:, :], xin[j][:, :, D // 2 + 1]).then_inc(taken, 1)
                    def hidden(n):
                        rows, c, cols, _, other = block_of(n)
                        dve.wait_ge(silu_ready, NB * i + n + 1)
                        v.scalar_tensor_tensor(hid[rows, c, cols], other, HSCALE / WSCALE, act_g[rows, c, cols],
                                               ALU.mult, ALU.mult).then_inc(hid_ready, 1)

                    def low(n):
                        rows, c, cols, _, _ = block_of(n)
                        dve.wait_ge(h1_ready, NB * i + n + 1)
                        v.tensor_tensor(h2[rows, c, cols], hid[rows, c, cols], h1[rows, c, cols], ALU.subtract
                                        ).then_inc(h2_ready, 1)

                    for n in range(NB - 2):
                        hidden(n)
                        low(n)
                    hidden(NB - 2)
                    hidden(NB - 1)
                    low(NB - 2)
                    low(NB - 1)
                    dve.wait_ge(down_mm, i + 2)
                    dve.wait_ge(taken, i + 1)
                    for t in range(TT):
                        last = v.tensor_scalar(y_sb[j][:, t, :], Y_BANK[t][:, 0:D], share[j][:, t:t + 1],
                                               1.0 / (WSCALE * HSCALE), ALU.mult, ALU.mult)
                    last.then_inc(y_ready, 1)

                for j in range(2):
                    tile(0, j, True)
                with dve.Fori(1, PAIRS) as h:
                    for j in range(2):
                        tile(h, j, False)
                for h, j in TAIL:
                    tile(h, j, False)

            @block.tensor
            def _(pe):
                mm = nc.tensor.matmul

                def transpose_rows(h, j):
                    pe.wait_ge(xin_in[j], 16 * h + 16)
                    for k in range(KD):
                        for t in range(TT):
                            last = nc.tensor.transpose(XT16[:, TS * k + P * t:TS * k + P * (t + 1)],
                                                       xin16[j][:, t, P * k:P * (k + 1)], ident[:, :])
                    last.then_inc(xT_mm, 1)

                def up(i, j, c, col):
                    last = None
                    for half in range(2):
                        n, cols = 2 * c + half, slice(TS * half, TS * (half + 1))
                        if half and c == CP - 1:
                            last.then_inc(up_mm, 1)
                        if n < FC - 2:
                            sources = ((G_BANK[c][:, cols], n * P, P), (U_BANK[c][:, cols], GU_UP + n * P, P))
                        elif n == FC - 2:
                            sources = ((G_BANK[c][:, 0:TS], n * P, P), (G_BANK[c][:, TS:2 * TS], GU_UP + n * P, P))
                        else:
                            sources = ((U_BANK[c][:, 0:TS], GU_LAST, GU - GU_LAST),)
                        for dst, at, width in sources:
                            for s in range(2 * KD):
                                k, part = s // 2, s % 2
                                last = mm(dst[0:width, :], gu_part[part][:, bass.ds(col + (k * GU + at), width)],
                                          xT[j][:, k, :], start=(s == 0), stop=(s == 2 * KD - 1))
                    last.then_inc(up_mm, 1)

                def expert_of(i):
                    return pe.value_load(table[0:1, 1, bass.ds(i, 1)], min_val=0, max_val=E - 1)

                def down(i, col, is_last):
                    following = None
                    for c in range(FC):
                        if c == FC - 2 and not is_last:
                            following = expert_of(i + 1)
                        rows = P if c < FC - 1 else FR
                        if c % 2 == 0:
                            pe.wait_ge(h1_ready, NB * i + c // 2 + 1)
                        for s, (h, w) in enumerate(((h1, 0), (h1, 1), (h2, 0))):
                            for t in range(TT):
                                if c % 2 == 0 and s == 2 and t == 0:
                                    pe.wait_ge(h2_ready, NB * i + c // 2 + 1)
                                if c == FC - 2 and s == 2 and t == TT - 1:
                                    pe.wait_ge(h2_ready, NB * i + NB)
                                at = (c % 2) * TS + t * P
                                last = mm(Y_BANK[t][:, 0:D], h[0:rows, c // 2, at:at + P],
                                          wd_part[w][0:rows, bass.ds(col + c * D, D)],
                                          start=(c == 0 and s == 0), stop=(c == FC - 1 and s == 2))
                    last.then_inc(down_mm, 1)
                    return following

                def tile(h, j, is_last, expert):
                    i = 2 * h + j
                    col_gu, col_d = expert * (KD * GU), expert * (FC * D)
                    pe.wait_ge(xT_ready, i + 1)
                    for c in range(CP):
                        up(i, j, c, col_gu)
                    if not is_last:
                        pe.wait_ge(silu_ready, NB * i + 1)
                        transpose_rows(h + j, 1 - j)
                    pe.wait_ge(y_ready, i + 1)
                    return down(i, col_d, is_last)

                pe.sem_inc(down_mm, 1)
                pe.wait_ge(table_ready, 1)
                transpose_rows(0, 0)
                LOOPS = (NTILE - 1) // UNROLL
                with pe.Fori(0, LOOPS) as h:
                    expert = expert_of(UNROLL * h)
                    for n in range(UNROLL):
                        expert = tile(UNROLL // 2 * h + n // 2, n % 2, False, expert)
                expert = expert_of(UNROLL * LOOPS)
                for i in range(UNROLL * LOOPS, NTILE):
                    expert = tile(i // 2, i % 2, i == NTILE - 1, expert)


def combine(nc, sb, sem, spare, x1_all, x1_in, ys_dram, out):
    TT = 2
    N = NT // TT
    RING = 4
    ys_v = ys_dram[0:TOP * B * T, :].rearrange("(i t p r) d -> i p t (r d)", t=TT, p=P, r=TOP)
    out_v = out.rearrange("b (h t p) d -> (b h) p t d", t=TT, p=P)
    stack = ExitStack()
    with stack:
        ys = [sb(stack, f"ys{j}", [P, TT, TOP * D], F32) for j in range(RING)]
        total = [sb(stack, f"total{r}", [P, TT, D], F32) for r in range(RING)]
        res = [sb(stack, f"res{j}", [P, TT, D], F32) for j in range(2)]
        nrm = [sb(stack, f"nrm{j}", [P, TT, D], F32) for j in range(2)]
        stats = [sb(stack, f"stats3_{r}", [P, TT, 6], F32) for r in range(RING)]
        mv = [sb(stack, f"mv3_{r}", [P, TT, 2], F32) for r in range(RING)]
        std = [sb(stack, f"std3_{r}", [P, TT], F32) for r in range(RING)]
        rstd = [sb(stack, f"rstd3_{r}", [P, TT], F32) for r in range(RING)]
        shift = [sb(stack, f"shift{r}", [P, TT], F32) for r in range(RING)]
        eps = sb(stack, "eps", [P, 1], F32)

        ys_in = [sem(f"ys_in{r}") for r in range(RING)]
        sum_ready = sem("sum_ready")
        eps_ready = sem("eps_ready")
        cchain = sem("cchain")
        var_ready = sem("var_ready3")
        std_ready = sem("std_ready3")
        shift_ready = sem("shift_ready")
        nrm_ready = sem("nrm_ready")
        fin = sem("fin")
        stored = [sem(f"stored{j}") for j in range(2)]

        with nc.Block() as block:
            @block.sync
            def _(sp):
                def load(h, r):
                    sp.dma_start(ys[r][:, :, :], ys_v[RING * h + r, :, :, :]).then_inc(ys_in[r], 16)

                def store(h, r):
                    hold(sp, fin, RING * h + r + 3, spare)
                    sp.dma_start(out_v[RING * h + r, :, :, :], res[r % 2][:, :, :]).then_inc(stored[r % 2], 16)

                for j in range(2):
                    sp.sem_inc(stored[j], 16)
                for r in range(RING):
                    load(0, r)
                with sp.Fori(0, N // RING - 1) as h:
                    for r in range(RING):
                        hold(sp, sum_ready, RING * h + r + 1, spare)
                        load(h + 1, r)
                        store(h, r)
                for r in range(RING):
                    store(N // RING - 1, r)
                for j in range(2):
                    sp.wait_ge(stored[j], 8 * N + 16)

            @block.gpsimd
            def _(pool):
                gp = nc.gpsimd
                gp.memset(eps[:, :], LN_EPS).then_inc(eps_ready, 1)
                pool.sem_inc(fin, 2)
                pool.wait_ge(x1_in, 16)
                with pool.Fori(0, N // 2) as h:
                    for j in range(2):
                        n = 2 * h + j
                        pool.wait_ge(stored[j], 16 * h + 16)
                        pool.wait_ge(nrm_ready, n + 1)
                        gp.tensor_tensor(res[j][:, :, :], nrm[j][:, :, :], x1_all[:, bass.ds(n * TT, TT), :],
                                         ALU.add).then_inc(fin, 1)

            @block.scalar
            def _(act):
                act.wait_ge(eps_ready, 1)

                def root(h, r):
                    act.wait_ge(var_ready, RING * h + r + 1)
                    nc.scalar.activation(std[r][:, :], mv[r][:, :, 1], ACT.Sqrt, bias=eps[:, 0:1]).then_inc(std_ready, 1)

                def normalise(h, r):
                    n, j = RING * h + r, r % 2
                    act.wait_ge(shift_ready, n + 1)
                    act.wait_ge(fin, n + 1)
                    for t in range(TT):
                        last = nc.scalar.activation(nrm[j][:, t, :], total[r][:, t, :], ACT.Identity,
                                                    bias=shift[r][:, t:t + 1], scale=rstd[r][:, t:t + 1])
                    last.then_inc(nrm_ready, 1)

                root(0, 0)
                for r in range(1, RING):
                    root(0, r)
                    normalise(0, r - 1)
                with act.Fori(1, N // RING) as h:
                    for r in range(RING):
                        root(h, r)
                        normalise(*((h, r - 1) if r else (h - 1, RING - 1)))
                normalise(N // RING - 1, RING - 1)

            @block.vector
            def _(dve):
                v = nc.vector
                ch = Chain(dve, cchain, spare)

                def step(h, r, first=False, early=False, last=False):
                    n, before = RING * h + r, (r - 1) % RING
                    ch.rebase(2 * n)
                    if first:
                        ch.n = 1
                    if not early:
                        dve.wait_ge(nrm_ready, n - 3)
                    if not last:
                        dve.wait_ge(ys_in[r], 16 * h + 16)
                        v.tensor_tensor(total[r][:, :, :], ys[r][:, :, 0:D], ys[r][:, :, D:2 * D], ALU.add
                                        ).then_inc(sum_ready, 1)
                    if not first:
                        dve.wait_ge(std_ready, n)
                        ch.mark(v.reciprocal(rstd[before][:, :], std[before][:, :]))
                    if not last:
                        dve.wait_ge(sum_ready, n + 1)
                        for t in range(TT):
                            done = v.bn_stats(stats[r][:, t, :], total[r][:, t, :])
                        ch.mark(done)
                    ch.settle()
                    if not last:
                        for t in range(TT):
                            done = v.bn_aggr(mv[r][:, t, :], stats[r][:, t, :])
                        done.then_inc(var_ready, 1)
                    if not first:
                        v.scalar_tensor_tensor(shift[before][:, :], mv[before][:, :, 0], -1.0, rstd[before][:, :],
                                               ALU.mult, ALU.mult).then_inc(shift_ready, 1)

                dve.sem_inc(cchain, 1)
                step(0, 0, first=True, early=True)
                for r in range(1, RING):
                    step(0, r, early=True)
                with dve.Fori(1, N // RING) as h:
                    for r in range(RING):
                        step(h, r)
                step(N // RING, 0, last=True)


_OUT = ("out_0", (B, T, D), "float32")


def kernel(**inputs):
    import numpy as np
    import concourse.bacc as bacc
    from concourse.bass_utils import run_bass_kernel_spmd

    a = {k: np.ascontiguousarray(v) for k, v in inputs.items()}

    def by_head(w):
        w = w.T.reshape(KD, P, G, J, HD)
        r = np.zeros((KD, P, G, J, 32), w.dtype)
        r[..., :HD] = w
        return np.ascontiguousarray(r.reshape(KD, P, G, P).transpose(1, 0, 2, 3))

    def bias_by_head(b, fill):
        r = np.zeros((G, J, 32), b.dtype)
        r[..., :HD] = b.reshape(G, J, HD)
        r[..., HD] = fill
        return np.ascontiguousarray(r.reshape(G, P).T)

    def by_slice(w):
        return np.ascontiguousarray(w.T.reshape(KD, P, D).transpose(1, 0, 2))

    arrays = {
        "x": a["L0_attn_hidden_states"],
        "wq": by_head(a["L0_attn_wq"]), "wk": by_head(a["L0_attn_wk"]),
        "wv": by_slice(a["L0_attn_wv"]), "wo": by_slice(a["L0_attn_wo"]),
        "bq": bias_by_head(a["L0_attn_bq"], 0), "bk": bias_by_head(a["L0_attn_bk"], 1),
        "bv": a["L0_attn_bv"], "bo": a["L0_attn_bo"],
        "ws": a["L0_ffn_Ws"], "bs": a["L0_ffn_bs"],
        "wg": a["L0_ffn_Wg"], "wu": a["L0_ffn_Wu"], "wd": a["L0_ffn_Wd"],
    }
    nc = bacc.Bacc("TRN2", target_bir_lowering=False, num_devices=1)
    args = [nc.dram_tensor(k, v.shape, mybir.dt.from_np(v.dtype), kind="ExternalInput").ap()
            for k, v in arrays.items()]
    out = nc.dram_tensor(_OUT[0], _OUT[1], mybir.dt.from_np(np.dtype(_OUT[2])), kind="ExternalOutput").ap()
    build(nc, *args, out)
    r = run_bass_kernel_spmd(nc, [arrays], core_ids=[0])
    return r.results[0][_OUT[0]]
```
